# Optimizing a Trainium2 kernel written in Bass

```python
import numpy as np
import jax
import jax.numpy as jnp

def _softmax(x, axis=-1):
    return jax.nn.softmax(x, axis=axis)

def _gelu(x):
    return jax.nn.gelu(x, approximate=True)

def _silu(x):
    return jax.nn.silu(x)

def _sigmoid(x):
    return jax.nn.sigmoid(x)

def _layernorm(x, axis=-1, eps=1e-05):
    m = jnp.mean(x, axis=axis, keepdims=True)
    v = jnp.var(x, axis=axis, keepdims=True)
    return (x - m) / jnp.sqrt(v + eps)

def _scatter_add(tgt, idx, src, axis=0):
    return tgt.at[idx].add(src)

def _segment_sum(src, seg, n):
    return jax.ops.segment_sum(src, seg, n)
kernel_name = 'mk_adaln_d2_jaxref_r8_f3b044'

def setup_inputs(seed: int=0):
    np.random.seed(seed)
    _w = jnp.asarray

    def _L0_attn_setup():
        import jax, jax.numpy as jnp
        import numpy as np
        import math
        EMBED_DIM = 128
        NUM_HEADS = 16
        HEAD_DIM = EMBED_DIM // NUM_HEADS
        key = jax.random.key(seed)
        ks = jax.random.split(key, 5)
        B, S, D = (2, 256, EMBED_DIM)
        s = 1.0 / math.sqrt(D)
        x = jax.random.normal(ks[0], (B, S, D), dtype=jnp.float32)
        W_qkv = jax.random.normal(ks[1], (3 * D, D), dtype=jnp.float32) * s
        b_qkv = jax.random.normal(ks[2], (3 * D,), dtype=jnp.float32) * 0.01
        W_out = jax.random.normal(ks[3], (D, D), dtype=jnp.float32) * s
        b_out = jax.random.normal(ks[4], (D,), dtype=jnp.float32) * 0.01
        return {'x': x, 'W_qkv': W_qkv, 'b_qkv': b_qkv, 'W_out': W_out, 'b_out': b_out}
    _L0_attn_in = _L0_attn_setup()

    def _L0_ffn_setup():
        import jax, jax.numpy as jnp
        import numpy as np
        B, S, H, E, F = (2, 256, 128, 8, 512)
        key = jax.random.key(seed)
        k1, k2, k3, k4 = jax.random.split(key, 4)
        h = jax.random.normal(k1, (B, S, H), dtype=jnp.float32)
        Wr = jax.random.normal(k2, (H, E), dtype=jnp.float32) / np.sqrt(H)
        W1 = jax.random.normal(k3, (E, H, F), dtype=jnp.float32) / np.sqrt(H)
        W2 = jax.random.normal(k4, (E, F, H), dtype=jnp.float32) / np.sqrt(F)
        return {'h': h, 'Wr': Wr, 'W1': W1, 'W2': W2}
    _L0_ffn_in = _L0_ffn_setup()
    _L0_c = _w((lambda *s: np.random.randn(*s).astype(np.float32) * 0.05)(32, 128))
    _L0_wmod = _w((lambda *s: np.random.randn(*s).astype(np.float32) * 0.05)(128, 6 * 128) * 128 ** (-0.5))

    def _L1_attn_setup():
        import jax, jax.numpy as jnp
        import numpy as np
        HIDDEN_DIM = 128
        NUM_HEADS = 16
        LN_EPS = 1e-06

        def _layernorm(x, scale, bias):
            mu = jnp.mean(x, axis=-1, keepdims=True)
            var = jnp.mean(jnp.square(x - mu), axis=-1, keepdims=True)
            return (x - mu) * jax.lax.rsqrt(var + LN_EPS) * scale + bias
        key = jax.random.key(seed)
        ks = jax.random.split(key, 4)
        B, S, D = (2, 256, HIDDEN_DIM)
        x = jax.random.normal(ks[0], (B, S, D), dtype=jnp.float32)
        scale = 1.0 / np.sqrt(D)
        wq = jax.random.normal(ks[1], (D, HIDDEN_DIM), dtype=jnp.float32) * scale
        wk = jax.random.normal(ks[2], (D, HIDDEN_DIM), dtype=jnp.float32) * scale
        wv = jax.random.normal(ks[3], (D, HIDDEN_DIM), dtype=jnp.float32) * scale
        ln_scale = jnp.ones((D,), dtype=jnp.float32)
        ln_bias = jnp.zeros((D,), dtype=jnp.float32)
        return {'x': x, 'ln_scale': ln_scale, 'ln_bias': ln_bias, 'wq': wq, 'wk': wk, 'wv': wv}
    _L1_attn_in = _L1_attn_setup()

    def _L1_ffn_setup():
        import jax, jax.numpy as jnp
        import numpy as np
        B, T, D, F, E = (2, 128, 128, 512, 8)
        EPS = 1e-06
        key = jax.random.key(seed)
        k = jax.random.split(key, 5)
        scale = 0.02
        return {'x': jax.random.normal(k[0], (B, T, D), dtype=jnp.float32), 'rms_w': jnp.ones((D,), dtype=jnp.float32), 'gate_w': jax.random.normal(k[1], (E, D), dtype=jnp.float32) * scale, 'W1': jax.random.normal(k[2], (E, D, F), dtype=jnp.float32) * scale, 'b1': jnp.zeros((E, F), dtype=jnp.float32), 'W2': jax.random.normal(k[3], (E, F, D), dtype=jnp.float32) * scale, 'b2': jnp.zeros((E, D), dtype=jnp.float32)}
    _L1_ffn_in = _L1_ffn_setup()
    _L1_c = _w((lambda *s: np.random.randn(*s).astype(np.float32) * 0.05)(32, 128))
    _L1_wmod = _w((lambda *s: np.random.randn(*s).astype(np.float32) * 0.05)(128, 6 * 128) * 128 ** (-0.5))
    _d = {'L0_attn_x': _L0_attn_in['x'], 'L0_attn_W_qkv': _L0_attn_in['W_qkv'], 'L0_attn_b_qkv': _L0_attn_in['b_qkv'], 'L0_attn_W_out': _L0_attn_in['W_out'], 'L0_attn_b_out': _L0_attn_in['b_out'], 'L0_ffn_Wr': _L0_ffn_in['Wr'], 'L0_ffn_W1': _L0_ffn_in['W1'], 'L0_ffn_W2': _L0_ffn_in['W2'], 'L0_c': _L0_c, 'L0_wmod': _L0_wmod, 'L1_attn_ln_scale': _L1_attn_in['ln_scale'], 'L1_attn_ln_bias': _L1_attn_in['ln_bias'], 'L1_attn_wq': _L1_attn_in['wq'], 'L1_attn_wk': _L1_attn_in['wk'], 'L1_attn_wv': _L1_attn_in['wv'], 'L1_ffn_rms_w': _L1_ffn_in['rms_w'], 'L1_ffn_gate_w': _L1_ffn_in['gate_w'], 'L1_ffn_W1': _L1_ffn_in['W1'], 'L1_ffn_b1': _L1_ffn_in['b1'], 'L1_ffn_W2': _L1_ffn_in['W2'], 'L1_ffn_b2': _L1_ffn_in['b2'], 'L1_c': _L1_c, 'L1_wmod': _L1_wmod}
    _x0 = _d['L0_attn_x']
    _d['L0_attn_x'] = jax.random.normal(jax.random.fold_in(jax.random.key(seed), 1), (32, 256, 128), dtype=_x0.dtype)
    del _x0
    return _d

def reference(L0_attn_x, L0_attn_W_qkv, L0_attn_b_qkv, L0_attn_W_out, L0_attn_b_out, L0_ffn_Wr, L0_ffn_W1, L0_ffn_W2, L0_c, L0_wmod, L1_attn_ln_scale, L1_attn_ln_bias, L1_attn_wq, L1_attn_wk, L1_attn_wv, L1_ffn_rms_w, L1_ffn_gate_w, L1_ffn_W1, L1_ffn_b1, L1_ffn_W2, L1_ffn_b2, L1_c, L1_wmod):

    def _L0_attn_ref(x, W_qkv, b_qkv, W_out, b_out):
        import jax, jax.numpy as jnp
        import numpy as np
        import math
        EMBED_DIM = 128
        NUM_HEADS = 16
        HEAD_DIM = EMBED_DIM // NUM_HEADS
        B, S, D = x.shape
        H, Hd = (NUM_HEADS, HEAD_DIM)
        slopes = jnp.power(2.0, 8.0 * jnp.arange(0, -H, -1, dtype=jnp.float32) / H)
        qkv = x @ W_qkv.T + b_qkv
        qkv = qkv.reshape(B, S, 3, H, Hd).transpose(2, 0, 3, 1, 4)
        q, k, v = (qkv[0], qkv[1], qkv[2])
        scores = jnp.einsum('bhqd,bhkd->bhqk', q, k) / math.sqrt(Hd)
        pos = jnp.arange(S)
        rel = jnp.abs(pos[None, :] - pos[:, None]).astype(jnp.float32)
        bias = -slopes[:, None, None] * rel
        probs = jax.nn.softmax(scores + bias[None], axis=-1)
        out = jnp.einsum('bhqk,bhkd->bhqd', probs, v)
        out = out.transpose(0, 2, 1, 3).reshape(B, S, D)
        return out @ W_out.T + b_out

    def _L0_ffn_ref(h, Wr, W1, W2):
        import jax, jax.numpy as jnp
        import numpy as np
        B, S, H, E, F = (2, 256, 128, 8, 512)
        g = jax.nn.softmax(h @ Wr, axis=-1)
        top2_w, top2_idx = jax.lax.top_k(g, 2)
        top2_w = top2_w / jnp.sum(top2_w, axis=-1, keepdims=True)
        hid = jax.nn.relu(jnp.einsum('bsh,ehf->bsef', h, W1))
        expert_out = jnp.einsum('bsef,efh->bseh', hid, W2)
        top2_out = jnp.take_along_axis(expert_out, top2_idx[..., None], axis=2)
        return jnp.sum(top2_out * top2_w[..., None], axis=2)

    def _L1_attn_ref(x, ln_scale, ln_bias, wq, wk, wv):
        import jax, jax.numpy as jnp
        import numpy as np
        HIDDEN_DIM = 128
        NUM_HEADS = 16
        LN_EPS = 1e-06

        def _layernorm(x, scale, bias):
            mu = jnp.mean(x, axis=-1, keepdims=True)
            var = jnp.mean(jnp.square(x - mu), axis=-1, keepdims=True)
            return (x - mu) * jax.lax.rsqrt(var + LN_EPS) * scale + bias
        bs, sl, fdim = x.shape
        h, hd = (NUM_HEADS, HIDDEN_DIM // NUM_HEADS)
        xn = _layernorm(x, ln_scale, ln_bias)
        q = (xn @ wq).reshape(bs, sl, h, hd).transpose(0, 2, 1, 3)
        k = (xn @ wk).reshape(bs, sl, h, hd).transpose(0, 2, 1, 3)
        v = (xn @ wv).reshape(bs, sl, h, hd).transpose(0, 2, 1, 3)
        scores = jnp.einsum('bhid,bhjd->bhij', q, k)
        probs = jax.nn.softmax(scores / jnp.sqrt(jnp.float32(HIDDEN_DIM)), axis=-1)
        out = jnp.einsum('bhij,bhjd->bhid', probs, v)
        out = out.transpose(0, 2, 1, 3).reshape(bs, sl, -1) + xn
        return out

    def _L1_ffn_ref(x, rms_w, gate_w, W1, b1, W2, b2):
        import jax, jax.numpy as jnp
        import numpy as np
        B, T, D, F, E = (2, 128, 128, 512, 8)
        EPS = 1e-06
        ms = jnp.mean(x * x, axis=-1, keepdims=True)
        xn = x * jax.lax.rsqrt(ms + EPS) * rms_w
        logits = jnp.einsum('btd,ed->bte', xn, gate_w)
        scores = jax.nn.softmax(logits, axis=-1)
        top1_idx = jnp.argmax(scores, axis=-1)
        top1_score = jnp.max(scores, axis=-1)
        out = jnp.zeros_like(xn)
        for e in range(E):
            h = jax.nn.silu(jnp.einsum('btd,df->btf', xn, W1[e]) + b1[e])
            ye = jnp.einsum('btf,fd->btd', h, W2[e]) + b2[e]
            out = jnp.where((top1_idx == e)[..., None], ye, out)
        return out * top1_score[..., None]
    x = L0_attn_x
    mod = (_silu(L0_c) @ L0_wmod).reshape(L0_c.shape[0], 6, 1, -1)
    sa, ca, ga, sb, cb, gb = (mod[:, 0], mod[:, 1], mod[:, 2], mod[:, 3], mod[:, 4], mod[:, 5])
    ga = (2 * (ga >= 0) - 1) * jnp.maximum(jnp.abs(ga), 0.25)
    gb = (2 * (gb >= 0) - 1) * jnp.maximum(jnp.abs(gb), 0.25)
    h = _layernorm(x, axis=-1) * (1 + ca) + sa
    x = x + ga * _L0_attn_ref(h, L0_attn_W_qkv, L0_attn_b_qkv, L0_attn_W_out, L0_attn_b_out)
    h = _layernorm(x, axis=-1) * (1 + cb) + sb
    x = x + gb * _L0_ffn_ref(h, L0_ffn_Wr, L0_ffn_W1, L0_ffn_W2)
    mod = (_silu(L1_c) @ L1_wmod).reshape(L1_c.shape[0], 6, 1, -1)
    sa, ca, ga, sb, cb, gb = (mod[:, 0], mod[:, 1], mod[:, 2], mod[:, 3], mod[:, 4], mod[:, 5])
    ga = (2 * (ga >= 0) - 1) * jnp.maximum(jnp.abs(ga), 0.25)
    gb = (2 * (gb >= 0) - 1) * jnp.maximum(jnp.abs(gb), 0.25)
    h = _layernorm(x, axis=-1) * (1 + ca) + sa
    x = x + ga * _L1_attn_ref(h, L1_attn_ln_scale, L1_attn_ln_bias, L1_attn_wq, L1_attn_wk, L1_attn_wv)
    h = _layernorm(x, axis=-1) * (1 + cb) + sb
    x = x + gb * _L1_ffn_ref(h, L1_ffn_rms_w, L1_ffn_gate_w, L1_ffn_W1, L1_ffn_b1, L1_ffn_W2, L1_ffn_b2)
    return x

_drawn_inputs = setup_inputs


def setup_inputs(seed=0):
    import zlib

    import numpy as np

    out = dict(_drawn_inputs(seed))
    spreads = {'L1_attn_ln_scale': (1.0, 0.2),
     'L1_attn_ln_bias': (0.0, 0.1),
     'L1_ffn_rms_w': (1.0, 0.6),
     'L1_ffn_b1': (0.0, 0.8),
     'L1_ffn_b2': (0.0, 0.8)}
    factors = {'L0_attn_b_qkv': 8.0,
     'L0_attn_b_out': 8.0,
     'L1_attn_wq': 7.266,
     'L1_attn_wk': 7.008,
     'L1_ffn_gate_w': 8.0,
     'L1_ffn_W1': 8.0,
     'L1_ffn_W2': 8.0}
    for name, (base, spread) in spreads.items():
        noise = np.random.default_rng([zlib.crc32(name.encode()), seed]).standard_normal(out[name].shape)
        drawn = base * np.exp(spread * noise) if base else spread * noise
        out[name] = jnp.asarray(drawn.astype(out[name].dtype))
    for name, factor in factors.items():
        out[name] = (out[name] * factor).astype(out[name].dtype)
    return out
```

```python
from contextlib import ExitStack

import concourse.bass as bass
from concourse import mybir

F32 = mybir.dt.float32
BF16 = mybir.dt.bfloat16
I32 = mybir.dt.int32
ACT = mybir.ActivationFunctionType
ALU = mybir.AluOpType
AX = mybir.AxisListType

P = 128
B, S, D = 32, 256, 128
NT = S // P
H, HD = 16, 8
HH = H // 2
E, F = 8, 512
FC = F // P
VW = 32
TOK = 256
REGION = B * S + TOK
SLOTS = {0: (2 * B * S + E * (TOK - 1)) // TOK, 1: (B * S + E * (TOK - 1)) // TOK}
SLOTS = {l: n + n % 2 for l, n in SLOTS.items()}
CHOICES = {0: 2, 1: 1}
PRODUCTS = [(0, 0), (0, 1), (0, 2), (1, 0), (1, 1), (2, 0)]
LIN = HD * len(PRODUCTS)
MROW = LIN + 2
KROWS = MROW + 2
SA, CA, GA, SB, CB, GB = range(6)
BIG = 3.0e38
EPS = {0: 1e-5, 1: 1e-5}
EPS_IN = 1e-6
EXP_SCALE = {0: (1.0, 2.0 ** -0.5), 1: (1.0, 1.0)}


class Signal:

    def __init__(self, handle, per):
        self.handle, self.per = handle, per

    def after(self, b, n=None):
        return 2 * self.per + b * self.per + (self.per if n is None else n)


class Transfers:

    def __init__(self, handles, dmas, begun=1):
        self.handles, self.step, self.begun = handles, 16 * dmas, begun

    def __getitem__(self, u):
        return self.handles[u]

    def start(self, eng):
        for h in self.handles:
            for x in h if isinstance(h, list) else [h]:
                eng.sem_inc(x, self.step * self.begun)

    def of(self, k):
        return self.step * (k + 1 + self.begun)


class Chain:

    def __init__(self, eng, handle):
        self.eng, self.handle, self.base, self.n = eng, handle, 0, 0

    def link(self, ins):
        self.mark(ins)
        self.settle()

    def mark(self, ins):
        ins.then_inc(self.handle, 1)
        self.n += 1

    def settle(self):
        self.eng.wait_ge(self.handle, self.base + self.n)

    def settle_apart(self):
        self.settle()
        self.apart()

    def apart(self):
        self.eng.sem_inc(self.handle, 1)
        self.n += 1

    def loop(self, i, per):
        self.base, self.n, self.entry, self.per = self.n_before + i * per, 0, self.n_before, per

    def before(self):
        self.n_before = self.base + self.n

    def done(self, times):
        assert self.n == self.per, (self.n, self.per)
        self.base, self.n = self.entry + times * self.per, 0


def build(nc, a, out):
    with ExitStack() as ctx:
        def sb(name, shape, dt=F32):
            return ctx.enter_context(nc.sbuf_tensor(name, shape, dt))

        def sem(name):
            return ctx.enter_context(nc.semaphore(name))

        def dram(name, shape, dt=F32):
            return nc.dram_tensor(name, shape, dt, kind="Internal").ap()

        mod_rows = [dram(f"mod_rows{l}", (B, 6 * D)) for l in range(2)]
        x_mid = [dram(f"x_mid{n}", (B * S, D)) for n in range(3)]
        gathered = [dram(f"gathered{l}", (E * REGION, D)) for l in range(2)]
        expert_out = [dram(f"expert_out{l}", (SLOTS[l] * TOK, D)) for l in range(2)]

        ident = sb("ident", [P, P])
        ident_b = sb("ident_b", [P, P], BF16)
        slope_ident = sb("slope_ident", [P, HH, P], BF16)
        dist = sb("dist", [P, 2, P], BF16)
        before_tri = sb("before_tri", [P, P], BF16)
        ones_b = sb("ones_b", [P, P], BF16)
        ones_row = sb("ones_row", [1, P])
        ones_col = sb("ones_col", [P, 1, 1])
        rev_iota = sb("rev_iota", [P, 2, E])
        region_row = sb("region_row", [P, E])
        tile_iota = sb("tile_iota", [P, SLOTS[0], E])
        zero_rows = sb("zero_rows", [P, TOK // P, D])
        wq, wk, wv = (sb(n, [P, 2, P]) for n in ("wq", "wk", "wv"))
        wo = sb("wo", [P, P])
        qk_bias = sb("qk_bias", [P, 2])
        q_scale = sb("q_scale", [P, 2])
        vo_bias = sb("vo_bias", [P, 2])
        out_bias = sb("out_bias", [P, 1])
        ln_cols = sb("ln_cols", [P, 3])
        gate_w = sb("gate_w", [P, 2, E])
        cT = sb("cT", [P, 2, B])
        silu = sb("silu", [P, 2, B])
        wmod = sb("wmod", [P, 2, 6 * D])
        modT = [sb(f"modT{l}", [P, 6, B]) for l in range(2)]
        gob = sb("gob", [P, B])
        mod_sb = sb("mod_sb", [B, 6 * D])
        w1 = sb("w1", [P, E, F])
        w2 = sb("w2", [P, E, FC, D])
        b1 = sb("b1", [P, E, FC])
        b2 = sb("b2", [1, E, D])

        X = [sb(f"X{u}", [P, NT, D]) for u in range(2)]
        XR = [sb(f"XR{u}", [P, NT, D]) for u in range(2)]
        X1 = [sb(f"X1{u}", [P, NT, D]) for u in range(2)]
        st = sb("st", [P, NT, 6])
        mv = [sb(f"mv{u}", [P, NT, 2]) for u in range(2)]
        rs = [sb(f"rs{u}", [P, NT]) for u in range(2)]
        xn = [sb(f"xn{u}", [P, NT, D]) for u in range(2)]
        hT = [sb(f"hT{u}", [P, S]) for u in range(2)]
        qk = sb("qk", [P, 2, S])
        rem = sb("rem", [P, 2, S])
        parts = [sb(f"parts{u}", [P, 2, 3, S], BF16) for u in range(2)]
        stack = [sb(f"stack{u}", [KROWS, H, 2, S], BF16) for u in range(2)]
        vals = [sb(f"vals{u}", [P, NT, H, VW]) for u in range(2)]
        mx = [sb(f"mx{u}", [P, H, NT]) for u in range(2)]
        mneg = sb("mneg", [P, 2, NT, 2, HH], BF16)
        mrow = [sb(f"mrow{u}", [2 * HH, S], BF16) for u in range(2)]
        probs = [sb(f"probs{n}", [P, 2, NT, S]) for n in range(4)]
        heads = [sb(f"heads{n}", [P, S]) for n in range(2)]
        rsum = sb("rsum", [P, NT, 4])
        On = [sb(f"On{u}", [P, NT, H, HD]) for u in range(2)]
        OnT = sb("OnT", [P, S])
        yT = sb("yT", [P, S])
        st2 = sb("st2", [P, NT, 6])
        mv2 = sb("mv2", [P, NT, 2])
        rs2 = sb("rs2", [P, NT])
        xn2 = sb("xn2", [P, NT, D])
        rows = [sb(f"rows{u}", [P, 5, D]) for u in range(2)]
        gb_row = [sb(f"gb_row{u}", [P, 1, D]) for u in range(2)]
        lnrow = sb("lnrow", [P, 2, D])
        h2 = [sb(f"h2{u}", [P, NT, D]) for u in range(2)]
        h3 = [sb(f"h3{u}", [P, NT, D]) for u in range(2)]
        h2T = sb("h2T", [P, S])
        newt = sb("newt", [P, 4, NT])
        lg = sb("lg", [P, NT, E])
        rt = sb("rt", [P, 8, NT, E])
        r1 = sb("r1", [P, 16, NT])
        sel = sb("sel", [P, NT, E], BF16)
        chosen = sb("chosen", [P, B, 2, NT, E])
        slotf = sb("slotf", [P, B, 2, NT])
        slot_in = [sb(f"slot_in{u}", [P, 2, NT], I32) for u in range(2)]
        wtok = sb("wtok", [P, B, 2, NT])
        run = sb("run", [P, E])
        run_i = sb("run_i", [P, E], I32)
        cnt_i = sb("cnt_i", [P, E], I32)
        n_tiles = sb("n_tiles", [P, E])
        tile_base = sb("tile_base", [P, E + 1])
        corr = sb("corr", [P, E])
        reached = sb("reached", [P, SLOTS[0], E])
        tile_tab = sb("tile_tab", [P, 4, SLOTS[0]])
        tile_e = sb("tile_e", [P, SLOTS[0]], I32)
        tile_row = sb("tile_row", [P, SLOTS[0]], I32)
        yslotf = sb("yslotf", [P, B, 2, NT])
        yslot = sb("yslot", [P, B, 2, NT], I32)
        w1s = [sb(f"w1s{u}", [P, F]) for u in range(2)]
        xt = [sb(f"xt{u}", [P, NT, D]) for u in range(2)]
        xtT = [sb(f"xtT{u}", [P, TOK]) for u in range(2)]
        hid = [sb(f"hid{u}", [P, FC, TOK]) for u in range(2)]
        yt = [sb(f"yt{u}", [P, NT, D]) for u in range(2)]
        gslot = [sb(f"gslot{u}", [P, 2, NT], I32) for u in range(2)]
        Y = [sb(f"Y{u}", [P, 2, NT, D]) for u in range(2)]

        A = [ctx.enter_context(nc.psum_tensor(f"A{n}", [P, NT, S], F32)) for n in range(2)]
        Bp = [ctx.enter_context(nc.psum_tensor(f"B{n}", [P, 2, NT, S], F32)) for n in range(2)]
        M0 = ctx.enter_context(nc.psum_tensor("M0", [P, 512], F32))
        M1 = ctx.enter_context(nc.psum_tensor("M1", [P, 512], F32))
        M0b = M0[:, :].bitcast(BF16)

        x_view = [a["x"].rearrange("b (t p) d -> b p t d", p=P)] + [
            m.rearrange("(b t p) d -> b p t d", t=NT, p=P) for m in x_mid]

        loads = [
            (ident[:, :], a["ident"]), (ident_b[:, :], a["ident_b"].bitcast(BF16)), (slope_ident[:, :, :], a["slope_ident"].bitcast(BF16)),
            (dist[:, :, :], a["dist"].bitcast(BF16)), (before_tri[:, :], a["before_tri"].bitcast(BF16)), (ones_b[:, :], a["ones_b"].bitcast(BF16)),
            (rev_iota[:, :, :], a["rev_iota"]), (region_row[:, :], a["region_row"]),
            (tile_iota[:, :, :], a["tile_iota"]),
            (wq[:, :, :], a["wq"]), (wk[:, :, :], a["wk"]), (wv[:, :, :], a["wv"]), (wo[:, :], a["wo"]),
            (qk_bias[:, :], a["qk_bias"]), (q_scale[:, :], a["q_scale"]), (vo_bias[:, :], a["vo_bias"]),
            (ln_cols[:, :], a["ln_cols"]), (lnrow[:, :, :], a["ln_rows"].broadcast_to([P, 2, D])), (gate_w[:, :, :], a["gate_w"]), (cT[:, :, :], a["cT"]),
            (wmod[:, 0, :], a["wmod0"]), (wmod[:, 1, :], a["wmod1"]),
        ] + [(stack[u][LIN:KROWS, :, :, :], a["stack_rows0"].bitcast(BF16)) for u in range(2)]
        loaded, ready, modp, moded, mod_out = (sem(n) for n in
            ("setup_loaded", "setup_ready", "setup_products", "setup_modulation", "mod_rows_written"))
        set_act, set_dve = sem("setup_act_order"), sem("setup_dve_order")

        with nc.Block() as block:
            @block.sync
            def _(sp):
                for dst, src in loads:
                    sp.dma_start(dst, src).then_inc(loaded, 16)
                for l in range(2):
                    sp.wait_ge(moded, 8 * (l + 1))
                    sp.dma_start(mod_rows[l], mod_sb[:, :]).then_inc(mod_out, 16)
                    sp.wait_ge(mod_out, 16 * (l + 1))

            @block.scalar
            def _(act):
                act.wait_ge(loaded, 16 * len(loads))
                act.activation(silu[:, :, :], cT[:, :, :], ACT.Exp, scale=-1.0).then_inc(set_act, 1)

            @block.tensor
            def _(pe):
                pe.wait_ge(ready, 1)
                for l in range(2):
                    if l:
                        pe.wait_ge(moded, 8)
                    for j in range(6):
                        pe.matmul(M0[:, j * B:(j + 1) * B], wmod[:, l, j * D:(j + 1) * D], silu[:, l, :],
                                  start=True, stop=True)
                    pe.matmul(A[0][0:B, :, :].rearrange("p t s -> p (t s)"), silu[:, l, :], wmod[:, l, 0:512],
                              start=True, stop=True)
                    pe.matmul(A[1][0:B, 0, :], silu[:, l, :], wmod[:, l, 512:768], start=True, stop=True)\
                        .then_inc(modp, 1)
                pe.matmul(M1[:, 0:1], wo[:, :], vo_bias[:, 0:1], start=True, stop=True).then_inc(modp, 1)

            @block.vector
            def _(dve):
                ch = Chain(dve, set_dve)
                for u in range(2):
                    dve.memset(vals[u][:, :, :, :], 0.0).then_inc(set_dve, 1)
                dve.wait_ge(set_dve, 2)
                ch.n = 2
                for u in range(2):
                    ch.mark(dve.memset(vals[u][:, :, :, HD:HD + 1], 1.0))
                ch.mark(dve.memset(ones_row[:, :], 1.0))
                ch.mark(dve.memset(ones_col[:, :, :], 1.0))
                ch.mark(dve.memset(zero_rows[:, :, :], 0.0))
                dve.wait_ge(loaded, 16 * len(loads))
                ch.mark(dve.tensor_copy(run[:, :], region_row[:, :]))
                dve.wait_ge(set_act, 1)
                ch.link(dve.tensor_scalar(silu[:, :, :], silu[:, :, :], 1.0, None, ALU.add))
                ch.link(dve.reciprocal(silu[:, :, :], silu[:, :, :]))
                dve.tensor_tensor(silu[:, :, :], silu[:, :, :], cT[:, :, :], ALU.mult).then_inc(ready, 1)
                for l in range(2):
                    dve.wait_ge(modp, l + 1)
                    if l:
                        dve.wait_ge(mod_out, 16)
                    m = modT[l]
                    am = A[0][0:B, :, :].rearrange("p t s -> p (t s)")
                    ch.mark(dve.tensor_copy(m[:, :, :].rearrange("p j b -> p (j b)"), M0[:, 0:6 * B]))
                    ch.mark(dve.tensor_copy(mod_sb[:, 0:512], am))
                    ch.link(dve.tensor_copy(mod_sb[:, 512:768], A[1][0:B, 0, :]))
                    n = 0
                    for j in (CA, CB):
                        dve.tensor_scalar(m[:, j, :], m[:, j, :], 1.0, None, ALU.add).then_inc(moded, 1)
                        dve.tensor_scalar(mod_sb[:, j * D:(j + 1) * D], mod_sb[:, j * D:(j + 1) * D], 1.0, None,
                                          ALU.add).then_inc(moded, 1)
                    for j in (GA, GB):
                        for g, t in ((m[:, j, :], qk[:, 0, 0:B]), (mod_sb[:, j * D:(j + 1) * D], qk[0:B, 1, 0:D])):
                            ch.link(dve.tensor_scalar(t, g, 0.0, 2.0, ALU.is_ge, ALU.mult))
                            ch.link(dve.tensor_scalar(t, t, -1.0, None, ALU.add))
                            ch.link(dve.scalar_tensor_tensor(out=g, in0=g, scalar=-1.0, in1=g, op0=ALU.mult, op1=ALU.max))
                            dve.scalar_tensor_tensor(out=g, in0=g, scalar=0.25, in1=t, op0=ALU.max, op1=ALU.mult)\
                                .then_inc(moded, 1)
                dve.wait_ge(modp, 3)
                ch.link(dve.tensor_tensor(out_bias[:, :], M1[:, 0:1], vo_bias[:, 1:2], ALU.add))
                dve.wait_ge(moded, 16)
                ch.link(dve.tensor_scalar(gob[:, :], modT[0][:, GA, :], out_bias[:, 0:1], None, ALU.mult))

        for layer in range(2):
            with nc.cleanup_on_exit():
                attention(nc, layer, locals())
            with nc.cleanup_on_exit():
                experts(nc, layer, locals())
        with nc.cleanup_on_exit():
            combine(nc, locals())


def attention(nc, l, g):
    (X, XR, X1, st, mv, rs, xn, hT, qk, rem, parts, stack, vals, mx, mneg, mrow, probs, heads, rsum, On, OnT, yT,
     st2, mv2, rs2, xn2, rows, h2, h3, h2T, newt, lg, rt, r1, sel, chosen, slotf, slot_in, wtok, run) = (g[n] for n in (
        "X XR X1 st mv rs xn hT qk rem parts stack vals mx mneg mrow probs heads rsum On OnT yT "
        "st2 mv2 rs2 xn2 rows h2 h3 h2T newt lg rt r1 sel chosen slotf slot_in wtok run").split())
    A, Bp, M0, M1, M0b, ident, ident_b, slope_ident, dist = (g[n] for n in
        "A Bp M0 M1 M0b ident ident_b slope_ident dist".split())
    wq, wk, wv, wo, qk_bias, q_scale, modT, gob, gate_w, ln_cols = (g[n] for n in
        "wq wk wv wo qk_bias q_scale modT gob gate_w ln_cols".split())
    before_tri, ones_b, rev_iota, mod_rows, gathered, x_view, region_row = (g[n] for n in
        "before_tri ones_b rev_iota mod_rows gathered x_view region_row".split())
    gb_row, ones_col, lnrow, gslot, Y, yslot, expert_out, XR, a, w1, w2, b1, b2 = (g[n] for n in
        "gb_row ones_col lnrow gslot Y yslot expert_out XR a w1 w2 b1 b2".split())
    n_choice = CHOICES[l]
    mod = modT[l]

    def sem(name):
        return nc.alloc_semaphore(f"L{l}_{name}")

    def signal(name, per):
        return Signal(sem(name), per)

    def signals(*names, per=1):
        return [signal(n, per) for n in names]

    weights_in, lin_in = sem("weights_in"), sem("lin_in")

    def transfers(name, dmas, begun=1):
        return Transfers([sem(f"{name}{u}") for u in range(2)], dmas, begun)

    x_in = transfers("x_in", 1)
    rows_in = transfers("rows_in", l + 1)
    stack_in = Transfers([[sem(f"stack_in{u}{h}") for h in range(2)] for u in range(2)], len(PRODUCTS))
    m_in = Transfers([[sem(f"m_in{u}{h}") for h in range(2)] for u in range(2)], 1)
    x1_out = transfers("x1_out", 1)
    scat_out = transfers("rows_out", NT * n_choice, 0)
    if l == 1:
        y_in = transfers("y_in", 2 * NT, 0)

    stats, xn_ready, qk_f32, x1_ready, stats2, xn2_ready, logits_read, slots_ready, pos_read = signals(
        "stats", "xn_ready", "qk_f32", "x1_ready", "stats2", "xn2_ready", "logits_read", "slots_ready", "pos_read")
    sel_ready, w_den = signals("sel_ready", "w_den")
    a_max, o_norm, m_split = signal("a_max", H), signal("o_norm", 4), signal("m_split", 2)
    rsqrt, h_ready, v_ready, onT_read, y_read, rsqrt2, h2T_read, w_exp = signals(
        "rsqrt", "h_ready", "v_ready", "onT_read", "y_read", "rsqrt2", "h2T_read", "w_exp")
    mT_read, b_exp, o_read = signal("mT_read", 2), signal("b_exp", HH), signal("o_read", 4)
    xn_T, qk_proj, v_proj, on_T, y_proj, y_T, h2_T, logits, pos = signals(
        "xn_T", "qk_proj", "v_proj", "on_T", "y_proj", "y_T", "h2_T", "logits", "pos")
    a_scores, m_T, b_scores, pv, o_T = (signal("a_scores", H), signal("m_T", 2), signal("b_scores", HH),
                                        signal("pv", 4), signal("o_T", 4))
    split, h2_ready, scattered = signals("split", "h2_ready", "scattered")
    if l == 1:
        h3_ready = signal("h3_ready", 1)
        gslot_ready, x2_ready, h_rows, base_ready, h_stats, h_rsqrt, rms_stats, rms_rsqrt = signals(
            "gslot_ready", "x2_ready", "h_rows", "base_ready", "h_stats", "h_rsqrt", "rms_stats", "rms_rsqrt")
    dve_order, act_order, pool_order = sem("dve_order"), sem("act_order"), sem("pool_order")

    def start(eng, *sigs):
        for s in sigs:
            eng.sem_inc(s.handle, 2 * s.per)

    with nc.Block() as block:

        @block.sync
        def _(sp):
            def load_x(b, k, u):
                sp.wait_ge(x1_ready.handle, x1_ready.after(b - 2))
                if l == 1:
                    sp.dma_start(X[u][:, :, :], x_view[1][bass.ds(b, 1)].rearrange("o p t d -> (o p) t d")).then_inc(x_in[u], 16)
                    sp.wait_ge(h2_ready.handle, h2_ready.after(b - 2))
                    sp.dma_start(rows[u][:, :, :], mod_rows[1][bass.ds(b, 1), 0:(CB + 1) * D]
                                 .rearrange("o (j d) -> o j d", j=5).broadcast_to([P, 5, D])).then_inc(rows_in[u], 16)
                    sp.dma_start(gb_row[u][:, :, :], mod_rows[0][bass.ds(b, 1), GB * D:(GB + 1) * D]
                                 .rearrange("o (j d) -> o j d", j=1).broadcast_to([P, 1, D])).then_inc(rows_in[u], 16)
                    return
                sp.dma_start(X[u][:, :, :], x_view[l][bass.ds(b, 1)].rearrange("o p t d -> (o p) t d")).then_inc(x_in[u], 16)
                sp.wait_ge(h2_ready.handle, h2_ready.after(b - 2))
                sp.dma_start(rows[u][:, 3:5, :], mod_rows[l][bass.ds(b, 1), SB * D:(CB + 1) * D]
                             .rearrange("o (j d) -> o j d", j=2).broadcast_to([P, 2, D])).then_inc(rows_in[u], 16)

            def stack_up(b, k, u, half):
                if half == 0:
                    sp.wait_ge(split.handle, split.after(b))
                sp.wait_ge(b_scores.handle, b_scores.after(b - 2, 4 * half + 4))
                for r, (pq, pk) in enumerate(PRODUCTS):
                    src = parts[u][:, :, :, :].rearrange("p q r s -> p (q r) s")
                    sp.dma_start(stack[u][HD * r:HD * r + HD, HH * half:HH * half + HH, :, :],
                                 src[64 * half:64 * half + 64, pq:4 + pk:3 + pk - pq, :])\
                        .then_inc(stack_in[u][half], 16)

            def stack_max(b, k, u, half):
                sp.wait_ge(mT_read.handle, mT_read.after(b, half + 1))
                sp.dma_start(stack[u][MROW:MROW + 2, HH * half:HH * half + HH, 0, :], mrow[half][:, :])\
                    .then_inc(m_in[u][half], 16)

            def store_x1(b, k, u):
                sp.wait_ge(x1_ready.handle, x1_ready.after(b))
                sp.dma_start(x_view[1 + 2 * l][bass.ds(b, 1)].rearrange("o p t d -> (o p) t d"), X1[u][:, :, :]).then_inc(x1_out[u], 16)

            for t in (x_in, rows_in, stack_in, m_in, x1_out):
                t.start(sp)
            weights = [(w1[:, :, :], a[f"w1_{l}"]), (w2[:, :, :, :], a[f"w2_{l}"])]
            if l == 1:
                weights += [(b1[:, :, :], a["b1"]), (b2[:, :, :], a["b2"])]
                for u in range(2):
                    sp.dma_start(stack[u][LIN:KROWS, :, :, :], a["stack_rows1"].bitcast(BF16)).then_inc(lin_in, 16)
                sp.wait_ge(lin_in, 32)
            for dst, src in weights:
                sp.dma_start(dst, src).then_inc(weights_in, 16)
            with sp.Fori(0, B // 2) as k:
                for u in range(2):
                    b = k * 2 + u
                    load_x(b, k, u)
                    stack_up(b, k, u, 0)
                    stack_up(b, k, u, 1)
                    stack_max(b, k, u, 0)
                    stack_max(b, k, u, 1)
                    store_x1(b, k, u)
            sp.wait_ge(weights_in, 16 * len(weights))
            for u in range(2):
                sp.wait_ge(x1_out[u], x1_out.of(B // 2 - 1))

        @block.gpsimd
        def _(pool):
            start(pool, split, h2_ready, scattered, *([base_ready] if l else []))
            ch = Chain(pool, pool_order)

            def split_qk(b, k, u):
                pool.wait_ge(qk_f32.handle, qk_f32.after(b))
                for half in range(2):
                    pool.wait_ge(stack_in[u][half], stack_in.of(k - 1))
                p = parts[u]
                one = ones_col[:, :, :].broadcast_to([P, 2, S])
                ch.link(pool.tensor_tensor(p[:, :, 0, :], qk[:, :, :], one, ALU.mult))
                ch.link(pool.tensor_tensor(rem[:, :, :], qk[:, :, :], p[:, :, 0, :], ALU.subtract))
                ch.link(pool.tensor_tensor(p[:, :, 1, :], rem[:, :, :], one, ALU.mult))
                pool.tensor_tensor(p[:, :, 2, :], rem[:, :, :], p[:, :, 1, :], ALU.subtract).then_inc(split.handle, 1)

            def gather(b, k, u):
                pool.wait_ge(gslot_ready.handle, gslot_ready.after(b))
                pool.wait_ge(x2_ready.handle, x2_ready.after(b - 2))
                ch.apart()
                for c in range(2):
                    for t in range(NT):
                        pool.indirect_dma_start(Y[u][:, c, t, :], None, expert_out[0],
                                                bass.IndirectOffsetOnAxis(ap=gslot[u][:, c, t:t + 1], axis=0))\
                            .then_inc(y_in[u], 16)

            def residual_base(b, k, u):
                pool.wait_ge(xn_ready.handle, xn_ready.after(b))
                pool.wait_ge(x1_ready.handle, x1_ready.after(b - 2))
                ch.link(pool.tensor_tensor(XR[u][:, :, :], xn[u][:, :, :], lnrow[:, 0:1, :].broadcast_to([P, NT, D]), ALU.mult))
                ch.link(pool.tensor_tensor(XR[u][:, :, :], XR[u][:, :, :], lnrow[:, 1:2, :].broadcast_to([P, NT, D]), ALU.add))
                ch.link(pool.tensor_tensor(XR[u][:, :, :], XR[u][:, :, :], rows[u][:, GA:GA + 1, :].broadcast_to([P, NT, D]), ALU.mult))
                pool.tensor_tensor(XR[u][:, :, :], XR[u][:, :, :], X[u][:, :, :], ALU.add).then_inc(base_ready.handle, 1)

            def modulate(b, k, u):
                pool.wait_ge(xn2_ready.handle, xn2_ready.after(b))
                pool.wait_ge(rows_in[u], rows_in.of(k))
                pool.wait_ge(scattered.handle, scattered.after(b - 2))
                ch.link(pool.tensor_tensor(h2[u][:, :, :], xn2[:, :, :],
                                           rows[u][:, CB:CB + 1, :].broadcast_to([P, NT, D]), ALU.mult))
                pool.tensor_tensor(h2[u][:, :, :], h2[u][:, :, :],
                                   rows[u][:, SB:SB + 1, :].broadcast_to([P, NT, D]), ALU.add).then_inc(h2_ready.handle, 1)

            def scatter(b, k, u):
                pool.wait_ge(slots_ready.handle, slots_ready.after(b))
                ch.apart()
                for c in range(n_choice):
                    for t in range(NT):
                        pool.indirect_dma_start(gathered[l], bass.IndirectOffsetOnAxis(ap=slot_in[u][:, c, t:t + 1], axis=0),
                                                (h3 if l else h2)[u][:, t, :], None).then_inc(scat_out[u], 16)

            def scatter_done(b, k, u):
                pool.wait_ge(scat_out[u], scat_out.of(k))
                pool.sem_inc(scattered.handle, 1)

            ch.before()
            with pool.Fori(0, B // 2) as k:
                ch.loop(k, 2 * (9 if l else 5))
                for u in range(2):
                    b = k * 2 + u
                    if l == 1:
                        gather(b, k, u)
                        residual_base(b, k, u)
                    split_qk(b, k, u)
                    modulate(b, k, u)
                    scatter(b, k, u)
                    scatter_done(b, k, u)
                assert ch.n == ch.per

        @block.scalar
        def _(act):
            start(act, rsqrt, h_ready, v_ready, onT_read, y_read, rsqrt2, h2T_read, w_exp, mT_read, b_exp, o_read)
            if l == 1:
                start(act, h_rsqrt, rms_rsqrt)
            ch = Chain(act, act_order)
            act.preload_act_table_set("natural_log_exp_and_others")

            def rsqrt_of(b, var, dst, ready, sig):
                act.wait_ge(ready.handle, ready.after(b))
                ch.link(act.activation(dst, var, ACT.Ln))
                act.activation(dst, dst, ACT.Exp, scale=-0.5).then_inc(sig.handle, 1)

            def first_h(b, k, u):
                act.wait_ge(xn_T.handle, xn_T.after(b))
                act.activation(hT[u][:, :], M0[:, 0:S], ACT.Identity,
                               bias=ln_cols[:, 1:2] if l else mod[:, SA, bass.ds(b, 1)],
                               scale=ln_cols[:, 0:1] if l else mod[:, CA, bass.ds(b, 1)]).then_inc(h_ready.handle, 1)

            def values(b, k, u):
                act.wait_ge(v_proj.handle, v_proj.after(b))
                act.wait_ge(pv.handle, pv.after(b - 2))
                act.activation(vals[u][:, :, :, 0:HD],
                               M0[:, 0:NT * D].rearrange("p (t h d) -> p t h d", t=NT, h=H), ACT.Copy)\
                    .then_inc(v_ready.handle, 1)

            def max_rows(b, k, u, half):
                act.wait_ge(m_T.handle, m_T.after(b, half + 1))
                act.wait_ge(m_in[1 - u][half], m_in.of(k - 1 + u))
                act.activation(mrow[half][:, :], M0b[0:2 * HH, 0:S], ACT.Copy).then_inc(mT_read.handle, 1)

            def exps(b, k, u, c):
                act.wait_ge(b_scores.handle, b_scores.after(b, c + 1))
                g4 = c // 2
                act.wait_ge(pv.handle, pv.after(b, g4 - 1) if g4 >= 2 else pv.after(b - 1, g4 + 3))
                act.activation(probs[c % 4][:, :, :, :], Bp[c % 2][:, :, :, :], ACT.Exp,
                               scale=EXP_SCALE[l][c // 4]).then_inc(b_exp.handle, 1)

            def head_sums(b, k, u, g):
                act.wait_ge(pv.handle, pv.after(b, g + 1))
                act.activation(heads[g % 2][:, :], M1[:, 0:S], ACT.Copy).then_inc(o_read.handle, 1)

            def back(b, k, u):
                act.wait_ge(on_T.handle, on_T.after(b))
                act.activation(OnT[:, :], M0[:, 0:S], ACT.Copy).then_inc(onT_read.handle, 1)
                act.wait_ge(y_proj.handle, y_proj.after(b))
                act.activation(yT[:, :], M0[:, 0:S], ACT.Identity, bias=gob[:, bass.ds(b, 1)],
                               scale=mod[:, GA, bass.ds(b, 1)]).then_inc(y_read.handle, 1)

            def second_h(b, k, u):
                act.wait_ge(h2_T.handle, h2_T.after(b))
                if l:
                    act.activation(h2T[:, :], M0[:, 0:S], ACT.Identity, scale=ln_cols[:, 2:3]).then_inc(h2T_read.handle, 1)
                else:
                    act.activation(h2T[:, :], M0[:, 0:S], ACT.Copy).then_inc(h2T_read.handle, 1)

            def weights(b, k, u):
                act.wait_ge(w_den.handle, w_den.after(b))
                if l:
                    act.activation(rt[:, 4, :, :], rt[:, 3, :, :], ACT.Exp).then_inc(w_exp.handle, 1)
                else:
                    act.activation(r1[:, 5, :], r1[:, 4, :], ACT.Exp).then_inc(w_exp.handle, 1)

            ch.before()
            with act.Fori(0, B // 2) as k:
                ch.loop(k, 2 * (4 if l else 2))
                for u in range(2):
                    b = k * 2 + u
                    rsqrt_of(b, mv[u][:, :, 1], rs[u][:, :], stats, rsqrt)
                    if l:
                        rsqrt_of(b, mv[u][:, :, 1], rs[u][:, :], h_stats, h_rsqrt)
                    first_h(b, k, u)
                    values(b, k, u)
                    max_rows(b, k, u, 0)
                    max_rows(b, k, u, 1)
                    for c in range(HH):
                        exps(b, k, u, c)
                        if c % 2:
                            head_sums(b, k, u, c // 2)
                    if l == 0:
                        back(b, k, u)
                    rsqrt_of(b, mv2[:, :, 1], rs2[:, :], stats2, rsqrt2)
                    if l:
                        rsqrt_of(b, mv2[:, :, 1], rs2[:, :], rms_stats, rms_rsqrt)
                    second_h(b, k, u)
                    weights(b, k, u)
                assert ch.n == ch.per

        @block.vector
        def _(dve):
            start(dve, stats, xn_ready, qk_f32, x1_ready, stats2, xn2_ready, logits_read, slots_ready, pos_read,
                  sel_ready, w_den, a_max, o_norm, m_split)
            if l == 1:
                start(dve, gslot_ready, x2_ready, h_rows, h_stats, rms_stats, h3_ready)
            ch = Chain(dve, dve_order)
            if l == 1:
                ch.link(dve.tensor_copy(run[:, :], region_row[:, :]))

            def moments(b, x, st, mv, sig, eps=EPS[l]):
                for t in range(NT):
                    ch.mark(dve.bn_stats(st[:, t, :], x[:, t, :]))
                ch.settle_apart()
                for t in range(NT):
                    ch.mark(dve.bn_aggr(mv[:, t, :], st[:, t, :]))
                ch.settle()
                dve.tensor_scalar(mv[:, :, 1], mv[:, :, 1], eps, None, ALU.add).then_inc(sig.handle, 1)

            def newton(mv, rs):
                n = newt
                ch.link(dve.tensor_tensor(n[:, 0, :], mv[:, :, 1], rs[:, :], ALU.mult))
                ch.link(dve.scalar_tensor_tensor(out=n[:, 1, :], in0=n[:, 0, :], scalar=-0.5, in1=rs[:, :],
                                                 op0=ALU.mult, op1=ALU.mult))
                ch.link(dve.scalar_tensor_tensor(out=n[:, 2, :], in0=n[:, 1, :], scalar=1.5, in1=rs[:, :],
                                                 op0=ALU.add, op1=ALU.mult))

            def normed(b, x, mv, rs, dst, sig):
                newton(mv, rs)
                n = newt
                for t in range(NT):
                    ins = dve.tensor_scalar(dst[:, t, :], x[:, t, :], mv[:, t, 0:1], n[:, 2, t:t + 1],
                                            ALU.subtract, ALU.mult)
                    if t < NT - 1:
                        ch.mark(ins)
                ch.settle()
                ins.then_inc(sig.handle, 1)

            def first_norm(b, k, u):
                dve.wait_ge(x_in[u], x_in.of(k))
                moments(b, X[u], st, mv[u], stats)
                dve.wait_ge(rsqrt.handle, rsqrt.after(b))
                dve.wait_ge(xn_T.handle, xn_T.after(b - 2))
                normed(b, X[u], mv[u], rs[u], xn[u], xn_ready)

            def gather_slots(b, k, u):
                dve.tensor_scalar(gslot[u][:, :, :], yslot[:, bass.ds(b, 1), :, :].rearrange("p o c t -> p (o c) t"), 1.0, None, ALU.mult)\
                    .then_inc(gslot_ready.handle, 1)

            def add_experts(b, k, u):
                dve.wait_ge(y_in[u], y_in.of(k))
                dve.wait_ge(rows_in[u], rows_in.of(k))
                dve.wait_ge(x_in[u], x_in.of(k))
                y = Y[u]
                for t in range(NT):
                    ch.mark(dve.tensor_scalar(y[:, 0, t, :], y[:, 0, t, :],
                                              wtok[:, bass.ds(b, 1), 0, t:t + 1].rearrange("p o t -> p (o t)"), None, ALU.mult))
                ch.settle()
                for t in range(NT):
                    ch.mark(dve.scalar_tensor_tensor(out=y[:, 0, t, :], in0=y[:, 1, t, :],
                                                     scalar=wtok[:, bass.ds(b, 1), 1, t:t + 1].rearrange("p o t -> p (o t)"),
                                                     in1=y[:, 0, t, :], op0=ALU.mult, op1=ALU.add))
                ch.settle()
                ch.link(dve.tensor_tensor(y[:, 0, :, :], y[:, 0, :, :], gb_row[u][:, :, :].broadcast_to([P, NT, D]), ALU.mult))
                dve.tensor_tensor(X[u][:, :, :], X[u][:, :, :], y[:, 0, :, :], ALU.add).then_inc(x2_ready.handle, 1)

            def first_norm_twice(b, k, u):
                dve.wait_ge(x2_ready.handle, x2_ready.after(b))
                moments(b, X[u], st, mv[u], stats)
                dve.wait_ge(rsqrt.handle, rsqrt.after(b))
                dve.wait_ge(xn_T.handle, xn_T.after(b - 2))
                dve.wait_ge(base_ready.handle, base_ready.after(b - 2))
                normed(b, X[u], mv[u], rs[u], xn[u], h_rows)
                dve.wait_ge(h_rows.handle, h_rows.after(b))
                ch.link(dve.tensor_tensor(xn[u][:, :, :], xn[u][:, :, :], rows[u][:, CA:CA + 1, :].broadcast_to([P, NT, D]), ALU.mult))
                ch.link(dve.tensor_tensor(xn[u][:, :, :], xn[u][:, :, :], rows[u][:, SA:SA + 1, :].broadcast_to([P, NT, D]), ALU.add))
                moments(b, xn[u], st, mv[u], h_stats, EPS_IN)
                dve.wait_ge(h_rsqrt.handle, h_rsqrt.after(b))
                normed(b, xn[u], mv[u], rs[u], xn[u], xn_ready)

            def residual_rows(b, k, u):
                dve.wait_ge(o_norm.handle, o_norm.after(b))
                dve.wait_ge(base_ready.handle, base_ready.after(b))
                dve.wait_ge(x1_out[u], x1_out.of(k - 1))
                dve.wait_ge(stats2.handle, stats2.after(b - 1))
                ch.link(dve.tensor_tensor(X1[u][:, :, :], On[u][:, :, :, :].rearrange("p t h d -> p t (h d)"),
                                          rows[u][:, GA:GA + 1, :].broadcast_to([P, NT, D]), ALU.mult))
                dve.tensor_tensor(X1[u][:, :, :], X1[u][:, :, :], XR[u][:, :, :], ALU.add).then_inc(x1_ready.handle, 1)

            def rms_norm(b, k, u):
                dve.wait_ge(h2_ready.handle, h2_ready.after(b))
                for t in range(NT):
                    ch.mark(dve.bn_stats(st2[:, t, :], h2[u][:, t, :]))
                ch.settle_apart()
                for t in range(NT):
                    ch.mark(dve.bn_aggr(mv2[:, t, :], st2[:, t, :]))
                ch.settle()
                ch.link(dve.tensor_tensor(mv2[:, :, 0], mv2[:, :, 0], mv2[:, :, 0], ALU.mult))
                dve.scalar_tensor_tensor(out=mv2[:, :, 1], in0=mv2[:, :, 1], scalar=EPS_IN, in1=mv2[:, :, 0],
                                         op0=ALU.add, op1=ALU.add).then_inc(rms_stats.handle, 1)
                dve.wait_ge(rms_rsqrt.handle, rms_rsqrt.after(b))
                newton(mv2, rs2)
                dve.wait_ge(scattered.handle, scattered.after(b - 2))
                for t in range(NT):
                    ch.mark(dve.tensor_scalar(h3[u][:, t, :], h2[u][:, t, :], newt[:, 2, t:t + 1], None, ALU.mult))
                ch.settle()
                dve.tensor_copy(r1[:, 12, :], newt[:, 2, :]).then_inc(h3_ready.handle, 1)

            def choose_one(b, k, u):
                dve.wait_ge(logits.handle, logits.after(b))
                dve.tensor_copy(lg[:, :, :], M0[:, 0:NT * E].rearrange("p (t e) -> p t e", t=NT))\
                    .then_inc(logits_read.handle, 1)
                dve.wait_ge(logits_read.handle, logits_read.after(b))
                first_of(lg[:, :, :], r1[:, 0, :], rt[:, 0, :, :], rt[:, 1, :, :], r1[:, 1, :], rt[:, 2, :, :])
                ch.mark(dve.tensor_scalar(chosen[:, bass.ds(b, 1), 0, :, :], rt[:, 2, :, :].unsqueeze(1), 1.0, None, ALU.mult))
                dve.tensor_tensor(rt[:, 3, :, :], lg[:, :, :], r1[:, 0, :].unsqueeze(2).broadcast_to([P, NT, E]),
                                  ALU.subtract).then_inc(w_den.handle, 1)
                dve.wait_ge(pos.handle, pos.after(b - 1))
                dve.tensor_copy(sel[:, :, :], rt[:, 2, :, :]).then_inc(sel_ready.handle, 1)
                dve.wait_ge(w_exp.handle, w_exp.after(b))
                ch.link(dve.tensor_reduce(r1[:, 6, :], rt[:, 4, :, :], AX.X, ALU.add))
                ch.link(dve.reciprocal(r1[:, 7, :], r1[:, 6, :]))
                ch.link(dve.tensor_scalar(wtok[:, bass.ds(b, 1), 0, :], r1[:, 7, :].unsqueeze(1), 1.0, None, ALU.mult))

            def read_qk(b, k, u):
                dve.wait_ge(qk_proj.handle, qk_proj.after(b))
                dve.wait_ge(split.handle, split.after(b - 1))
                m = M0[:, :].rearrange("p (j s) -> p j s", j=2)
                if l:
                    ch.link(dve.tensor_scalar(qk[:, 0, :], m[:, 0, :], q_scale[:, 1:2], None, ALU.mult))
                    dve.tensor_copy(qk[:, 1, :], m[:, 1, :]).then_inc(qk_f32.handle, 1)
                    return
                ch.link(dve.tensor_scalar(qk[:, 0, :], m[:, 0, :], qk_bias[:, 0:1], q_scale[:, 0:1],
                                          ALU.add, ALU.mult))
                dve.tensor_scalar(qk[:, 1, :], m[:, 1, :], qk_bias[:, 1:2], None, ALU.add).then_inc(qk_f32.handle, 1)

            def row_max(b, k, u, h):
                dve.wait_ge(a_scores.handle, a_scores.after(b, h + 1))
                if h == 0:
                    dve.wait_ge(m_split.handle, m_split.after(b - 1))
                dve.tensor_reduce(mx[u][:, h, :], A[h % 2][:, :, :], AX.X, ALU.max).then_inc(a_max.handle, 1)

            def split_max(b, k, u, half):
                dve.wait_ge(a_max.handle, a_max.after(b, HH * (half + 1)))
                dve.wait_ge(m_T.handle, m_T.after(b - 1, half + 1))
                v = mx[u][:, HH * half:HH * half + HH, :].rearrange("p h t -> p t h")
                ch.link(dve.tensor_scalar(mneg[:, half, :, 0, :], v, -1.0, None, ALU.mult))
                dve.scalar_tensor_tensor(out=mneg[:, half, :, 1, :], in0=v, scalar=-1.0, in1=mneg[:, half, :, 0, :],
                                         op0=ALU.mult, op1=ALU.subtract).then_inc(m_split.handle, 1)

            def normalise(b, k, u, g):
                dve.wait_ge(o_T.handle, o_T.after(b, g + 1))
                if g == 0:
                    if l:
                        dve.wait_ge(x1_ready.handle, x1_ready.after(b - 2))
                    else:
                        dve.wait_ge(on_T.handle, on_T.after(b - 2))
                o = M1[:, S:2 * S].rearrange("p (t j w) -> p t j w", t=NT, j=4)
                ch.link(dve.reciprocal(rsum[:, :, :], o[:, :, :, HD]))
                dst = On[u][:, :, 4 * g:4 * g + 4, :] if l == 0 else \
                    On[u][:, :, :, :].rearrange("p t (h f) d -> p t f h d", f=2)[:, :, g // 2, 4 * (g % 2):4 * (g % 2) + 4, :]
                dve.tensor_tensor(dst, o[:, :, :, 0:HD],
                                  rsum[:, :, :].unsqueeze(3).broadcast_to([P, NT, 4, HD]), ALU.mult)\
                    .then_inc(o_norm.handle, 1)

            def residual(b, k, u):
                dve.wait_ge(y_T.handle, y_T.after(b))
                dve.wait_ge(x1_out[u], x1_out.of(k - 1))
                dve.tensor_tensor(X1[u][:, :, :], X[u][:, :, :], M0[:, 0:S].rearrange("p (t d) -> p t d", t=NT),
                                  ALU.add).then_inc(x1_ready.handle, 1)

            def second_norm(b, k, u):
                dve.wait_ge(x1_ready.handle, x1_ready.after(b))
                moments(b, X1[u], st2, mv2, stats2)
                dve.wait_ge(rsqrt2.handle, rsqrt2.after(b))
                dve.wait_ge(h2_ready.handle, h2_ready.after(b - 1))
                normed(b, X1[u], mv2, rs2, xn2, xn2_ready)

            def first_of(src, top, eq, cand, idx, dst):
                ch.link(dve.tensor_reduce(top, src, AX.X, ALU.max))
                ch.link(dve.tensor_tensor(eq, src, top.unsqueeze(2).broadcast_to([P, NT, E]), ALU.is_equal))
                ch.link(dve.tensor_tensor(cand, eq, rev_iota[:, :, :], ALU.mult))
                ch.link(dve.tensor_reduce(idx, cand, AX.X, ALU.max))
                ch.link(dve.tensor_tensor(dst, rev_iota[:, :, :], idx.unsqueeze(2).broadcast_to([P, NT, E]),
                                          ALU.is_equal))

            def choose(b, k, u):
                dve.wait_ge(logits.handle, logits.after(b))
                dve.tensor_copy(lg[:, :, :], M0[:, 0:NT * E].rearrange("p (t e) -> p t e", t=NT))\
                    .then_inc(logits_read.handle, 1)
                dve.wait_ge(logits_read.handle, logits_read.after(b))
                first_of(lg[:, :, :], r1[:, 0, :], rt[:, 0, :, :], rt[:, 1, :, :], r1[:, 1, :], rt[:, 2, :, :])
                ch.mark(dve.tensor_scalar(chosen[:, bass.ds(b, 1), 0, :, :], rt[:, 2, :, :].unsqueeze(1), 1.0, None, ALU.mult))
                ch.link(dve.scalar_tensor_tensor(out=rt[:, 3, :, :], in0=rt[:, 2, :, :], scalar=-BIG, in1=lg[:, :, :],
                                                 op0=ALU.mult, op1=ALU.add))
                first_of(rt[:, 3, :, :], r1[:, 2, :], rt[:, 0, :, :], rt[:, 1, :, :], r1[:, 3, :], rt[:, 4, :, :])
                ch.mark(dve.tensor_scalar(chosen[:, bass.ds(b, 1), 1, :, :], rt[:, 4, :, :].unsqueeze(1), 1.0, None, ALU.mult))
                dve.tensor_tensor(r1[:, 4, :], r1[:, 2, :], r1[:, 0, :], ALU.subtract).then_inc(w_den.handle, 1)
                dve.wait_ge(pos.handle, pos.after(b - 1))
                dve.tensor_tensor(sel[:, :, :], rt[:, 2, :, :], rt[:, 4, :, :], ALU.add).then_inc(sel_ready.handle, 1)
                dve.wait_ge(w_exp.handle, w_exp.after(b))
                ch.link(dve.tensor_scalar(r1[:, 6, :], r1[:, 5, :], 1.0, None, ALU.add))
                ch.link(dve.reciprocal(r1[:, 7, :], r1[:, 6, :]))
                ch.mark(dve.tensor_scalar(wtok[:, bass.ds(b, 1), 0, :], r1[:, 7, :].unsqueeze(1), 1.0, None, ALU.mult))
                ch.link(dve.tensor_tensor(wtok[:, bass.ds(b, 1), 1, :], r1[:, 5, :].unsqueeze(1),
                                          r1[:, 7, :].unsqueeze(1), ALU.mult))

            def place(b, k, u):
                dve.wait_ge(pos.handle, pos.after(b))
                dve.wait_ge(scattered.handle, scattered.after(b - 2))
                ch.link(dve.tensor_tensor(rt[:, 5, :, :], M0[:, 0:NT * E].rearrange("p (t e) -> p t e", t=NT),
                                          run[:, :].unsqueeze(1).broadcast_to([P, NT, E]), ALU.add))
                dve.tensor_tensor(run[:, :], run[:, :], M0[:, NT * E:NT * E + E], ALU.add)\
                    .then_inc(pos_read.handle, 1)
                for c in range(n_choice):
                    ch.link(dve.tensor_tensor(rt[:, 6, :, :], rt[:, 2 + 2 * c, :, :], rt[:, 5, :, :], ALU.mult))
                    ch.link(dve.tensor_reduce(r1[:, 8 + c, :], rt[:, 6, :, :], AX.X, ALU.add))
                ch.mark(dve.tensor_scalar(slotf[:, bass.ds(b, 1), 0:n_choice, :],
                                        r1[:, 8:8 + n_choice, :].unsqueeze(1), 1.0, None, ALU.mult))
                ch.settle()
                dve.wait_ge(pos_read.handle, pos_read.after(b))
                dve.tensor_copy(slot_in[u][:, 0:n_choice, :], r1[:, 8:8 + n_choice, :]).then_inc(slots_ready.handle, 1)

            ch.before()
            with dve.Fori(0, B // 2) as k:
                ch.loop(k, 2 * (66 if l else 48))
                for u in range(2):
                    b = k * 2 + u
                    if l:
                        gather_slots(b, k, u)
                        add_experts(b, k, u)
                        first_norm_twice(b, k, u)
                    else:
                        first_norm(b, k, u)
                    read_qk(b, k, u)
                    for half in range(2):
                        for h in range(HH * half, HH * half + HH):
                            row_max(b, k, u, h)
                        split_max(b, k, u, half)
                    for g4 in range(4):
                        normalise(b, k, u, g4)
                    if l:
                        residual_rows(b, k, u)
                    else:
                        residual(b, k, u)
                    second_norm(b, k, u)
                    if l:
                        rms_norm(b, k, u)
                        choose_one(b, k, u)
                    else:
                        choose(b, k, u)
                    place(b, k, u)
                assert ch.n == ch.per, ch.n

        @block.tensor
        def _(pe):
            start(pe, xn_T, qk_proj, v_proj, on_T, y_proj, y_T, h2_T, logits, pos, a_scores, m_T, b_scores, pv, o_T)

            def turn(src, ready, b, free, sig):
                pe.wait_ge(ready.handle, ready.after(b))
                free()
                for t in range(NT):
                    ins = pe.transpose(M0[:, t * P:(t + 1) * P], src[:, t * P:(t + 1) * P], ident[:, :])
                ins.then_inc(sig.handle, 1)

            def flat(x):
                return x[:, :, :].rearrange("p t d -> p (t d)")

            def free(sig, b, n=None):
                return lambda: pe.wait_ge(sig.handle, sig.after(b, n))

            def project_qk(b, k, u):
                pe.wait_ge(h_ready.handle, h_ready.after(b))
                pe.matmul(M0[:, 0:S], wq[:, l, :], hT[u][:, :], start=True, stop=True)
                pe.matmul(M0[:, S:2 * S], wk[:, l, :], hT[u][:, :], start=True, stop=True).then_inc(qk_proj.handle, 1)

            def project_v(b, k, u):
                pe.wait_ge(qk_f32.handle, qk_f32.after(b))
                for t in range(NT):
                    ins = pe.matmul(M0[:, t * P:(t + 1) * P], hT[u][:, t * P:(t + 1) * P], wv[:, l, :],
                                    start=True, stop=True)
                ins.then_inc(v_proj.handle, 1)

            def scores_a(b, k, u, h):
                if h % HH == 0:
                    pe.wait_ge(stack_in[u][h // HH], stack_in.of(k))
                pe.wait_ge(a_max.handle, a_max.after(b, h - 1) if h >= 2 else a_max.after(b - 1, H + h - 1))
                n = MROW if l == 0 else LIN
                for t in range(NT):
                    ins = pe.matmul(A[h % 2][:, t, :], stack[u][0:n, h, 0, t * P:(t + 1) * P],
                                    stack[u][0:n, h, 1, :], start=True, stop=(l == 1))
                    if l == 0:
                        ins = pe.matmul(A[h % 2][:, t, t * P:(t + 1) * P], slope_ident[:, h % HH, :],
                                        dist[:, t, :], start=False, stop=True)
                ins.then_inc(a_scores.handle, 1)

            def turn_max(b, k, u, half, fr):
                pe.wait_ge(m_split.handle, m_split.after(b, half + 1))
                fr()
                for t in range(NT):
                    ins = pe.transpose(M0b[0:2 * HH, t * P:(t + 1) * P],
                                       mneg[:, half, t, :, :].rearrange("p c h -> p (c h)"), ident_b[:, :])
                ins.then_inc(m_T.handle, 1)

            def scores_b(b, k, u, c):
                if c % 4 == 0:
                    pe.wait_ge(m_in[u][c // 4], m_in.of(k))
                pe.wait_ge(b_exp.handle, b_exp.after(b, c - 1) if c >= 2 else b_exp.after(b - 1, HH + c - 1))
                for j in range(2):
                    h = 2 * c + j
                    for t in range(NT):
                        ins = pe.matmul(Bp[c % 2][:, j, t, :], stack[u][0:KROWS, h, 1, t * P:(t + 1) * P],
                                        stack[u][0:KROWS, h, 0, :], start=True, stop=(l == 1))
                        if l == 0:
                            ins = pe.matmul(Bp[c % 2][:, j, t, t * P:(t + 1) * P], slope_ident[:, h % HH, :],
                                            dist[:, 1 - t, :], start=False, stop=True)
                ins.then_inc(b_scores.handle, 1)

            def weigh(b, k, u, g):
                if g == 0:
                    pe.wait_ge(v_ready.handle, v_ready.after(b))
                pe.wait_ge(b_exp.handle, b_exp.after(b, 2 * g + 2))
                pe.wait_ge(o_norm.handle, o_norm.after(b, g) if g else o_norm.after(b - 1))
                for t in range(NT):
                    for j in range(4):
                        ins = pe.matmul(M1[VW * j:VW * j + VW, 0:S], vals[u][:, t, 4 * g + j, :],
                                        probs[(2 * g + j // 2) % 4][:, j % 2, t, :],
                                        start=(t == 0), stop=(t == NT - 1), tile_position=(0, VW * j))
                ins.then_inc(pv.handle, 1)

            def turn_heads(b, k, u, g):
                pe.wait_ge(o_read.handle, o_read.after(b, g + 1))
                for t in range(NT):
                    ins = pe.transpose(M1[:, S + t * P:S + (t + 1) * P], heads[g % 2][:, t * P:(t + 1) * P], ident[:, :])
                ins.then_inc(o_T.handle, 1)

            def project_out(b, k, u):
                pe.wait_ge(onT_read.handle, onT_read.after(b))
                pe.matmul(M0[:, 0:S], wo[:, :], OnT[:, :], start=True, stop=True).then_inc(y_proj.handle, 1)

            def gate(b, k, u):
                pe.wait_ge(h2T_read.handle, h2T_read.after(b))
                for t in range(NT):
                    ins = pe.matmul(M0[:, t * E:(t + 1) * E], h2T[:, t * P:(t + 1) * P], gate_w[:, l, :],
                                    start=True, stop=True)
                ins.then_inc(logits.handle, 1)

            def count(b, k, u):
                pe.wait_ge(sel_ready.handle, sel_ready.after(b))
                pe.wait_ge(logits_read.handle, logits_read.after(b))
                pe.matmul(M0[:, 0:E], before_tri[:, :], sel[:, 0, :], start=True, stop=True)
                pe.matmul(M0[:, E:2 * E], before_tri[:, :], sel[:, 1, :], start=True, stop=False)
                pe.matmul(M0[:, E:2 * E], ones_b[:, :], sel[:, 0, :], start=False, stop=True)
                pe.matmul(M0[:, 2 * E:3 * E], ones_b[:, :], sel[:, 0, :], start=True, stop=False)
                pe.matmul(M0[:, 2 * E:3 * E], ones_b[:, :], sel[:, 1, :], start=False, stop=True)\
                    .then_inc(pos.handle, 1)

            with pe.Fori(0, B // 2) as k:
                for u in range(2):
                    b = k * 2 + u
                    turn(flat(xn[u]), xn_ready, b, free(pos_read, b - 1), xn_T)
                    project_qk(b, k, u)
                    project_v(b, k, u)
                    for half in range(2):
                        for h in range(HH * half, HH * half + HH):
                            scores_a(b, k, u, h)
                        turn_max(b, k, u, half, free(v_ready, b) if half == 0 else free(mT_read, b, 1))
                    for c in range(HH):
                        scores_b(b, k, u, c)
                        if c % 2:
                            weigh(b, k, u, c // 2)
                            turn_heads(b, k, u, c // 2)
                    if l == 0:
                        turn(On[u][:, :, :, :].rearrange("p t h d -> p (t h d)"), o_norm, b, free(mT_read, b), on_T)
                        project_out(b, k, u)
                        turn(yT, y_read, b, free(y_read, b), y_T)
                        turn(flat(h2[u]), h2_ready, b, free(x1_ready, b), h2_T)
                    else:
                        turn(flat(h3[u]), h3_ready, b, free(mT_read, b), h2_T)
                    gate(b, k, u)
                    count(b, k, u)


def experts(nc, l, g):
    (ident, ones_row, zero_rows, region_row, tile_iota, run, run_i, cnt_i, n_tiles, tile_base, corr, reached, tile_tab,
     tile_e, tile_row, yslotf, yslot, chosen, slotf, w1, w2, b1, b2, w1s, xt, xtT, hid, yt, A, Bp, M0, M1, ln_cols,
     gathered, expert_out) = (g[n] for n in (
        "ident ones_row zero_rows region_row tile_iota run run_i cnt_i n_tiles tile_base corr reached tile_tab "
        "tile_e tile_row yslotf yslot chosen slotf w1 w2 b1 b2 w1s xt xtT hid yt A Bp M0 M1 ln_cols "
        "gathered expert_out").split())
    slots, n_choice = SLOTS[l], CHOICES[l]

    def sem(name):
        return nc.alloc_semaphore(f"L{l}_{name}")

    def signals(*names):
        return [Signal(sem(n), 1) for n in names]

    run_ready, table_ready = sem("run_ready"), sem("table_ready")
    zeroed = sem("slack_zeroed")
    xt_in = Transfers([sem(f"xt_in{u}") for u in range(2)], 1)
    yt_out = Transfers([sem(f"yt_out{u}") for u in range(2)], 1)
    xt_T, xtT_ready, w1_staged, first, hidden, second, y_done = signals(
        "xt_T", "xtT_ready", "w1_staged", "first_products", "hidden", "second_products", "y_done")
    dve_order = sem("tiles_dve_order")

    with nc.Block() as block:

        @block.sync
        def _(sp):
            for t in (xt_in, yt_out):
                t.start(sp)
            sp.wait_ge(run_ready, 1)
            for e in range(E):
                r = sp.value_load(run_i[0:1, e:e + 1], min_val=e * REGION, max_val=(e + 1) * REGION - TOK)
                sp.dma_start(gathered[l][bass.ds(r, TOK), :].rearrange("(t p) d -> p t d", p=P), zero_rows[:, :, :])\
                    .then_inc(zeroed, 16)
            sp.wait_ge(table_ready, 1)
            sp.wait_ge(zeroed, 16 * E)
            out_view = expert_out[l].rearrange("(s t p) d -> s p t d", t=NT, p=P)

            def load_tile(s, k, u):
                row = sp.value_load(tile_row[0:1, bass.ds(s, 1)], min_val=0, max_val=E * REGION - TOK)
                sp.wait_ge(xt_T.handle, xt_T.after(s - 2))
                sp.dma_start(xt[u][:, :, :], gathered[l][bass.ds(row, TOK), :].rearrange("(t p) d -> p t d", p=P))\
                    .then_inc(xt_in[u], 16)

            def store_tile(s, k, u):
                sp.wait_ge(y_done.handle, y_done.after(s))
                sp.dma_start(out_view[bass.ds(s, 1)].rearrange("o p t d -> (o p) t d"), yt[u][:, :, :])\
                    .then_inc(yt_out[u], 16)

            with sp.Fori(0, slots // 2) as k:
                for u in range(2):
                    load_tile(k * 2 + u, k, u)
                for u in range(2):
                    store_tile(k * 2 + u, k, u)
            for u in range(2):
                sp.wait_ge(yt_out[u], yt_out.of(slots // 2 - 1))

        @block.vector
        def _(dve):
            ch = Chain(dve, dve_order)
            for s in (xtT_ready, w1_staged, y_done):
                dve.sem_inc(s.handle, 2)
            dve.tensor_copy(run_i[:, :], run[:, :]).then_inc(run_ready, 1)
            ch.link(dve.tensor_tensor(n_tiles[:, :], run[:, :], region_row[:, :], ALU.subtract))
            ch.link(dve.tensor_scalar(n_tiles[:, :], n_tiles[:, :], float(TOK - 1), None, ALU.add))
            ch.link(dve.tensor_copy(cnt_i[:, :], n_tiles[:, :]))
            ch.link(dve.tensor_scalar(cnt_i[:, :], cnt_i[:, :], TOK.bit_length() - 1, None, ALU.logical_shift_right))
            ch.mark(dve.tensor_copy(n_tiles[:, :], cnt_i[:, :]))
            ch.link(dve.memset(tile_base[:, 0:1], 0.0))
            for e in range(E):
                ch.link(dve.tensor_tensor(tile_base[:, e + 1:e + 2], tile_base[:, e:e + 1], n_tiles[:, e:e + 1], ALU.add))
            base = tile_base[:, 0:E].unsqueeze(1).broadcast_to([P, slots, E])
            r = reached[:, 0:slots, :]
            tab = tile_tab[:, :, 0:slots]
            ch.link(dve.tensor_tensor(r, tile_iota[:, 0:slots, :], base, ALU.is_ge))
            ch.link(dve.tensor_reduce(tab[:, 0, :], r, AX.X, ALU.add))
            ch.link(dve.tensor_tensor(r, r, base, ALU.mult))
            ch.link(dve.tensor_reduce(tab[:, 1, :], r, AX.X, ALU.max))
            ch.link(dve.tensor_tensor(tab[:, 1, :], tile_iota[:, 0:slots, 0], tab[:, 1, :], ALU.subtract))
            ch.link(dve.tensor_scalar(tab[:, 0, :], tab[:, 0, :], -1.0, None, ALU.add))
            ch.link(dve.tensor_scalar(tab[:, 1, :], tab[:, 1, :], float(TOK), None, ALU.mult))
            ch.link(dve.scalar_tensor_tensor(out=tab[:, 1, :], in0=tab[:, 0, :], scalar=float(REGION), in1=tab[:, 1, :],
                                             op0=ALU.mult, op1=ALU.add))
            ch.link(dve.tensor_scalar(tab[:, 2, :], tile_iota[:, 0:slots, 0], tile_base[:, E:E + 1], None, ALU.is_lt))
            ch.mark(dve.tensor_tensor(tile_e[:, 0:slots], tab[:, 0, :], tab[:, 2, :], ALU.mult))
            ch.mark(dve.tensor_tensor(tile_row[:, 0:slots], tab[:, 1, :], tab[:, 2, :], ALU.mult))
            ch.link(dve.scalar_tensor_tensor(out=corr[:, :], in0=tile_base[:, 0:E], scalar=float(TOK), in1=region_row[:, :],
                                             op0=ALU.mult, op1=ALU.subtract))
            dve.tensor_copy(n_tiles[:, :], corr[:, :]).then_inc(table_ready, 1)
            for c in range(n_choice):
                v = chosen[:, :, c, :, :]
                for t in range(NT):
                    ch.mark(dve.tensor_tensor(v[:, :, t, :], v[:, :, t, :], corr[:, :].unsqueeze(1).broadcast_to([P, B, E]), ALU.mult))
                ch.settle()
                ch.link(dve.tensor_reduce(yslotf[:, :, c, :], v, AX.X, ALU.add))
                ch.link(dve.tensor_tensor(yslot[:, :, c, :], yslotf[:, :, c, :], slotf[:, :, c, :], ALU.add))

            dve.wait_ge(table_ready, 1)

            def stage_w1(s, k, u):
                e = dve.value_load(tile_e[0:1, bass.ds(s, 1)], min_val=0, max_val=E - 1)
                dve.wait_ge(first.handle, first.after(s - 2))
                dve.tensor_scalar(w1s[u][:, :], w1[:, bass.ds(e, 1), :].rearrange("p o f -> p (o f)"), 1.0, None, ALU.mult)\
                    .then_inc(w1_staged.handle, 1)

            def read_xT(s, k, u):
                dve.wait_ge(xt_T.handle, xt_T.after(s))
                dve.wait_ge(first.handle, first.after(s - 2))
                m = (M0, M1)[u]
                if l:
                    dve.tensor_scalar(xtT[u][:, :], m[:, 0:TOK], ln_cols[:, 2:3], None, ALU.mult).then_inc(xtT_ready.handle, 1)
                else:
                    dve.tensor_copy(xtT[u][:, :], m[:, 0:TOK]).then_inc(xtT_ready.handle, 1)

            def read_y(s, k, u):
                dve.wait_ge(second.handle, second.after(s))
                dve.wait_ge(yt_out[u], yt_out.of(k - 1))
                dve.tensor_copy(yt[u][:, :, :], A[u][:, :, 0:D]).then_inc(y_done.handle, 1)

            with dve.Fori(0, slots // 2) as k:
                for u in range(2):
                    stage_w1(k * 2 + u, k, u)
                    read_xT(k * 2 + u, k, u)
                for u in range(2):
                    read_y(k * 2 + u, k, u)

        @block.scalar
        def _(act):
            act.sem_inc(hidden.handle, 2)
            act.preload_act_table(ACT.Silu if l else ACT.Relu)
            act.wait_ge(table_ready, 1)

            def activate(s, k, u):
                act.wait_ge(first.handle, first.after(s))
                act.wait_ge(second.handle, second.after(s - 2))
                src = Bp[u][:, :, :, :].rearrange("p j t s -> p (j t) s")
                if l == 0:
                    act.activation(hid[u][:, :, :], src, ACT.Relu).then_inc(hidden.handle, 1)
                else:
                    e = act.value_load(tile_e[0:1, bass.ds(s, 1)], min_val=0, max_val=E - 1)
                    for f in range(FC):
                        ins = act.activation(hid[u][:, f, :], src[:, f, :], ACT.Silu,
                                             bias=b1[:, bass.ds(e, 1), f:f + 1].rearrange("p o f -> p (o f)"))
                    ins.then_inc(hidden.handle, 1)

            with act.Fori(0, slots // 2) as k:
                for u in range(2):
                    activate(k * 2 + u, k, u)

        @block.tensor
        def _(pe):
            for s in (xt_T, first, second):
                pe.sem_inc(s.handle, 2)
            pe.wait_ge(table_ready, 1)

            def turn_x(s, k, u):
                pe.wait_ge(xt_in[u], xt_in.of(k))
                pe.wait_ge(xtT_ready.handle, xtT_ready.after(s - 2))
                for t in range(NT):
                    ins = pe.transpose((M0, M1)[u][:, t * P:(t + 1) * P], xt[u][:, t, :], ident[:, :])
                ins.then_inc(xt_T.handle, 1)

            def to_hidden(s, k, u):
                pe.wait_ge(w1_staged.handle, w1_staged.after(s))
                pe.wait_ge(xtT_ready.handle, xtT_ready.after(s))
                pe.wait_ge(hidden.handle, hidden.after(s - 2))
                dst = Bp[u][:, :, :, :].rearrange("p j t s -> p (j t) s")
                for f in range(FC):
                    ins = pe.matmul(dst[:, f, :], w1s[u][:, f * P:(f + 1) * P], xtT[u][:, :], start=True, stop=True)
                ins.then_inc(first.handle, 1)

            def from_hidden(s, k, u):
                e = pe.value_load(tile_e[0:1, bass.ds(s, 1)], min_val=0, max_val=E - 1)
                pe.wait_ge(hidden.handle, hidden.after(s))
                pe.wait_ge(y_done.handle, y_done.after(s - 2))
                for t in range(NT):
                    for f in range(FC):
                        ins = pe.matmul(A[u][:, t, 0:D], hid[u][:, f, t * P:(t + 1) * P],
                                        w2[:, bass.ds(e, 1), f, :].rearrange("p o d -> p (o d)"),
                                        start=(f == 0), stop=(l == 0 and f == FC - 1))
                    if l:
                        ins = pe.matmul(A[u][:, t, 0:D], ones_row[:, :], b2[:, bass.ds(e, 1), :].rearrange("p o d -> p (o d)"),
                                        start=False, stop=True)
                ins.then_inc(second.handle, 1)

            with pe.Fori(0, slots // 2) as k:
                for u in range(2):
                    turn_x(k * 2 + u, k, u)
                for u in range(2):
                    to_hidden(k * 2 + u, k, u)
                for u in range(2):
                    from_hidden(k * 2 + u, k, u)


def combine(nc, g):
    X, Y, X1, yslot, wtok, gb_row, gslot, expert_out, mod_rows, x_view, out = (g[n] for n in
        "X Y X1 yslot wtok gb_row gslot expert_out mod_rows x_view out".split())

    def sem(name):
        return nc.alloc_semaphore(f"out_{name}")

    x_in, y_in, stored = (Transfers([sem(f"{n}{u}") for u in range(2)], dmas)
                          for n, dmas in (("x_in", 2), ("y_in", NT), ("stored", 1)))
    y_in.begun = 0
    gslot_ready, summed = Signal(sem("gslot_ready"), 1), Signal(sem("summed"), 1)
    dve_order, pool_order = sem("dve_order"), sem("pool_order")

    with nc.Block() as block:

        @block.sync
        def _(sp):
            for t in (x_in, stored):
                t.start(sp)

            def load(b, k, u):
                sp.wait_ge(summed.handle, summed.after(b - 2))
                sp.dma_start(X[u][:, :, :], x_view[3][bass.ds(b, 1)].rearrange("o p t d -> (o p) t d")).then_inc(x_in[u], 16)
                sp.dma_start(gb_row[u][:, :, :], mod_rows[1][bass.ds(b, 1), GB * D:(GB + 1) * D]
                             .rearrange("o (j d) -> o j d", j=1).broadcast_to([P, 1, D])).then_inc(x_in[u], 16)

            def store(b, k, u):
                sp.wait_ge(summed.handle, summed.after(b))
                sp.dma_start(out[bass.ds(b, 1)].rearrange("o (t p) d -> p (o t) d", p=P), X1[u][:, :, :]).then_inc(stored[u], 16)

            with sp.Fori(0, B // 2) as k:
                for u in range(2):
                    load(k * 2 + u, k, u)
                for u in range(2):
                    store(k * 2 + u, k, u)
            for u in range(2):
                sp.wait_ge(stored[u], stored.of(B // 2 - 1))

        @block.gpsimd
        def _(pool):
            ch = Chain(pool, pool_order)
            with pool.Fori(0, B // 2) as k:
                for u in range(2):
                    b = k * 2 + u
                    pool.wait_ge(gslot_ready.handle, gslot_ready.after(b))
                    pool.wait_ge(summed.handle, summed.after(b - 2))
                    ch.apart()
                    for t in range(NT):
                        pool.indirect_dma_start(Y[u][:, 0, t, :], None, expert_out[1],
                                                bass.IndirectOffsetOnAxis(ap=gslot[u][:, 0, t:t + 1], axis=0))\
                            .then_inc(y_in[u], 16)

        @block.vector
        def _(dve):
            ch = Chain(dve, dve_order)
            for s in (gslot_ready, summed):
                dve.sem_inc(s.handle, 2)
            ch.before()
            with dve.Fori(0, B // 2) as k:
                ch.loop(k, 2 * 3)
                for u in range(2):
                    b = k * 2 + u
                    dve.tensor_scalar(gslot[u][:, 0, :], yslot[:, bass.ds(b, 1), 0, :].rearrange("p o t -> p (o t)"), 1.0, None, ALU.mult)\
                        .then_inc(gslot_ready.handle, 1)
                for u in range(2):
                    b = k * 2 + u
                    dve.wait_ge(y_in[u], y_in.of(k))
                    dve.wait_ge(x_in[u], x_in.of(k))
                    dve.wait_ge(stored[u], stored.of(k - 1))
                    for t in range(NT):
                        ch.mark(dve.tensor_scalar(Y[u][:, 1, t, :], Y[u][:, 0, t, :],
                                                  wtok[:, bass.ds(b, 1), 0, t:t + 1].rearrange("p o t -> p (o t)"), None, ALU.mult))
                    ch.settle()
                    ch.link(dve.tensor_tensor(Y[u][:, 0, :, :], Y[u][:, 1, :, :],
                                              gb_row[u][:, :, :].broadcast_to([P, NT, D]), ALU.mult))
                    dve.tensor_tensor(X1[u][:, :, :], X[u][:, :, :], Y[u][:, 0, :, :], ALU.add).then_inc(summed.handle, 1)
                assert ch.n == ch.per


def inputs_of(x):
    import numpy as np

    def bits(x):
        return (np.ascontiguousarray(x, np.float32).view(np.uint32) >> 16).astype(np.uint16)

    n = {k: np.asarray(v) for k, v in x.items()}
    r, c = np.arange(P)[:, None], np.arange(P)[None, :]
    half, d, h8 = np.meshgrid(np.arange(2), np.arange(HD), np.arange(HH), indexing="ij")
    stacked = (16 * h8 + 8 * half + d).reshape(-1)
    half, h8, d = np.meshgrid(np.arange(2), np.arange(HH), np.arange(HD), indexing="ij")
    by_head = (16 * h8 + 8 * half + d).reshape(-1)
    wqkv, bqkv = n["L0_attn_W_qkv"], n["L0_attn_b_qkv"]
    slope = 2.0 ** -np.arange(HH)
    pos = np.arange(S)
    rows = np.zeros((4, H, 2, S))
    sign = np.where(pos < P, 1.0, -1.0)
    rows[0, :, 0] = np.tile(slope, 2)[:, None] * (sign * pos)[None]
    rows[1, :, 0] = -np.tile(slope, 2)[:, None] * sign[None]
    rows[0, :, 1] = 1.0
    rows[1, :, 1] = pos
    rows[2:, :, 1] = 1.0
    rows1 = rows.copy()
    rows1[:2, :, 0] = 0.0
    f = np.float32
    slots = SLOTS[0]
    return {
        "x": n["L0_attn_x"],
        "ident": np.eye(P, dtype=f), "ident_b": bits(np.eye(P)),
        "slope_ident": bits(np.eye(P)[:, None, :] * slope[None, :, None]),
        "dist": bits(np.stack([-2.0 * np.maximum(r - c, 0), -2.0 * np.maximum(c - r, 0)], 1)),
        "before_tri": bits(r < c), "ones_b": bits(np.ones((P, P))),
        "rev_iota": np.broadcast_to(E - np.arange(E, dtype=f), (P, 2, E)).copy(),
        "region_row": np.broadcast_to(np.arange(E, dtype=f) * REGION, (P, E)).copy(),
        "tile_iota": np.broadcast_to(np.arange(slots, dtype=f)[None, :, None], (P, slots, E)).copy(),
        "stack_rows0": bits(rows), "stack_rows1": bits(rows1),
        "wq": np.stack([wqkv[0:D].T[:, stacked], n["L1_attn_wq"][:, stacked]], 1),
        "wk": np.stack([wqkv[D:2 * D].T[:, stacked], n["L1_attn_wk"][:, stacked]], 1),
        "wv": np.stack([wqkv[2 * D:].T[:, by_head], n["L1_attn_wv"][:, by_head]], 1),
        "wo": n["L0_attn_W_out"].T[by_head],
        "qk_bias": np.stack([bqkv[0:D][stacked], bqkv[D:2 * D][stacked]], 1),
        "q_scale": np.stack([np.where(np.arange(D) < 64, HD ** -0.5, (2.0 / HD) ** 0.5), np.full(D, D ** -0.5)], 1).astype(f),
        "vo_bias": np.stack([bqkv[2 * D:][by_head], n["L0_attn_b_out"]], 1),
        "ln_cols": np.stack([n["L1_attn_ln_scale"], n["L1_attn_ln_bias"], n["L1_ffn_rms_w"]], 1),
        "ln_rows": np.stack([n["L1_attn_ln_scale"], n["L1_attn_ln_bias"]])[None],
        "gate_w": np.stack([n["L0_ffn_Wr"], n["L1_ffn_gate_w"].T], 1),
        "cT": np.stack([n["L0_c"].T, n["L1_c"].T], 1),
        "wmod0": n["L0_wmod"], "wmod1": n["L1_wmod"],
        "w1_0": n["L0_ffn_W1"].transpose(1, 0, 2), "w1_1": n["L1_ffn_W1"].transpose(1, 0, 2),
        "w2_0": n["L0_ffn_W2"].reshape(E, FC, P, D).transpose(2, 0, 1, 3),
        "w2_1": n["L1_ffn_W2"].reshape(E, FC, P, D).transpose(2, 0, 1, 3),
        "b1": n["L1_ffn_b1"].reshape(E, FC, P).transpose(2, 0, 1),
        "b2": n["L1_ffn_b2"][None],
    }


def kernel(**inputs):
    import numpy as np
    import concourse.bacc as bacc
    from concourse.bass_utils import run_bass_kernel_spmd as launch

    nc = bacc.Bacc("TRN2", target_bir_lowering=False, num_devices=1)
    arrays = {f"in_{k}": np.ascontiguousarray(v) for k, v in inputs_of(inputs).items()}
    aps = {k[3:]: nc.dram_tensor(k, v.shape, mybir.dt.from_np(v.dtype), kind="ExternalInput").ap()
           for k, v in arrays.items()}
    out = nc.dram_tensor("out_0", (B, S, D), F32, kind="ExternalOutput").ap()
    build(nc, aps, out)
    return launch(nc, [arrays], core_ids=[0]).results[0]["out_0"]
```

```python
from contextlib import ExitStack

import concourse.bass as bass
from concourse import mybir

F32 = mybir.dt.float32
BF16 = mybir.dt.bfloat16
I32 = mybir.dt.int32
ACT = mybir.ActivationFunctionType
ALU = mybir.AluOpType
AX = mybir.AxisListType

P = 128
B, S, D = 32, 256, 128
NT = S // P
H, HD = 16, 8
HH = H // 2
E, F = 8, 512
FC = F // P
VW = 32
TOK = 256
REGION = B * S + TOK
SLOTS = {0: (2 * B * S + E * (TOK - 1)) // TOK, 1: (B * S + E * (TOK - 1)) // TOK}
SLOTS = {l: n + n % 2 for l, n in SLOTS.items()}
CHOICES = {0: 2, 1: 1}
PRODUCTS = [(0, 0), (0, 1), (0, 2), (1, 0), (1, 1), (2, 0)]
LIN = HD * len(PRODUCTS)
MROW = LIN + 2
KROWS = MROW + 2
SA, CA, GA, SB, CB, GB = range(6)
BIG = 3.0e38
LG, PS = S + P, S + P + NT * E
EPS = {0: 1e-5, 1: 1e-5}
EPS_IN = 1e-6
EXP_SCALE = {0: (1.0, 2.0 ** -0.5), 1: (1.0, 1.0)}


class Signal:

    def __init__(self, handle, per):
        self.handle, self.per = handle, per

    def after(self, b, n=None):
        return 2 * self.per + b * self.per + (self.per if n is None else n)


class Transfers:

    def __init__(self, handles, dmas, begun=1):
        self.handles, self.step, self.begun = handles, 16 * dmas, begun

    def __getitem__(self, u):
        return self.handles[u]

    def start(self, eng):
        for h in self.handles:
            for x in h if isinstance(h, list) else [h]:
                eng.sem_inc(x, self.step * self.begun)

    def of(self, k):
        return self.step * (k + 1 + self.begun)


class Chain:

    def __init__(self, eng, handle):
        self.eng, self.handle, self.base, self.n = eng, handle, 0, 0

    def link(self, ins):
        self.mark(ins)
        self.settle()

    def mark(self, ins):
        ins.then_inc(self.handle, 1)
        self.n += 1

    def settle(self):
        self.eng.wait_ge(self.handle, self.base + self.n)

    def settle_apart(self):
        self.settle()
        self.apart()

    def apart(self):
        self.eng.sem_inc(self.handle, 1)
        self.n += 1

    def loop(self, i, per):
        self.base, self.n, self.entry, self.per = self.n_before + i * per, 0, self.n_before, per

    def before(self):
        self.n_before = self.base + self.n

    def done(self, times):
        assert self.n == self.per, (self.n, self.per)
        self.base, self.n = self.entry + times * self.per, 0


def build(nc, a, out):
    with ExitStack() as ctx:
        def sb(name, shape, dt=F32):
            return ctx.enter_context(nc.sbuf_tensor(name, shape, dt))

        def sem(name):
            return ctx.enter_context(nc.semaphore(name))

        def dram(name, shape, dt=F32):
            return nc.dram_tensor(name, shape, dt, kind="Internal").ap()

        mod_rows = [dram(f"mod_rows{l}", (B, 6 * D)) for l in range(2)]
        x_mid = [dram(f"x_mid{n}", (B * S, D)) for n in range(3)]
        gathered = [dram(f"gathered{l}", (E * REGION, D)) for l in range(2)]
        expert_out = [dram(f"expert_out{l}", (SLOTS[l] * TOK, D)) for l in range(2)]

        ident = sb("ident", [P, P])
        ident_b = sb("ident_b", [P, P], BF16)
        slope_ident = sb("slope_ident", [P, HH, P], BF16)
        dist = sb("dist", [P, 2, P], BF16)
        before_tri = sb("before_tri", [P, P], BF16)
        ones_b = sb("ones_b", [P, P], BF16)
        ones_row = sb("ones_row", [1, P])
        ones_col = sb("ones_col", [P, 1, 1])
        rev_iota = sb("rev_iota", [P, 2, E])
        region_row = sb("region_row", [P, E])
        tile_iota = sb("tile_iota", [P, SLOTS[0], E])
        zero_rows = sb("zero_rows", [P, TOK // P, D])
        wq, wk, wv = (sb(n, [P, 2, P]) for n in ("wq", "wk", "wv"))
        wo = sb("wo", [P, P])
        qk_bias = sb("qk_bias", [P, 2])
        q_scale = sb("q_scale", [P, 2])
        qs_bias = sb("qs_bias", [P, 1])
        vo_bias = sb("vo_bias", [P, 2])
        out_bias = sb("out_bias", [P, 1])
        ln_cols = sb("ln_cols", [P, 3])
        gate_w = sb("gate_w", [P, 2, E])
        cT = sb("cT", [P, 2, B])
        silu = sb("silu", [P, 2, B])
        wmod = sb("wmod", [P, 2, 6 * D])
        modT = [sb(f"modT{l}", [P, 6, B]) for l in range(2)]
        gob = sb("gob", [P, B])
        mod_sb = sb("mod_sb", [B, 6 * D])
        w1 = sb("w1", [P, E, F])
        w2 = sb("w2", [P, E, FC, D])
        b1 = sb("b1", [P, E, FC])
        b2 = sb("b2", [1, E, D])

        X = [sb(f"X{u}", [P, NT, D]) for u in range(2)]
        XR = [sb(f"XR{u}", [P, NT, D]) for u in range(2)]
        X1 = [sb(f"X1{u}", [P, NT, D]) for u in range(2)]
        st = sb("st", [P, NT, 6])
        mv = [sb(f"mv{u}", [P, NT, 2]) for u in range(2)]
        rs = [sb(f"rs{u}", [P, NT]) for u in range(2)]
        xn = [sb(f"xn{u}", [P, NT, D]) for u in range(2)]
        hT = [sb(f"hT{u}", [P, S]) for u in range(2)]
        qk = sb("qk", [P, 2, S])
        rem = sb("rem", [P, 2, S])
        parts = [sb(f"parts{u}", [P, 2, 3, S], BF16) for u in range(2)]
        stack = [sb(f"stack{u}", [KROWS, H, 2, S], BF16) for u in range(2)]
        vals = [sb(f"vals{u}", [P, NT, H, VW]) for u in range(2)]
        mx = [sb(f"mx{u}", [P, H, NT]) for u in range(2)]
        mneg = sb("mneg", [P, 2, NT, 2, HH], BF16)
        mrow = [sb(f"mrow{u}", [2 * HH, S], BF16) for u in range(2)]
        probs = [sb(f"probs{n}", [P, 2, NT, S]) for n in range(4)]
        heads = [sb(f"heads{n}", [P, S]) for n in range(2)]
        rsum = sb("rsum", [P, NT, 4])
        On = [sb(f"On{u}", [P, NT, H, HD]) for u in range(2)]
        OnT = sb("OnT", [P, S])
        yT = sb("yT", [P, S])
        st2 = sb("st2", [P, NT, 6])
        mv2 = sb("mv2", [P, NT, 2])
        rs2 = sb("rs2", [P, NT])
        xn2 = sb("xn2", [P, NT, D])
        front_rows = [sb(f"front_rows{u}", [P, 3, D]) for u in range(2)]
        back_rows = [sb(f"back_rows{u}", [P, 3, D]) for u in range(2)]
        xh = [sb(f"xh{u}", [P, NT, D]) for u in range(2)]
        gb_row = [sb(f"gb_row{u}", [P, 1, D]) for u in range(2)]
        lnrow = sb("lnrow", [P, 2, D])
        h2 = [sb(f"h2{u}", [P, NT, D]) for u in range(2)]
        h3 = [sb(f"h3{u}", [P, NT, D]) for u in range(2)]
        h2T = sb("h2T", [P, S])
        newt = sb("newt", [P, 4, NT])
        lg = sb("lg", [P, NT, E])
        rt = sb("rt", [P, 8, NT, E])
        r1 = sb("r1", [P, 16, NT])
        sel = sb("sel", [P, NT, E], BF16)
        chosen = sb("chosen", [P, B, 2, NT, E])
        slotf = sb("slotf", [P, B, 2, NT])
        slot_in = [sb(f"slot_in{u}", [P, 2, NT], I32) for u in range(2)]
        wtok = sb("wtok", [P, B, 2, NT])
        run = sb("run", [P, E])
        run_i = sb("run_i", [P, E], I32)
        cnt_i = sb("cnt_i", [P, E], I32)
        n_tiles = sb("n_tiles", [P, E])
        tile_base = sb("tile_base", [P, E + 1])
        corr = sb("corr", [P, E])
        reached = sb("reached", [P, SLOTS[0], E])
        tile_tab = sb("tile_tab", [P, 4, SLOTS[0]])
        tile_e = sb("tile_e", [P, SLOTS[0]], I32)
        tile_row = sb("tile_row", [P, SLOTS[0]], I32)
        yslotf = sb("yslotf", [P, B, 2, NT])
        yslot = sb("yslot", [P, B, 2, NT], I32)
        w1s = [sb(f"w1s{u}", [P, F]) for u in range(2)]
        xt = [sb(f"xt{u}", [P, NT, D]) for u in range(2)]
        xtT = [sb(f"xtT{u}", [P, TOK]) for u in range(2)]
        hid = [sb(f"hid{u}", [P, FC, TOK]) for u in range(2)]
        yt = [sb(f"yt{u}", [P, NT, D]) for u in range(2)]
        gslot = [sb(f"gslot{u}", [P, 2, NT], I32) for u in range(2)]
        Y = [sb(f"Y{u}", [P, 2, NT, D]) for u in range(2)]

        A = [ctx.enter_context(nc.psum_tensor(f"A{n}", [P, NT, S], F32)) for n in range(2)]
        Bp = [ctx.enter_context(nc.psum_tensor(f"B{n}", [P, 2, NT, S], F32)) for n in range(2)]
        M0 = ctx.enter_context(nc.psum_tensor("M0", [P, 512], F32))
        M1 = ctx.enter_context(nc.psum_tensor("M1", [P, 512], F32))
        M0b = M0[:, :].bitcast(BF16)

        x_view = [a["x"].rearrange("b (t p) d -> b p t d", p=P)] + [
            m.rearrange("(b t p) d -> b p t d", t=NT, p=P) for m in x_mid]

        loads = [
            (ident[:, :], a["ident"]), (ident_b[:, :], a["ident_b"].bitcast(BF16)), (slope_ident[:, :, :], a["slope_ident"].bitcast(BF16)),
            (dist[:, :, :], a["dist"].bitcast(BF16)), (before_tri[:, :], a["before_tri"].bitcast(BF16)), (ones_b[:, :], a["ones_b"].bitcast(BF16)),
            (rev_iota[:, :, :], a["rev_iota"]), (region_row[:, :], a["region_row"]),
            (tile_iota[:, :, :], a["tile_iota"]),
            (wq[:, :, :], a["wq"]), (wk[:, :, :], a["wk"]), (wv[:, :, :], a["wv"]), (wo[:, :], a["wo"]),
            (qk_bias[:, :], a["qk_bias"]), (q_scale[:, :], a["q_scale"]), (vo_bias[:, :], a["vo_bias"]),
            (ln_cols[:, :], a["ln_cols"]), (lnrow[:, :, :], a["ln_rows"].broadcast_to([P, 2, D])), (gate_w[:, :, :], a["gate_w"]), (cT[:, :, :], a["cT"]),
            (wmod[:, 0, :], a["wmod0"]), (wmod[:, 1, :], a["wmod1"]),
        ] + [(stack[u][LIN:KROWS, :, :, :], a["stack_rows0"].bitcast(BF16)) for u in range(2)]
        loaded, ready, modp, moded, mod_out = (sem(n) for n in
            ("setup_loaded", "setup_ready", "setup_products", "setup_modulation", "mod_rows_written"))
        set_act, set_dve = sem("setup_act_order"), sem("setup_dve_order")

        with nc.Block() as block:
            @block.sync
            def _(sp):
                for dst, src in loads:
                    sp.dma_start(dst, src).then_inc(loaded, 16)
                for l in range(2):
                    sp.wait_ge(moded, 8 * (l + 1))
                    sp.dma_start(mod_rows[l], mod_sb[:, :]).then_inc(mod_out, 16)
                    sp.wait_ge(mod_out, 16 * (l + 1))

            @block.scalar
            def _(act):
                act.wait_ge(loaded, 16 * len(loads))
                act.activation(silu[:, :, :], cT[:, :, :], ACT.Exp, scale=-1.0).then_inc(set_act, 1)

            @block.tensor
            def _(pe):
                pe.wait_ge(ready, 1)
                for l in range(2):
                    if l:
                        pe.wait_ge(moded, 8)
                    for j in range(6):
                        pe.matmul(M0[:, j * B:(j + 1) * B], wmod[:, l, j * D:(j + 1) * D], silu[:, l, :],
                                  start=True, stop=True)
                    pe.matmul(A[0][0:B, :, :].rearrange("p t s -> p (t s)"), silu[:, l, :], wmod[:, l, 0:512],
                              start=True, stop=True)
                    pe.matmul(A[1][0:B, 0, :], silu[:, l, :], wmod[:, l, 512:768], start=True, stop=True)\
                        .then_inc(modp, 1)
                pe.matmul(M1[:, 0:1], wo[:, :], vo_bias[:, 0:1], start=True, stop=True).then_inc(modp, 1)

            @block.vector
            def _(dve):
                ch = Chain(dve, set_dve)
                for u in range(2):
                    dve.memset(vals[u][:, :, :, :], 0.0).then_inc(set_dve, 1)
                dve.wait_ge(set_dve, 2)
                ch.n = 2
                for u in range(2):
                    ch.mark(dve.memset(vals[u][:, :, :, HD:HD + 1], 1.0))
                ch.mark(dve.memset(ones_row[:, :], 1.0))
                ch.mark(dve.memset(ones_col[:, :, :], 1.0))
                ch.mark(dve.memset(zero_rows[:, :, :], 0.0))
                dve.wait_ge(loaded, 16 * len(loads))
                ch.mark(dve.tensor_copy(run[:, :], region_row[:, :]))
                ch.mark(dve.tensor_tensor(qs_bias[:, :], qk_bias[:, 0:1], q_scale[:, 0:1], ALU.mult))
                dve.wait_ge(set_act, 1)
                ch.link(dve.tensor_scalar(silu[:, :, :], silu[:, :, :], 1.0, None, ALU.add))
                ch.link(dve.reciprocal(silu[:, :, :], silu[:, :, :]))
                dve.tensor_tensor(silu[:, :, :], silu[:, :, :], cT[:, :, :], ALU.mult).then_inc(ready, 1)
                for l in range(2):
                    dve.wait_ge(modp, l + 1)
                    if l:
                        dve.wait_ge(mod_out, 16)
                    m = modT[l]
                    am = A[0][0:B, :, :].rearrange("p t s -> p (t s)")
                    ch.mark(dve.tensor_copy(m[:, :, :].rearrange("p j b -> p (j b)"), M0[:, 0:6 * B]))
                    ch.mark(dve.tensor_copy(mod_sb[:, 0:512], am))
                    ch.link(dve.tensor_copy(mod_sb[:, 512:768], A[1][0:B, 0, :]))
                    n = 0
                    for j in (CA, CB):
                        dve.tensor_scalar(m[:, j, :], m[:, j, :], 1.0, None, ALU.add).then_inc(moded, 1)
                        dve.tensor_scalar(mod_sb[:, j * D:(j + 1) * D], mod_sb[:, j * D:(j + 1) * D], 1.0, None,
                                          ALU.add).then_inc(moded, 1)
                    for j in (GA, GB):
                        for g, t in ((m[:, j, :], qk[:, 0, 0:B]), (mod_sb[:, j * D:(j + 1) * D], qk[0:B, 1, 0:D])):
                            ch.link(dve.tensor_scalar(t, g, 0.0, 2.0, ALU.is_ge, ALU.mult))
                            ch.link(dve.tensor_scalar(t, t, -1.0, None, ALU.add))
                            ch.link(dve.scalar_tensor_tensor(out=g, in0=g, scalar=-1.0, in1=g, op0=ALU.mult, op1=ALU.max))
                            dve.scalar_tensor_tensor(out=g, in0=g, scalar=0.25, in1=t, op0=ALU.max, op1=ALU.mult)\
                                .then_inc(moded, 1)
                dve.wait_ge(modp, 3)
                ch.link(dve.tensor_tensor(out_bias[:, :], M1[:, 0:1], vo_bias[:, 1:2], ALU.add))
                dve.wait_ge(moded, 16)
                ch.link(dve.tensor_scalar(gob[:, :], modT[0][:, GA, :], out_bias[:, 0:1], None, ALU.mult))

        for layer in range(2):
            with nc.cleanup_on_exit():
                attention(nc, layer, locals())
            with nc.cleanup_on_exit():
                experts(nc, layer, locals())
        with nc.cleanup_on_exit():
            combine(nc, locals())


DEPTH = 3


def run_ticks(eng, tick, ch=None, per=0):
    def peeled(i):
        return lambda off: (i + off, (i + off) // 2, (i + off) % 2) if 0 <= i + off < B else None

    for i in range(-DEPTH, DEPTH):
        tick(peeled(i))
    pairs = (B - 2 * DEPTH) // 2
    if ch:
        ch.before()
    with eng.Fori(0, pairs) as k:
        if ch:
            ch.loop(k, 2 * per)
        for i in (DEPTH, DEPTH + 1):
            tick(lambda off: (k * 2 + (i + off), k + (i + off) // 2, (i + off) % 2))
        if ch:
            assert ch.n == 2 * per, ch.n
    if ch:
        ch.done(pairs)
    for i in range(DEPTH + 2 * pairs, B + DEPTH):
        tick(peeled(i))


def attention(nc, l, g):
    (X, XR, X1, st, mv, rs, xn, hT, qk, rem, parts, stack, vals, mx, mneg, mrow, probs, heads, rsum, On, OnT, yT,
     st2, mv2, rs2, xn2, front_rows, back_rows, xh, qs_bias, h2, h3, h2T, newt, lg, rt, r1, sel, chosen, slotf, slot_in, wtok, run) = (g[n] for n in (
        "X XR X1 st mv rs xn hT qk rem parts stack vals mx mneg mrow probs heads rsum On OnT yT "
        "st2 mv2 rs2 xn2 front_rows back_rows xh qs_bias h2 h3 h2T newt lg rt r1 sel chosen slotf slot_in wtok run").split())
    A, Bp, M0, M1, M0b, ident, ident_b, slope_ident, dist = (g[n] for n in
        "A Bp M0 M1 M0b ident ident_b slope_ident dist".split())
    wq, wk, wv, wo, qk_bias, q_scale, modT, gob, gate_w, ln_cols = (g[n] for n in
        "wq wk wv wo qk_bias q_scale modT gob gate_w ln_cols".split())
    before_tri, ones_b, rev_iota, mod_rows, gathered, x_view, region_row = (g[n] for n in
        "before_tri ones_b rev_iota mod_rows gathered x_view region_row".split())
    gb_row, ones_col, lnrow, gslot, Y, yslot, expert_out, XR, a, w1, w2, b1, b2 = (g[n] for n in
        "gb_row ones_col lnrow gslot Y yslot expert_out XR a w1 w2 b1 b2".split())
    n_choice = CHOICES[l]
    mod = modT[l]

    def sem(name):
        return nc.alloc_semaphore(f"L{l}_{name}")

    def signal(name, per):
        return Signal(sem(name), per)

    def signals(*names, per=1):
        return [signal(n, per) for n in names]

    weights_in, lin_in = sem("weights_in"), sem("lin_in")

    def transfers(name, dmas, begun=1):
        return Transfers([sem(f"{name}{u}") for u in range(2)], dmas, begun)

    x_in = transfers("x_in", 1)
    front_in = transfers("front_in", 2)
    back_in = transfers("back_in", 2)
    base_out = transfers("base_out", 1)
    stack_in = Transfers([[sem(f"stack_in{u}{h}") for h in range(2)] for u in range(2)], len(PRODUCTS))
    m_in = Transfers([[sem(f"m_in{u}{h}") for h in range(2)] for u in range(2)], 1)
    x1_out = transfers("x1_out", 1)
    scat_out = transfers("rows_out", NT * n_choice, 0)
    if l == 1:
        y_in = transfers("y_in", 2 * NT, 0)

    stats, xn_ready, qk_f32, x1_ready, stats2, xn2_ready, logits_read, slots_ready, pos_read = signals(
        "stats", "xn_ready", "qk_f32", "x1_ready", "stats2", "xn2_ready", "logits_read", "slots_ready", "pos_read")
    sel_ready, w_den = signals("sel_ready", "w_den")
    a_max, o_norm, m_split = signal("a_max", H), signal("o_norm", 4), signal("m_split", 2)
    rsqrt, h_ready, v_ready, onT_read, y_read, rsqrt2, h2T_read, w_exp = signals(
        "rsqrt", "h_ready", "v_ready", "onT_read", "y_read", "rsqrt2", "h2T_read", "w_exp")
    mT_read, b_exp, o_read = signal("mT_read", 2), signal("b_exp", HH), signal("o_read", 4)
    xn_T, qk_proj, v_proj, on_T, y_proj, y_T, h2_T, logits, pos = signals(
        "xn_T", "qk_proj", "v_proj", "on_T", "y_proj", "y_T", "h2_T", "logits", "pos")
    a_scores, m_T, b_scores, pv, o_T = (signal("a_scores", H), signal("m_T", 2), signal("b_scores", HH),
                                        signal("pv", 4), signal("o_T", 4))
    split, h2_ready, scattered = signals("split", "h2_ready", "scattered")
    if l == 1:
        h3_ready = signal("h3_ready", 1)
        gslot_ready, x2_ready, h_rows, base_ready, h_stats, h_rsqrt, rms_stats, rms_rsqrt = signals(
            "gslot_ready", "x2_ready", "h_rows", "base_ready", "h_stats", "h_rsqrt", "rms_stats", "rms_rsqrt")
    dve_order, act_order, pool_order = sem("dve_order"), sem("act_order"), sem("pool_order")

    def start(eng, *sigs):
        for s in sigs:
            eng.sem_inc(s.handle, 2 * s.per)

    with nc.Block() as block:

        @block.sync
        def _(sp):
            def rows_of(view, b):
                return view[bass.ds(b, 1)].rearrange("o p t d -> (o p) t d")

            def mod_of(layer, b, first, n):
                return mod_rows[layer][bass.ds(b, 1), first * D:(first + n) * D]\
                    .rearrange("o (j d) -> o j d", j=n).broadcast_to([P, n, D])

            def load_front(b, k, u):
                if l == 0:
                    sp.wait_ge(xn_ready.handle, xn_ready.after(b - 2))
                    sp.dma_start(X[u][:, :, :], rows_of(x_view[0], b)).then_inc(x_in[u], 16)
                else:
                    sp.wait_ge(base_ready.handle, base_ready.after(b - 2))
                    sp.dma_start(X[u][:, :, :], rows_of(x_view[1], b)).then_inc(x_in[u], 16)
                    sp.dma_start(front_rows[u][:, :, :], mod_of(1, b, SA, 3)).then_inc(front_in[u], 16)
                    sp.dma_start(gb_row[u][:, :, :], mod_of(0, b, GB, 1)).then_inc(front_in[u], 16)

            def load_back(b, k, u):
                sp.wait_ge(h2_ready.handle, h2_ready.after(b - 2))
                if l == 1:
                    sp.wait_ge(base_out[u], base_out.of(k))
                sp.dma_start(XR[u][:, :, :], rows_of(x_view[2 * l], b)).then_inc(back_in[u], 16)
                sp.dma_start(back_rows[u][:, :, :], mod_of(l, b, GA, 3)).then_inc(back_in[u], 16)

            def store_base(b, k, u):
                sp.wait_ge(base_ready.handle, base_ready.after(b))
                sp.dma_start(rows_of(x_view[2], b), xh[u][:, :, :]).then_inc(base_out[u], 16)

            def stack_up(b, k, u, half):
                if half == 0:
                    sp.wait_ge(split.handle, split.after(b))
                sp.wait_ge(b_scores.handle, b_scores.after(b - 2, 4 * half + 4))
                for r, (pq, pk) in enumerate(PRODUCTS):
                    src = parts[u][:, :, :, :].rearrange("p q r s -> p (q r) s")
                    sp.dma_start(stack[u][HD * r:HD * r + HD, HH * half:HH * half + HH, :, :],
                                 src[64 * half:64 * half + 64, pq:4 + pk:3 + pk - pq, :])\
                        .then_inc(stack_in[u][half], 16)

            def stack_max(b, k, u, half):
                sp.wait_ge(mT_read.handle, mT_read.after(b, half + 1))
                sp.dma_start(stack[u][MROW:MROW + 2, HH * half:HH * half + HH, 0, :], mrow[half][:, :])\
                    .then_inc(m_in[u][half], 16)

            def store_x1(b, k, u):
                sp.wait_ge(x1_ready.handle, x1_ready.after(b))
                sp.dma_start(rows_of(x_view[1 + 2 * l], b), X1[u][:, :, :]).then_inc(x1_out[u], 16)

            weights = [(w1[:, :, :], a[f"w1_{l}"]), (w2[:, :, :, :], a[f"w2_{l}"])]
            if l == 1:
                weights += [(b1[:, :, :], a["b1"]), (b2[:, :, :], a["b2"])]
                for u in range(2):
                    sp.dma_start(stack[u][LIN:KROWS, :, :, :], a["stack_rows1"].bitcast(BF16)).then_inc(lin_in, 16)
                sp.wait_ge(lin_in, 32)
            for t in (x_in, stack_in, m_in, x1_out, front_in, back_in, base_out):
                t.start(sp)

            def tick(at):
                if at(0):
                    stack_up(*at(0), 1)
                if l == 1 and at(1):
                    store_base(*at(1))
                if at(-1):
                    stack_max(*at(-1), 1)
                    load_back(*at(-1))
                if at(1):
                    stack_up(*at(1), 0)
                if at(-2) and l == 1:
                    store_x1(*at(-2))
                if at(3):
                    load_front(*at(3))
                if at(-2) and l == 0:
                    store_x1(*at(-2))
                if at(0):
                    stack_max(*at(0), 0)

            for dst, src in weights:
                sp.dma_start(dst, src).then_inc(weights_in, 16)
            run_ticks(sp, tick)
            sp.wait_ge(weights_in, 16 * len(weights))
            for u in range(2):
                sp.wait_ge(x1_out[u], x1_out.of(B // 2 - 1))
                if l == 1:
                    sp.wait_ge(base_out[u], base_out.of(B // 2 - 1))

        @block.gpsimd
        def _(pool):
            start(pool, split, h2_ready, scattered, *([base_ready] if l else []))
            ch = Chain(pool, pool_order)

            def split_qk(b, k, u):
                pool.wait_ge(qk_f32.handle, qk_f32.after(b))
                for half in range(2):
                    pool.wait_ge(stack_in[u][half], stack_in.of(k - 1))
                p = parts[u]
                one = ones_col[:, :, :].broadcast_to([P, 2, S])
                ch.link(pool.tensor_tensor(p[:, :, 0, :], qk[:, :, :], one, ALU.mult))
                ch.link(pool.tensor_tensor(rem[:, :, :], qk[:, :, :], p[:, :, 0, :], ALU.subtract))
                ch.link(pool.tensor_tensor(p[:, :, 1, :], rem[:, :, :], one, ALU.mult))
                pool.tensor_tensor(p[:, :, 2, :], rem[:, :, :], p[:, :, 1, :], ALU.subtract).then_inc(split.handle, 1)

            def gather(b, k, u):
                pool.wait_ge(gslot_ready.handle, gslot_ready.after(b))
                pool.wait_ge(x2_ready.handle, x2_ready.after(b - 2))
                ch.apart()
                for c in range(2):
                    for t in range(NT):
                        pool.indirect_dma_start(Y[u][:, c, t, :], None, expert_out[0],
                                                bass.IndirectOffsetOnAxis(ap=gslot[u][:, c, t:t + 1], axis=0))\
                            .then_inc(y_in[u], 16)

            def residual_base(b, k, u):
                def row(n, x):
                    return x[:, n:n + 1, :].broadcast_to([P, NT, D])
                pool.wait_ge(xn_ready.handle, xn_ready.after(b))
                pool.wait_ge(base_out[u], base_out.of(k - 1))
                h = xh[u][:, :, :]
                ch.link(pool.tensor_tensor(h, xn[u][:, :, :], row(0, lnrow), ALU.mult))
                ch.link(pool.tensor_tensor(h, h, row(1, lnrow), ALU.add))
                ch.link(pool.tensor_tensor(h, h, row(GA, front_rows[u]), ALU.mult))
                pool.tensor_tensor(h, h, X[u][:, :, :], ALU.add).then_inc(base_ready.handle, 1)

            def modulate(b, k, u):
                pool.wait_ge(xn2_ready.handle, xn2_ready.after(b))
                pool.wait_ge(back_in[u], back_in.of(k))
                pool.wait_ge(scattered.handle, scattered.after(b - 2))
                ch.link(pool.tensor_tensor(h2[u][:, :, :], xn2[:, :, :],
                                           back_rows[u][:, CB - GA:CB - GA + 1, :].broadcast_to([P, NT, D]), ALU.mult))
                pool.tensor_tensor(h2[u][:, :, :], h2[u][:, :, :],
                                   back_rows[u][:, SB - GA:SB - GA + 1, :].broadcast_to([P, NT, D]), ALU.add)\
                    .then_inc(h2_ready.handle, 1)

            def scatter(b, k, u):
                pool.wait_ge(slots_ready.handle, slots_ready.after(b))
                ch.apart()
                for c in range(n_choice):
                    for t in range(NT):
                        pool.indirect_dma_start(gathered[l], bass.IndirectOffsetOnAxis(ap=slot_in[u][:, c, t:t + 1], axis=0),
                                                (h3 if l else h2)[u][:, t, :], None).then_inc(scat_out[u], 16)

            def scatter_done(b, k, u):
                pool.wait_ge(scat_out[u], scat_out.of(k))
                pool.sem_inc(scattered.handle, 1)

            def tick(at):
                if at(1):
                    split_qk(*at(1))
                if at(-2) and l == 1:
                    modulate(*at(-2))
                if at(-3):
                    scatter(*at(-3))
                if l == 1:
                    if at(1):
                        residual_base(*at(1))
                    if at(3):
                        gather(*at(3))
                if at(-2) and l == 0:
                    modulate(*at(-2))
                if at(-3):
                    scatter_done(*at(-3))

            run_ticks(pool, tick, ch, 9 if l else 5)

        @block.scalar
        def _(act):
            start(act, rsqrt, h_ready, v_ready, onT_read, y_read, rsqrt2, h2T_read, w_exp, mT_read, b_exp, o_read, qk_f32)
            if l == 1:
                start(act, h_rsqrt, rms_rsqrt)
            ch = Chain(act, act_order)
            act.preload_act_table_set("natural_log_exp_and_others")

            def rsqrt_of(b, var, dst, ready, sig):
                act.wait_ge(ready.handle, ready.after(b))
                ch.link(act.activation(dst, var, ACT.Ln))
                act.activation(dst, dst, ACT.Exp, scale=-0.5).then_inc(sig.handle, 1)

            def first_rsqrt(b, k, u):
                rsqrt_of(b, mv[u][:, :, 1], rs[u][:, :], stats, rsqrt)

            def inner_rsqrt(b, k, u):
                rsqrt_of(b, mv[u][:, :, 1], rs[u][:, :], h_stats, h_rsqrt)

            def second_rsqrt(b, k, u):
                rsqrt_of(b, mv2[:, :, 1], rs2[:, :], stats2, rsqrt2)

            def rms_rsqrt_of(b, k, u):
                rsqrt_of(b, mv2[:, :, 1], rs2[:, :], rms_stats, rms_rsqrt)

            def first_h(b, k, u):
                act.wait_ge(xn_T.handle, xn_T.after(b))
                act.wait_ge(v_proj.handle, v_proj.after(b - 2))
                act.activation(hT[u][:, :], M0[:, 0:S], ACT.Identity,
                               bias=ln_cols[:, 1:2] if l else mod[:, SA, bass.ds(b, 1)],
                               scale=ln_cols[:, 0:1] if l else mod[:, CA, bass.ds(b, 1)]).then_inc(h_ready.handle, 1)

            def read_qk(b, k, u):
                act.wait_ge(qk_proj.handle, qk_proj.after(b))
                act.wait_ge(split.handle, split.after(b - 1))
                m = M0[:, :].rearrange("p (j s) -> p j s", j=2)
                if l:
                    ch.mark(act.activation(qk[:, 0, :], m[:, 0, :], ACT.Identity, scale=q_scale[:, 1:2]))
                    ins = act.activation(qk[:, 1, :], m[:, 1, :], ACT.Copy)
                else:
                    ch.mark(act.activation(qk[:, 0, :], m[:, 0, :], ACT.Identity, bias=qs_bias[:, 0:1],
                                           scale=q_scale[:, 0:1]))
                    ins = act.activation(qk[:, 1, :], m[:, 1, :], ACT.Identity, bias=qk_bias[:, 1:2])
                ins.then_inc(qk_f32.handle, 1)

            def values(b, k, u):
                act.wait_ge(v_proj.handle, v_proj.after(b))
                act.wait_ge(pv.handle, pv.after(b - 2))
                act.activation(vals[u][:, :, :, 0:HD],
                               M0[:, 0:NT * D].rearrange("p (t h d) -> p t h d", t=NT, h=H), ACT.Copy)\
                    .then_inc(v_ready.handle, 1)

            def max_rows(b, k, u, half):
                act.wait_ge(m_T.handle, m_T.after(b, half + 1))
                act.wait_ge(m_in[1 - u][half], m_in.of(k - 1 + u))
                act.activation(mrow[half][:, :], M0b[0:2 * HH, 2 * S:3 * S], ACT.Copy).then_inc(mT_read.handle, 1)

            def exps(b, k, u, c):
                act.wait_ge(b_scores.handle, b_scores.after(b, c + 1))
                g4 = c // 2
                act.wait_ge(pv.handle, pv.after(b, g4 - 1) if g4 >= 2 else pv.after(b - 1, g4 + 3))
                act.activation(probs[c % 4][:, :, :, :], Bp[c % 2][:, :, :, :], ACT.Exp,
                               scale=EXP_SCALE[l][c // 4]).then_inc(b_exp.handle, 1)

            def head_sums(b, k, u, g):
                act.wait_ge(pv.handle, pv.after(b, g + 1))
                act.wait_ge(o_T.handle, o_T.after(b, g - 1) if g >= 2 else o_T.after(b - 1, g + 3))
                act.activation(heads[g % 2][:, :], M1[:, 0:S], ACT.Copy).then_inc(o_read.handle, 1)

            def read_on(b, k, u):
                act.wait_ge(on_T.handle, on_T.after(b))
                act.activation(OnT[:, :], M0[:, 0:S], ACT.Copy).then_inc(onT_read.handle, 1)

            def read_y(b, k, u):
                act.wait_ge(y_proj.handle, y_proj.after(b))
                act.activation(yT[:, :], M0[:, S:2 * S], ACT.Identity, bias=gob[:, bass.ds(b, 1)],
                               scale=mod[:, GA, bass.ds(b, 1)]).then_inc(y_read.handle, 1)

            def second_h(b, k, u):
                act.wait_ge(h2_T.handle, h2_T.after(b))
                if l:
                    act.activation(h2T[:, :], M0[:, 0:S], ACT.Identity, scale=ln_cols[:, 2:3]).then_inc(h2T_read.handle, 1)
                else:
                    act.activation(h2T[:, :], M0[:, 0:S], ACT.Copy).then_inc(h2T_read.handle, 1)

            def weights(b, k, u):
                act.wait_ge(w_den.handle, w_den.after(b))
                if l:
                    act.activation(rt[:, 4, :, :], rt[:, 3, :, :], ACT.Exp).then_inc(w_exp.handle, 1)
                else:
                    act.activation(r1[:, 5, :], r1[:, 4, :], ACT.Exp).then_inc(w_exp.handle, 1)

            def tick(at):
                if at(1):
                    first_h(*at(1))
                if at(-3):
                    weights(*at(-3))
                if at(-1):
                    exps(*at(-1), 0)
                if at(-2):
                    head_sums(*at(-2), 3)
                if at(1):
                    read_qk(*at(1))
                if at(-1):
                    exps(*at(-1), 1)
                    max_rows(*at(-1), 1)
                if at(0):
                    values(*at(0))
                if at(2):
                    first_rsqrt(*at(2))
                if at(-1):
                    exps(*at(-1), 2)
                if at(-2):
                    if l == 0:
                        read_on(*at(-2))
                if at(-1):
                    head_sums(*at(-1), 0)
                if at(-2):
                    if l == 0:
                        read_y(*at(-2))
                    else:
                        second_rsqrt(*at(-2))
                if at(-1):
                    exps(*at(-1), 3)
                if at(0):
                    max_rows(*at(0), 0)
                if at(-1):
                    exps(*at(-1), 4)
                    head_sums(*at(-1), 1)
                if at(2) and l:
                    inner_rsqrt(*at(2))
                if at(-2) and l == 0:
                    second_rsqrt(*at(-2))
                if at(-2) and l == 1:
                    rms_rsqrt_of(*at(-2))
                if at(-1):
                    exps(*at(-1), 5)
                if at(-1):
                    exps(*at(-1), 6)
                    head_sums(*at(-1), 2)
                if at(-2):
                    second_h(*at(-2))
                if at(-1):
                    exps(*at(-1), 7)

            run_ticks(act, tick, ch, 5 if l else 3)

        @block.vector
        def _(dve):
            start(dve, stats, xn_ready, x1_ready, stats2, xn2_ready, logits_read, slots_ready, pos_read,
                  sel_ready, w_den, a_max, o_norm, m_split)
            if l == 1:
                start(dve, gslot_ready, x2_ready, h_rows, h_stats, rms_stats, h3_ready)
            ch = Chain(dve, dve_order)
            if l == 1:
                ch.link(dve.tensor_copy(run[:, :], region_row[:, :]))

            def aggregate(st, mv):
                ch.settle_apart()
                for t in range(NT):
                    ch.mark(dve.bn_aggr(mv[:, t, :], st[:, t, :]))
                ch.settle()

            def moments(x, st, mv, sig, eps=EPS[l]):
                for t in range(NT):
                    ch.mark(dve.bn_stats(st[:, t, :], x[:, t, :]))
                aggregate(st, mv)
                dve.tensor_scalar(mv[:, :, 1], mv[:, :, 1], eps, None, ALU.add).then_inc(sig.handle, 1)

            def newton(mv, rs):
                n = newt
                ch.link(dve.tensor_tensor(n[:, 0, :], mv[:, :, 1], rs[:, :], ALU.mult))
                ch.link(dve.scalar_tensor_tensor(out=n[:, 1, :], in0=n[:, 0, :], scalar=-0.5, in1=rs[:, :],
                                                 op0=ALU.mult, op1=ALU.mult))
                ch.link(dve.scalar_tensor_tensor(out=n[:, 2, :], in0=n[:, 1, :], scalar=1.5, in1=rs[:, :],
                                                 op0=ALU.add, op1=ALU.mult))

            def normed(x, mv, rs, dst, sig):
                newton(mv, rs)
                n = newt
                for t in range(NT):
                    ins = dve.tensor_scalar(dst[:, t, :], x[:, t, :], mv[:, t, 0:1], n[:, 2, t:t + 1],
                                            ALU.subtract, ALU.mult)
                    if t < NT - 1:
                        ch.mark(ins)
                ch.settle()
                ins.then_inc(sig.handle, 1)

            def first_stats(b, k, u):
                dve.wait_ge(x_in[u], x_in.of(k))
                moments(X[u], st, mv[u], stats)

            def first_norm(b, k, u):
                dve.wait_ge(rsqrt.handle, rsqrt.after(b))
                dve.wait_ge(xn_T.handle, xn_T.after(b - 2))
                normed(X[u], mv[u], rs[u], xn[u], xn_ready)

            def gather_slots(b, k, u):
                dve.tensor_scalar(gslot[u][:, :, :], yslot[:, bass.ds(b, 1), :, :].rearrange("p o c t -> p (o c) t"),
                                  1.0, None, ALU.mult).then_inc(gslot_ready.handle, 1)

            def add_experts(b, k, u):
                dve.wait_ge(y_in[u], y_in.of(k))
                dve.wait_ge(front_in[u], front_in.of(k))
                dve.wait_ge(x_in[u], x_in.of(k))
                y = Y[u]
                for t in range(NT):
                    ch.mark(dve.tensor_scalar(y[:, 0, t, :], y[:, 0, t, :],
                                              wtok[:, bass.ds(b, 1), 0, t:t + 1].rearrange("p o t -> p (o t)"), None, ALU.mult))
                ch.settle()
                for t in range(NT):
                    ch.mark(dve.scalar_tensor_tensor(out=y[:, 0, t, :], in0=y[:, 1, t, :],
                                                     scalar=wtok[:, bass.ds(b, 1), 1, t:t + 1].rearrange("p o t -> p (o t)"),
                                                     in1=y[:, 0, t, :], op0=ALU.mult, op1=ALU.add))
                ch.settle()
                ch.link(dve.tensor_tensor(y[:, 0, :, :], y[:, 0, :, :], gb_row[u][:, :, :].broadcast_to([P, NT, D]), ALU.mult))
                dve.tensor_tensor(X[u][:, :, :], X[u][:, :, :], y[:, 0, :, :], ALU.add).then_inc(x2_ready.handle, 1)

            def added_stats(b, k, u):
                dve.wait_ge(x2_ready.handle, x2_ready.after(b))
                moments(X[u], st, mv[u], stats)

            def outer_norm(b, k, u):
                dve.wait_ge(rsqrt.handle, rsqrt.after(b))
                dve.wait_ge(xn_T.handle, xn_T.after(b - 2))
                dve.wait_ge(base_ready.handle, base_ready.after(b - 2))
                normed(X[u], mv[u], rs[u], xn[u], h_rows)
                dve.wait_ge(h_rows.handle, h_rows.after(b))
                ch.link(dve.tensor_tensor(xn[u][:, :, :], xn[u][:, :, :],
                                          front_rows[u][:, CA:CA + 1, :].broadcast_to([P, NT, D]), ALU.mult))
                ch.link(dve.tensor_tensor(xn[u][:, :, :], xn[u][:, :, :],
                                          front_rows[u][:, SA:SA + 1, :].broadcast_to([P, NT, D]), ALU.add))
                moments(xn[u], st, mv[u], h_stats, EPS_IN)

            def inner_norm(b, k, u):
                dve.wait_ge(h_rsqrt.handle, h_rsqrt.after(b))
                normed(xn[u], mv[u], rs[u], xn[u], xn_ready)

            def row_max(b, k, u, h):
                dve.wait_ge(a_scores.handle, a_scores.after(b, h + 1))
                if h == 0:
                    dve.wait_ge(m_split.handle, m_split.after(b - 2))
                dve.tensor_reduce(mx[u][:, h, :], A[h % 2][:, :, :], AX.X, ALU.max).then_inc(a_max.handle, 1)

            def split_max(b, k, u, half):
                dve.wait_ge(a_max.handle, a_max.after(b, HH * (half + 1)))
                dve.wait_ge(m_T.handle, m_T.after(b - 1, half + 1))
                v = mx[u][:, HH * half:HH * half + HH, :].rearrange("p h t -> p t h")
                ch.link(dve.tensor_scalar(mneg[:, half, :, 0, :], v, -1.0, None, ALU.mult))
                dve.scalar_tensor_tensor(out=mneg[:, half, :, 1, :], in0=v, scalar=-1.0, in1=mneg[:, half, :, 0, :],
                                         op0=ALU.mult, op1=ALU.subtract).then_inc(m_split.handle, 1)

            def normalise(b, k, u, g):
                dve.wait_ge(o_T.handle, o_T.after(b, g + 1))
                if g == 0:
                    if l:
                        dve.wait_ge(x1_ready.handle, x1_ready.after(b - 2))
                    else:
                        dve.wait_ge(on_T.handle, on_T.after(b - 2))
                dve.wait_ge(o_norm.handle, o_norm.after(b, g) if g else o_norm.after(b - 1))
                o = M1[:, S:2 * S].rearrange("p (t j w) -> p t j w", t=NT, j=4)
                ch.link(dve.reciprocal(rsum[:, :, :], o[:, :, :, HD]))
                dst = On[u][:, :, 4 * g:4 * g + 4, :] if l == 0 else \
                    On[u][:, :, :, :].rearrange("p t (h f) d -> p t f h d", f=2)[:, :, g // 2, 4 * (g % 2):4 * (g % 2) + 4, :]
                dve.tensor_tensor(dst, o[:, :, :, 0:HD],
                                  rsum[:, :, :].unsqueeze(3).broadcast_to([P, NT, 4, HD]), ALU.mult)\
                    .then_inc(o_norm.handle, 1)

            def residual(b, k, u):
                dve.wait_ge(back_in[u], back_in.of(k))
                dve.wait_ge(x1_out[u], x1_out.of(k - 1))
                if l:
                    dve.wait_ge(o_norm.handle, o_norm.after(b))
                    ch.link(dve.tensor_tensor(X1[u][:, :, :], On[u][:, :, :, :].rearrange("p t h d -> p t (h d)"),
                                              back_rows[u][:, 0:1, :].broadcast_to([P, NT, D]), ALU.mult))
                    dve.tensor_tensor(X1[u][:, :, :], X1[u][:, :, :], XR[u][:, :, :], ALU.add).then_inc(x1_ready.handle, 1)
                else:
                    dve.wait_ge(y_T.handle, y_T.after(b))
                    dve.tensor_tensor(X1[u][:, :, :], XR[u][:, :, :], M0[:, 0:S].rearrange("p (t d) -> p t d", t=NT),
                                      ALU.add).then_inc(x1_ready.handle, 1)

            def second_stats(b, k, u):
                dve.wait_ge(x1_ready.handle, x1_ready.after(b))
                moments(X1[u], st2, mv2, stats2)

            def second_norm(b, k, u):
                dve.wait_ge(rsqrt2.handle, rsqrt2.after(b))
                dve.wait_ge(h2_ready.handle, h2_ready.after(b - 1))
                normed(X1[u], mv2, rs2, xn2, xn2_ready)

            def rms_moments(b, k, u):
                dve.wait_ge(h2_ready.handle, h2_ready.after(b))
                for t in range(NT):
                    ch.mark(dve.bn_stats(st2[:, t, :], h2[u][:, t, :]))
                aggregate(st2, mv2)
                ch.link(dve.tensor_tensor(mv2[:, :, 0], mv2[:, :, 0], mv2[:, :, 0], ALU.mult))
                dve.scalar_tensor_tensor(out=mv2[:, :, 1], in0=mv2[:, :, 1], scalar=EPS_IN, in1=mv2[:, :, 0],
                                         op0=ALU.add, op1=ALU.add).then_inc(rms_stats.handle, 1)

            def rms_norm(b, k, u):
                dve.wait_ge(rms_rsqrt.handle, rms_rsqrt.after(b))
                newton(mv2, rs2)
                dve.wait_ge(scattered.handle, scattered.after(b - 2))
                ch.mark(dve.tensor_scalar(h3[u][:, 0, :], h2[u][:, 0, :], newt[:, 2, 0:1], None, ALU.mult))
                ch.settle()
                dve.tensor_scalar(h3[u][:, 1, :], h2[u][:, 1, :], newt[:, 2, 1:2], None, ALU.mult)\
                    .then_inc(h3_ready.handle, 1)

            def first_of(src, top, eq, cand, idx, dst):
                ch.link(dve.tensor_reduce(top, src, AX.X, ALU.max))
                ch.link(dve.tensor_tensor(eq, src, top.unsqueeze(2).broadcast_to([P, NT, E]), ALU.is_equal))
                ch.link(dve.tensor_tensor(cand, eq, rev_iota[:, :, :], ALU.mult))
                ch.link(dve.tensor_reduce(idx, cand, AX.X, ALU.max))
                ch.link(dve.tensor_tensor(dst, rev_iota[:, :, :], idx.unsqueeze(2).broadcast_to([P, NT, E]),
                                          ALU.is_equal))

            def choose_first(b, k, u):
                dve.wait_ge(logits.handle, logits.after(b))
                dve.tensor_copy(lg[:, :, :], M0[:, LG:LG + NT * E].rearrange("p (t e) -> p t e", t=NT))\
                    .then_inc(logits_read.handle, 1)
                dve.wait_ge(logits_read.handle, logits_read.after(b))
                first_of(lg[:, :, :], r1[:, 0, :], rt[:, 0, :, :], rt[:, 1, :, :], r1[:, 1, :], rt[:, 2, :, :])
                ch.mark(dve.tensor_scalar(chosen[:, bass.ds(b, 1), 0, :, :], rt[:, 2, :, :].unsqueeze(1), 1.0, None, ALU.mult))
                if l:
                    dve.wait_ge(pos.handle, pos.after(b - 1))
                    dve.tensor_copy(sel[:, :, :], rt[:, 2, :, :]).then_inc(sel_ready.handle, 1)
                    dve.tensor_tensor(rt[:, 3, :, :], lg[:, :, :], r1[:, 0, :].unsqueeze(2).broadcast_to([P, NT, E]),
                                      ALU.subtract).then_inc(w_den.handle, 1)

            def choose_second(b, k, u):
                ch.link(dve.scalar_tensor_tensor(out=rt[:, 3, :, :], in0=rt[:, 2, :, :], scalar=-BIG, in1=lg[:, :, :],
                                                 op0=ALU.mult, op1=ALU.add))
                first_of(rt[:, 3, :, :], r1[:, 2, :], rt[:, 0, :, :], rt[:, 1, :, :], r1[:, 3, :], rt[:, 4, :, :])
                dve.wait_ge(pos.handle, pos.after(b - 1))
                dve.tensor_tensor(sel[:, :, :], rt[:, 2, :, :], rt[:, 4, :, :], ALU.add).then_inc(sel_ready.handle, 1)
                dve.tensor_tensor(r1[:, 4, :], r1[:, 2, :], r1[:, 0, :], ALU.subtract).then_inc(w_den.handle, 1)
                ch.mark(dve.tensor_scalar(chosen[:, bass.ds(b, 1), 1, :, :], rt[:, 4, :, :].unsqueeze(1), 1.0, None, ALU.mult))

            def weigh_choices(b, k, u):
                dve.wait_ge(w_exp.handle, w_exp.after(b))
                if l:
                    ch.link(dve.tensor_reduce(r1[:, 6, :], rt[:, 4, :, :], AX.X, ALU.add))
                    ch.link(dve.reciprocal(r1[:, 7, :], r1[:, 6, :]))
                    ch.mark(dve.tensor_scalar(wtok[:, bass.ds(b, 1), 0, :], r1[:, 7, :].unsqueeze(1), 1.0, None, ALU.mult))
                else:
                    ch.link(dve.tensor_scalar(r1[:, 6, :], r1[:, 5, :], 1.0, None, ALU.add))
                    ch.link(dve.reciprocal(r1[:, 7, :], r1[:, 6, :]))
                    ch.mark(dve.tensor_scalar(wtok[:, bass.ds(b, 1), 0, :], r1[:, 7, :].unsqueeze(1), 1.0, None, ALU.mult))
                    ch.mark(dve.tensor_tensor(wtok[:, bass.ds(b, 1), 1, :], r1[:, 5, :].unsqueeze(1),
                                              r1[:, 7, :].unsqueeze(1), ALU.mult))

            def place(b, k, u):
                dve.wait_ge(pos.handle, pos.after(b))
                dve.wait_ge(scattered.handle, scattered.after(b - 2))
                ch.settle()
                ch.link(dve.tensor_tensor(rt[:, 5, :, :], M0[:, PS:PS + NT * E].rearrange("p (t e) -> p t e", t=NT),
                                          run[:, :].unsqueeze(1).broadcast_to([P, NT, E]), ALU.add))
                dve.tensor_tensor(run[:, :], run[:, :], M0[:, PS + NT * E:PS + NT * E + E], ALU.add)\
                    .then_inc(pos_read.handle, 1)
                for c in range(n_choice):
                    ch.link(dve.tensor_tensor(rt[:, 6, :, :], rt[:, 2 + 2 * c, :, :], rt[:, 5, :, :], ALU.mult))
                    ch.link(dve.tensor_reduce(r1[:, 8 + c, :], rt[:, 6, :, :], AX.X, ALU.add))
                ch.mark(dve.tensor_scalar(slotf[:, bass.ds(b, 1), 0:n_choice, :], r1[:, 8:8 + n_choice, :].unsqueeze(1),
                                          1.0, None, ALU.mult))
                dve.wait_ge(pos_read.handle, pos_read.after(b))
                dve.tensor_copy(slot_in[u][:, 0:n_choice, :], r1[:, 8:8 + n_choice, :]).then_inc(slots_ready.handle, 1)

            def tick(at):
                def maxima(first, n):
                    if at(0):
                        for h in range(first, first + n):
                            row_max(*at(0), h)

                if at(-1):
                    split_max(*at(-1), 1)
                maxima(0, 1)
                if at(-2):
                    normalise(*at(-2), 2)
                maxima(1, 1)
                if at(-3):
                    place(*at(-3))
                if l and at(3):
                    gather_slots(*at(3))
                maxima(2, 1)
                if at(-3):
                    weigh_choices(*at(-3))
                maxima(3, 1)
                if at(2):
                    if l:
                        add_experts(*at(2))
                        added_stats(*at(2))
                    else:
                        first_stats(*at(2))
                maxima(4, 1)
                if at(-2):
                    normalise(*at(-2), 3)
                    if l:
                        residual(*at(-2))
                        second_stats(*at(-2))
                maxima(5, 1)
                if at(2):
                    if l:
                        outer_norm(*at(2))
                    else:
                        first_norm(*at(2))
                maxima(6, 2)
                if at(0):
                    split_max(*at(0), 0)
                if at(-2) and l:
                    second_norm(*at(-2))
                maxima(8, 1)
                if at(-1):
                    normalise(*at(-1), 0)
                if at(-2) and l == 0:
                    residual(*at(-2))
                    second_stats(*at(-2))
                maxima(9, 1)
                if at(2) and l:
                    inner_norm(*at(2))
                maxima(10, 1)
                if at(-2) and l:
                    rms_moments(*at(-2))
                maxima(11, 1)
                if at(-2) and l == 0:
                    second_norm(*at(-2))
                maxima(12, 1)
                if at(-1):
                    normalise(*at(-1), 1)
                if at(-2) and l:
                    rms_norm(*at(-2))
                maxima(13, 3)
                if at(-2):
                    choose_first(*at(-2))
                    if l == 0:
                        choose_second(*at(-2))

            run_ticks(dve, tick, ch, 64 if l else 47)

        @block.tensor
        def _(pe):
            start(pe, xn_T, qk_proj, v_proj, on_T, y_proj, y_T, h2_T, logits, pos, a_scores, m_T, b_scores, pv, o_T)

            def turn(src, ready, b, sig):
                pe.wait_ge(ready.handle, ready.after(b))
                for t in range(NT):
                    ins = pe.transpose(M0[:, t * P:(t + 1) * P], src[:, t * P:(t + 1) * P], ident[:, :])
                ins.then_inc(sig.handle, 1)

            def flat(x):
                return x[:, :, :].rearrange("p t d -> p (t d)")

            def project_qk(b, k, u):
                pe.wait_ge(h_ready.handle, h_ready.after(b))
                pe.matmul(M0[:, 0:S], wq[:, l, :], hT[u][:, :], start=True, stop=True)
                pe.matmul(M0[:, S:2 * S], wk[:, l, :], hT[u][:, :], start=True, stop=True).then_inc(qk_proj.handle, 1)

            def project_v(b, k, u):
                for t in range(NT):
                    ins = pe.matmul(M0[:, t * P:(t + 1) * P], hT[u][:, t * P:(t + 1) * P], wv[:, l, :],
                                    start=True, stop=True)
                ins.then_inc(v_proj.handle, 1)

            def scores_a(b, k, u, h):
                if h % HH == 0:
                    pe.wait_ge(stack_in[u][h // HH], stack_in.of(k))
                pe.wait_ge(a_max.handle, a_max.after(b, h - 1) if h >= 2 else a_max.after(b - 1, H + h - 1))
                n = MROW if l == 0 else LIN
                for t in range(NT):
                    ins = pe.matmul(A[h % 2][:, t, :], stack[u][0:n, h, 0, t * P:(t + 1) * P],
                                    stack[u][0:n, h, 1, :], start=True, stop=(l == 1))
                    if l == 0:
                        ins = pe.matmul(A[h % 2][:, t, t * P:(t + 1) * P], slope_ident[:, h % HH, :],
                                        dist[:, t, :], start=False, stop=True)
                ins.then_inc(a_scores.handle, 1)

            def turn_max(b, k, u, half):
                pe.wait_ge(m_split.handle, m_split.after(b, half + 1))
                for t in range(NT):
                    ins = pe.transpose(M0b[0:2 * HH, 2 * S + t * P:2 * S + (t + 1) * P],
                                       mneg[:, half, t, :, :].rearrange("p c h -> p (c h)"), ident_b[:, :])
                ins.then_inc(m_T.handle, 1)

            def scores_b(b, k, u, c):
                if c % 4 == 0:
                    pe.wait_ge(m_in[u][c // 4], m_in.of(k))
                pe.wait_ge(b_exp.handle, b_exp.after(b, c - 1) if c >= 2 else b_exp.after(b - 1, HH + c - 1))
                for j in range(2):
                    h = 2 * c + j
                    for t in range(NT):
                        ins = pe.matmul(Bp[c % 2][:, j, t, :], stack[u][0:KROWS, h, 1, t * P:(t + 1) * P],
                                        stack[u][0:KROWS, h, 0, :], start=True, stop=(l == 1))
                        if l == 0:
                            ins = pe.matmul(Bp[c % 2][:, j, t, t * P:(t + 1) * P], slope_ident[:, h % HH, :],
                                            dist[:, 1 - t, :], start=False, stop=True)
                ins.then_inc(b_scores.handle, 1)

            def weigh(b, k, u, g):
                if g == 0:
                    pe.wait_ge(v_ready.handle, v_ready.after(b))
                pe.wait_ge(b_exp.handle, b_exp.after(b, 2 * g + 2))
                pe.wait_ge(o_norm.handle, o_norm.after(b, g) if g else o_norm.after(b - 1))
                for t in range(NT):
                    for j in range(4):
                        ins = pe.matmul(M1[VW * j:VW * j + VW, 0:S], vals[u][:, t, 4 * g + j, :],
                                        probs[(2 * g + j // 2) % 4][:, j % 2, t, :],
                                        start=(t == 0), stop=(t == NT - 1), tile_position=(0, VW * j))
                ins.then_inc(pv.handle, 1)

            def turn_heads(b, k, u, g):
                pe.wait_ge(o_read.handle, o_read.after(b, g + 1))
                for t in range(NT):
                    ins = pe.transpose(M1[:, S + t * P:S + (t + 1) * P], heads[g % 2][:, t * P:(t + 1) * P], ident[:, :])
                ins.then_inc(o_T.handle, 1)

            def project_out(b, k, u):
                pe.wait_ge(onT_read.handle, onT_read.after(b))
                pe.matmul(M0[:, S:2 * S], wo[:, :], OnT[:, :], start=True, stop=True).then_inc(y_proj.handle, 1)

            def gate(b, k, u):
                pe.wait_ge(h2T_read.handle, h2T_read.after(b))
                for t in range(NT):
                    ins = pe.matmul(M0[:, LG + t * E:LG + (t + 1) * E], h2T[:, t * P:(t + 1) * P], gate_w[:, l, :],
                                    start=True, stop=True)
                ins.then_inc(logits.handle, 1)

            def count(b, k, u):
                pe.wait_ge(sel_ready.handle, sel_ready.after(b))
                pe.matmul(M0[:, PS:PS + E], before_tri[:, :], sel[:, 0, :], start=True, stop=True)
                pe.matmul(M0[:, PS + E:PS + 2 * E], before_tri[:, :], sel[:, 1, :], start=True, stop=False)
                pe.matmul(M0[:, PS + E:PS + 2 * E], ones_b[:, :], sel[:, 0, :], start=False, stop=True)
                pe.matmul(M0[:, PS + 2 * E:PS + 3 * E], ones_b[:, :], sel[:, 0, :], start=True, stop=False)
                pe.matmul(M0[:, PS + 2 * E:PS + 3 * E], ones_b[:, :], sel[:, 1, :], start=False, stop=True)\
                    .then_inc(pos.handle, 1)

            def tick(at):
                def a_pass(*hs):
                    if at(0):
                        for h in hs:
                            scores_a(*at(0), h)

                def m0_read(*uses):
                    for sig, off, *n in uses:
                        if at(off):
                            pe.wait_ge(sig.handle, sig.after(at(off)[0], *n))
                            return

                a_pass(0)
                if at(1):
                    m0_read((logits_read, -3), (mT_read, -1, 1), (qk_f32, 0))
                    turn(flat(xn[at(1)[2]]), xn_ready, at(1)[0], xn_T)
                a_pass(1)
                if at(-3):
                    m0_read((h_ready, 1), (logits_read, -3))
                    count(*at(-3))
                if at(-1):
                    scores_b(*at(-1), 0)
                if at(-2):
                    weigh(*at(-2), 3)
                a_pass(2, 3)
                if at(1):
                    m0_read((pos_read, -3))
                    project_qk(*at(1))
                if at(-1):
                    scores_b(*at(-1), 1)
                if at(-2):
                    turn_heads(*at(-2), 3)
                a_pass(4)
                if at(-1):
                    m0_read((qk_f32, 1), (pos_read, -3))
                    turn_max(*at(-1), 1)
                a_pass(5)
                if at(0):
                    m0_read((mT_read, -1, 2), (qk_f32, 1))
                    project_v(*at(0))
                if at(-1):
                    scores_b(*at(-1), 2)
                    weigh(*at(-1), 0)
                a_pass(6)
                if at(-2) and l == 0:
                    m0_read((v_ready, 0), (mT_read, -1, 2), (pos_read, -3))
                    turn(On[at(-2)[2]][:, :, :, :].rearrange("p t h d -> p (t h d)"), o_norm, at(-2)[0], on_T)
                a_pass(7)
                if at(-2) and l == 0:
                    project_out(*at(-2))
                if at(-1):
                    scores_b(*at(-1), 3)
                    turn_heads(*at(-1), 0)
                a_pass(8, 9)
                if at(-2) and l == 0:
                    turn(yT, y_read, at(-2)[0], y_T)
                if at(-1):
                    scores_b(*at(-1), 4)
                    weigh(*at(-1), 1)
                if at(0):
                    m0_read(*[(x1_ready, -2)] * (l == 0), (v_ready, 0))
                    turn_max(*at(0), 0)
                a_pass(10, 11)
                if at(-1):
                    scores_b(*at(-1), 5)
                    turn_heads(*at(-1), 1)
                a_pass(12, 13)
                if at(-2):
                    m0_read((mT_read, 0, 1), *[(x1_ready, -2)] * (l == 0), (mT_read, -1, 2), (pos_read, -3))
                    turn(flat((h3 if l else h2)[at(-2)[2]]), h3_ready if l else h2_ready, at(-2)[0], h2_T)
                if at(-1):
                    scores_b(*at(-1), 6)
                    weigh(*at(-1), 2)
                a_pass(14, 15)
                if at(-2):
                    gate(*at(-2))
                if at(-1):
                    scores_b(*at(-1), 7)
                    turn_heads(*at(-1), 2)

            run_ticks(pe, tick)


def experts(nc, l, g):
    (ident, ones_row, zero_rows, region_row, tile_iota, run, run_i, cnt_i, n_tiles, tile_base, corr, reached, tile_tab,
     tile_e, tile_row, yslotf, yslot, chosen, slotf, w1, w2, b1, b2, w1s, xt, xtT, hid, yt, A, Bp, M0, M1, ln_cols,
     gathered, expert_out) = (g[n] for n in (
        "ident ones_row zero_rows region_row tile_iota run run_i cnt_i n_tiles tile_base corr reached tile_tab "
        "tile_e tile_row yslotf yslot chosen slotf w1 w2 b1 b2 w1s xt xtT hid yt A Bp M0 M1 ln_cols "
        "gathered expert_out").split())
    slots, n_choice = SLOTS[l], CHOICES[l]

    def sem(name):
        return nc.alloc_semaphore(f"L{l}_{name}")

    def signals(*names):
        return [Signal(sem(n), 1) for n in names]

    run_ready, table_ready = sem("run_ready"), sem("table_ready")
    zeroed = sem("slack_zeroed")
    xt_in = Transfers([sem(f"xt_in{u}") for u in range(2)], 1)
    yt_out = Transfers([sem(f"yt_out{u}") for u in range(2)], 1)
    xt_T, xtT_ready, w1_staged, first, hidden, second, y_done = signals(
        "xt_T", "xtT_ready", "w1_staged", "first_products", "hidden", "second_products", "y_done")
    dve_order = sem("tiles_dve_order")

    with nc.Block() as block:

        @block.sync
        def _(sp):
            for t in (xt_in, yt_out):
                t.start(sp)
            sp.wait_ge(run_ready, 1)
            for e in range(E):
                r = sp.value_load(run_i[0:1, e:e + 1], min_val=e * REGION, max_val=(e + 1) * REGION - TOK)
                sp.dma_start(gathered[l][bass.ds(r, TOK), :].rearrange("(t p) d -> p t d", p=P), zero_rows[:, :, :])\
                    .then_inc(zeroed, 16)
            sp.wait_ge(table_ready, 1)
            sp.wait_ge(zeroed, 16 * E)
            out_view = expert_out[l].rearrange("(s t p) d -> s p t d", t=NT, p=P)

            def load_tile(s, k, u):
                row = sp.value_load(tile_row[0:1, bass.ds(s, 1)], min_val=0, max_val=E * REGION - TOK)
                sp.wait_ge(xt_T.handle, xt_T.after(s - 2))
                sp.dma_start(xt[u][:, :, :], gathered[l][bass.ds(row, TOK), :].rearrange("(t p) d -> p t d", p=P))\
                    .then_inc(xt_in[u], 16)

            def store_tile(s, k, u):
                sp.wait_ge(y_done.handle, y_done.after(s))
                sp.dma_start(out_view[bass.ds(s, 1)].rearrange("o p t d -> (o p) t d"), yt[u][:, :, :])\
                    .then_inc(yt_out[u], 16)

            with sp.Fori(0, slots // 2) as k:
                for u in range(2):
                    load_tile(k * 2 + u, k, u)
                for u in range(2):
                    store_tile(k * 2 + u, k, u)
            for u in range(2):
                sp.wait_ge(yt_out[u], yt_out.of(slots // 2 - 1))

        @block.vector
        def _(dve):
            ch = Chain(dve, dve_order)
            for s in (xtT_ready, w1_staged, y_done):
                dve.sem_inc(s.handle, 2)
            dve.tensor_copy(run_i[:, :], run[:, :]).then_inc(run_ready, 1)
            ch.link(dve.tensor_tensor(n_tiles[:, :], run[:, :], region_row[:, :], ALU.subtract))
            ch.link(dve.tensor_scalar(n_tiles[:, :], n_tiles[:, :], float(TOK - 1), None, ALU.add))
            ch.link(dve.tensor_copy(cnt_i[:, :], n_tiles[:, :]))
            ch.link(dve.tensor_scalar(cnt_i[:, :], cnt_i[:, :], TOK.bit_length() - 1, None, ALU.logical_shift_right))
            ch.mark(dve.tensor_copy(n_tiles[:, :], cnt_i[:, :]))
            ch.link(dve.memset(tile_base[:, 0:1], 0.0))
            for e in range(E):
                ch.link(dve.tensor_tensor(tile_base[:, e + 1:e + 2], tile_base[:, e:e + 1], n_tiles[:, e:e + 1], ALU.add))
            base = tile_base[:, 0:E].unsqueeze(1).broadcast_to([P, slots, E])
            r = reached[:, 0:slots, :]
            tab = tile_tab[:, :, 0:slots]
            ch.link(dve.tensor_tensor(r, tile_iota[:, 0:slots, :], base, ALU.is_ge))
            ch.link(dve.tensor_reduce(tab[:, 0, :], r, AX.X, ALU.add))
            ch.link(dve.tensor_tensor(r, r, base, ALU.mult))
            ch.link(dve.tensor_reduce(tab[:, 1, :], r, AX.X, ALU.max))
            ch.link(dve.tensor_tensor(tab[:, 1, :], tile_iota[:, 0:slots, 0], tab[:, 1, :], ALU.subtract))
            ch.link(dve.tensor_scalar(tab[:, 0, :], tab[:, 0, :], -1.0, None, ALU.add))
            ch.link(dve.tensor_scalar(tab[:, 1, :], tab[:, 1, :], float(TOK), None, ALU.mult))
            ch.link(dve.scalar_tensor_tensor(out=tab[:, 1, :], in0=tab[:, 0, :], scalar=float(REGION), in1=tab[:, 1, :],
                                             op0=ALU.mult, op1=ALU.add))
            ch.link(dve.tensor_scalar(tab[:, 2, :], tile_iota[:, 0:slots, 0], tile_base[:, E:E + 1], None, ALU.is_lt))
            ch.mark(dve.tensor_tensor(tile_e[:, 0:slots], tab[:, 0, :], tab[:, 2, :], ALU.mult))
            ch.mark(dve.tensor_tensor(tile_row[:, 0:slots], tab[:, 1, :], tab[:, 2, :], ALU.mult))
            ch.link(dve.scalar_tensor_tensor(out=corr[:, :], in0=tile_base[:, 0:E], scalar=float(TOK), in1=region_row[:, :],
                                             op0=ALU.mult, op1=ALU.subtract))
            dve.tensor_copy(n_tiles[:, :], corr[:, :]).then_inc(table_ready, 1)
            for c in range(n_choice):
                v = chosen[:, :, c, :, :]
                for t in range(NT):
                    ch.mark(dve.tensor_tensor(v[:, :, t, :], v[:, :, t, :], corr[:, :].unsqueeze(1).broadcast_to([P, B, E]), ALU.mult))
                ch.settle()
                ch.link(dve.tensor_reduce(yslotf[:, :, c, :], v, AX.X, ALU.add))
                ch.link(dve.tensor_tensor(yslot[:, :, c, :], yslotf[:, :, c, :], slotf[:, :, c, :], ALU.add))

            dve.wait_ge(table_ready, 1)

            def stage_w1(s, k, u):
                e = dve.value_load(tile_e[0:1, bass.ds(s, 1)], min_val=0, max_val=E - 1)
                dve.wait_ge(first.handle, first.after(s - 2))
                dve.tensor_scalar(w1s[u][:, :], w1[:, bass.ds(e, 1), :].rearrange("p o f -> p (o f)"), 1.0, None, ALU.mult)\
                    .then_inc(w1_staged.handle, 1)

            def read_xT(s, k, u):
                dve.wait_ge(xt_T.handle, xt_T.after(s))
                dve.wait_ge(first.handle, first.after(s - 2))
                m = (M0, M1)[u]
                if l:
                    dve.tensor_scalar(xtT[u][:, :], m[:, 0:TOK], ln_cols[:, 2:3], None, ALU.mult).then_inc(xtT_ready.handle, 1)
                else:
                    dve.tensor_copy(xtT[u][:, :], m[:, 0:TOK]).then_inc(xtT_ready.handle, 1)

            def read_y(s, k, u):
                dve.wait_ge(second.handle, second.after(s))
                dve.wait_ge(yt_out[u], yt_out.of(k - 1))
                dve.tensor_copy(yt[u][:, :, :], A[u][:, :, 0:D]).then_inc(y_done.handle, 1)

            with dve.Fori(0, slots // 2) as k:
                for u in range(2):
                    stage_w1(k * 2 + u, k, u)
                    read_xT(k * 2 + u, k, u)
                for u in range(2):
                    read_y(k * 2 + u, k, u)

        @block.scalar
        def _(act):
            act.sem_inc(hidden.handle, 2)
            act.preload_act_table(ACT.Silu if l else ACT.Relu)
            act.wait_ge(table_ready, 1)

            def activate(s, k, u):
                act.wait_ge(first.handle, first.after(s))
                act.wait_ge(second.handle, second.after(s - 2))
                src = Bp[u][:, :, :, :].rearrange("p j t s -> p (j t) s")
                if l == 0:
                    act.activation(hid[u][:, :, :], src, ACT.Relu).then_inc(hidden.handle, 1)
                else:
                    e = act.value_load(tile_e[0:1, bass.ds(s, 1)], min_val=0, max_val=E - 1)
                    for f in range(FC):
                        ins = act.activation(hid[u][:, f, :], src[:, f, :], ACT.Silu,
                                             bias=b1[:, bass.ds(e, 1), f:f + 1].rearrange("p o f -> p (o f)"))
                    ins.then_inc(hidden.handle, 1)

            with act.Fori(0, slots // 2) as k:
                for u in range(2):
                    activate(k * 2 + u, k, u)

        @block.tensor
        def _(pe):
            for s in (xt_T, first, second):
                pe.sem_inc(s.handle, 2)
            pe.wait_ge(table_ready, 1)

            def turn_x(s, k, u):
                pe.wait_ge(xt_in[u], xt_in.of(k))
                pe.wait_ge(xtT_ready.handle, xtT_ready.after(s - 2))
                for t in range(NT):
                    ins = pe.transpose((M0, M1)[u][:, t * P:(t + 1) * P], xt[u][:, t, :], ident[:, :])
                ins.then_inc(xt_T.handle, 1)

            def to_hidden(s, k, u):
                pe.wait_ge(w1_staged.handle, w1_staged.after(s))
                pe.wait_ge(xtT_ready.handle, xtT_ready.after(s))
                pe.wait_ge(hidden.handle, hidden.after(s - 2))
                dst = Bp[u][:, :, :, :].rearrange("p j t s -> p (j t) s")
                for f in range(FC):
                    ins = pe.matmul(dst[:, f, :], w1s[u][:, f * P:(f + 1) * P], xtT[u][:, :], start=True, stop=True)
                ins.then_inc(first.handle, 1)

            def from_hidden(s, k, u):
                e = pe.value_load(tile_e[0:1, bass.ds(s, 1)], min_val=0, max_val=E - 1)
                pe.wait_ge(hidden.handle, hidden.after(s))
                pe.wait_ge(y_done.handle, y_done.after(s - 2))
                for t in range(NT):
                    for f in range(FC):
                        ins = pe.matmul(A[u][:, t, 0:D], hid[u][:, f, t * P:(t + 1) * P],
                                        w2[:, bass.ds(e, 1), f, :].rearrange("p o d -> p (o d)"),
                                        start=(f == 0), stop=(l == 0 and f == FC - 1))
                    if l:
                        ins = pe.matmul(A[u][:, t, 0:D], ones_row[:, :], b2[:, bass.ds(e, 1), :].rearrange("p o d -> p (o d)"),
                                        start=False, stop=True)
                ins.then_inc(second.handle, 1)

            with pe.Fori(0, slots // 2) as k:
                for u in range(2):
                    turn_x(k * 2 + u, k, u)
                for u in range(2):
                    to_hidden(k * 2 + u, k, u)
                for u in range(2):
                    from_hidden(k * 2 + u, k, u)


def combine(nc, g):
    X, Y, X1, yslot, wtok, gb_row, gslot, expert_out, mod_rows, x_view, out = (g[n] for n in
        "X Y X1 yslot wtok gb_row gslot expert_out mod_rows x_view out".split())

    def sem(name):
        return nc.alloc_semaphore(f"out_{name}")

    x_in, y_in, stored = (Transfers([sem(f"{n}{u}") for u in range(2)], dmas)
                          for n, dmas in (("x_in", 2), ("y_in", NT), ("stored", 1)))
    y_in.begun = 0
    gslot_ready, summed = Signal(sem("gslot_ready"), 1), Signal(sem("summed"), 1)
    dve_order, pool_order = sem("dve_order"), sem("pool_order")

    with nc.Block() as block:

        @block.sync
        def _(sp):
            for t in (x_in, stored):
                t.start(sp)

            def load(b, k, u):
                sp.wait_ge(summed.handle, summed.after(b - 2))
                sp.dma_start(X[u][:, :, :], x_view[3][bass.ds(b, 1)].rearrange("o p t d -> (o p) t d")).then_inc(x_in[u], 16)
                sp.dma_start(gb_row[u][:, :, :], mod_rows[1][bass.ds(b, 1), GB * D:(GB + 1) * D]
                             .rearrange("o (j d) -> o j d", j=1).broadcast_to([P, 1, D])).then_inc(x_in[u], 16)

            def store(b, k, u):
                sp.wait_ge(summed.handle, summed.after(b))
                sp.dma_start(out[bass.ds(b, 1)].rearrange("o (t p) d -> p (o t) d", p=P), X1[u][:, :, :]).then_inc(stored[u], 16)

            with sp.Fori(0, B // 2) as k:
                for u in range(2):
                    load(k * 2 + u, k, u)
                for u in range(2):
                    store(k * 2 + u, k, u)
            for u in range(2):
                sp.wait_ge(stored[u], stored.of(B // 2 - 1))

        @block.gpsimd
        def _(pool):
            ch = Chain(pool, pool_order)
            with pool.Fori(0, B // 2) as k:
                for u in range(2):
                    b = k * 2 + u
                    pool.wait_ge(gslot_ready.handle, gslot_ready.after(b))
                    pool.wait_ge(summed.handle, summed.after(b - 2))
                    ch.apart()
                    for t in range(NT):
                        pool.indirect_dma_start(Y[u][:, 0, t, :], None, expert_out[1],
                                                bass.IndirectOffsetOnAxis(ap=gslot[u][:, 0, t:t + 1], axis=0))\
                            .then_inc(y_in[u], 16)

        @block.vector
        def _(dve):
            ch = Chain(dve, dve_order)
            for s in (gslot_ready, summed):
                dve.sem_inc(s.handle, 2)
            ch.before()
            with dve.Fori(0, B // 2) as k:
                ch.loop(k, 2 * 3)
                for u in range(2):
                    b = k * 2 + u
                    dve.tensor_scalar(gslot[u][:, 0, :], yslot[:, bass.ds(b, 1), 0, :].rearrange("p o t -> p (o t)"), 1.0, None, ALU.mult)\
                        .then_inc(gslot_ready.handle, 1)
                for u in range(2):
                    b = k * 2 + u
                    dve.wait_ge(y_in[u], y_in.of(k))
                    dve.wait_ge(x_in[u], x_in.of(k))
                    dve.wait_ge(stored[u], stored.of(k - 1))
                    for t in range(NT):
                        ch.mark(dve.tensor_scalar(Y[u][:, 1, t, :], Y[u][:, 0, t, :],
                                                  wtok[:, bass.ds(b, 1), 0, t:t + 1].rearrange("p o t -> p (o t)"), None, ALU.mult))
                    ch.settle()
                    ch.link(dve.tensor_tensor(Y[u][:, 0, :, :], Y[u][:, 1, :, :],
                                              gb_row[u][:, :, :].broadcast_to([P, NT, D]), ALU.mult))
                    dve.tensor_tensor(X1[u][:, :, :], X[u][:, :, :], Y[u][:, 0, :, :], ALU.add).then_inc(summed.handle, 1)
                assert ch.n == ch.per


def inputs_of(x):
    import numpy as np

    def bits(x):
        return (np.ascontiguousarray(x, np.float32).view(np.uint32) >> 16).astype(np.uint16)

    n = {k: np.asarray(v) for k, v in x.items()}
    r, c = np.arange(P)[:, None], np.arange(P)[None, :]
    half, d, h8 = np.meshgrid(np.arange(2), np.arange(HD), np.arange(HH), indexing="ij")
    stacked = (16 * h8 + 8 * half + d).reshape(-1)
    half, h8, d = np.meshgrid(np.arange(2), np.arange(HH), np.arange(HD), indexing="ij")
    by_head = (16 * h8 + 8 * half + d).reshape(-1)
    wqkv, bqkv = n["L0_attn_W_qkv"], n["L0_attn_b_qkv"]
    slope = 2.0 ** -np.arange(HH)
    pos = np.arange(S)
    rows = np.zeros((4, H, 2, S))
    sign = np.where(pos < P, 1.0, -1.0)
    rows[0, :, 0] = np.tile(slope, 2)[:, None] * (sign * pos)[None]
    rows[1, :, 0] = -np.tile(slope, 2)[:, None] * sign[None]
    rows[0, :, 1] = 1.0
    rows[1, :, 1] = pos
    rows[2:, :, 1] = 1.0
    rows1 = rows.copy()
    rows1[:2, :, 0] = 0.0
    f = np.float32
    slots = SLOTS[0]
    return {
        "x": n["L0_attn_x"],
        "ident": np.eye(P, dtype=f), "ident_b": bits(np.eye(P)),
        "slope_ident": bits(np.eye(P)[:, None, :] * slope[None, :, None]),
        "dist": bits(np.stack([-2.0 * np.maximum(r - c, 0), -2.0 * np.maximum(c - r, 0)], 1)),
        "before_tri": bits(r < c), "ones_b": bits(np.ones((P, P))),
        "rev_iota": np.broadcast_to(E - np.arange(E, dtype=f), (P, 2, E)).copy(),
        "region_row": np.broadcast_to(np.arange(E, dtype=f) * REGION, (P, E)).copy(),
        "tile_iota": np.broadcast_to(np.arange(slots, dtype=f)[None, :, None], (P, slots, E)).copy(),
        "stack_rows0": bits(rows), "stack_rows1": bits(rows1),
        "wq": np.stack([wqkv[0:D].T[:, stacked], n["L1_attn_wq"][:, stacked]], 1),
        "wk": np.stack([wqkv[D:2 * D].T[:, stacked], n["L1_attn_wk"][:, stacked]], 1),
        "wv": np.stack([wqkv[2 * D:].T[:, by_head], n["L1_attn_wv"][:, by_head]], 1),
        "wo": n["L0_attn_W_out"].T[by_head],
        "qk_bias": np.stack([bqkv[0:D][stacked], bqkv[D:2 * D][stacked]], 1),
        "q_scale": np.stack([np.where(np.arange(D) < 64, HD ** -0.5, (2.0 / HD) ** 0.5), np.full(D, D ** -0.5)], 1).astype(f),
        "vo_bias": np.stack([bqkv[2 * D:][by_head], n["L0_attn_b_out"]], 1),
        "ln_cols": np.stack([n["L1_attn_ln_scale"], n["L1_attn_ln_bias"], n["L1_ffn_rms_w"]], 1),
        "ln_rows": np.stack([n["L1_attn_ln_scale"], n["L1_attn_ln_bias"]])[None],
        "gate_w": np.stack([n["L0_ffn_Wr"], n["L1_ffn_gate_w"].T], 1),
        "cT": np.stack([n["L0_c"].T, n["L1_c"].T], 1),
        "wmod0": n["L0_wmod"], "wmod1": n["L1_wmod"],
        "w1_0": n["L0_ffn_W1"].transpose(1, 0, 2), "w1_1": n["L1_ffn_W1"].transpose(1, 0, 2),
        "w2_0": n["L0_ffn_W2"].reshape(E, FC, P, D).transpose(2, 0, 1, 3),
        "w2_1": n["L1_ffn_W2"].reshape(E, FC, P, D).transpose(2, 0, 1, 3),
        "b1": n["L1_ffn_b1"].reshape(E, FC, P).transpose(2, 0, 1),
        "b2": n["L1_ffn_b2"][None],
    }


def kernel(**inputs):
    import numpy as np
    import concourse.bacc as bacc
    from concourse.bass_utils import run_bass_kernel_spmd as launch

    nc = bacc.Bacc("TRN2", target_bir_lowering=False, num_devices=1)
    arrays = {f"in_{k}": np.ascontiguousarray(v) for k, v in inputs_of(inputs).items()}
    aps = {k[3:]: nc.dram_tensor(k, v.shape, mybir.dt.from_np(v.dtype), kind="ExternalInput").ap()
           for k, v in arrays.items()}
    out = nc.dram_tensor("out_0", (B, S, D), F32, kind="ExternalOutput").ap()
    build(nc, aps, out)
    return launch(nc, [arrays], core_ids=[0]).results[0]["out_0"]
```

```python
from contextlib import ExitStack

import concourse.bass as bass
from concourse import mybir

F32 = mybir.dt.float32
BF16 = mybir.dt.bfloat16
I32 = mybir.dt.int32
ACT = mybir.ActivationFunctionType
ALU = mybir.AluOpType
AX = mybir.AxisListType

P = 128
B, S, D = 32, 256, 128
NT = S // P
H, HD = 16, 8
HH = H // 2
E, F = 8, 512
FC = F // P
VW = 32
TOK = 256
TAIL = E
PADS = E + TAIL
TOKEN, REV, W0, W1 = range(D, D + 4)
W = D + 4
REGION = B * S + TOK
SLOTS = {0: (2 * B * S + E * (TOK - 1)) // TOK, 1: (B * S + E * (TOK - 1)) // TOK}
SLOTS = {l: n + n % 2 for l, n in SLOTS.items()}
CHOICES = {0: 2, 1: 1}
PRODUCTS = [(0, 0), (0, 1), (0, 2), (1, 0), (1, 1), (2, 0)]
LIN = HD * len(PRODUCTS)
MROW = P - 2
SA, CA, GA, SB, CB, GB = range(6)
BIG = 3.0e38
LG, PS = S + P, S + P + NT * E
EPS = 1e-5
EPS_IN = 1e-6
DVE_MARKS = (36, 42)
MIDST = (2, 4, 5, 7, 8, 10, 11, 13, 14)
EXP_SCALE = {0: (1.0, 2.0 ** -0.5), 1: (1.0, 1.0)}


class Signal:

    def __init__(self, handle, per):
        self.handle, self.per = handle, per

    def after(self, b, n=None):
        return 2 * self.per + b * self.per + (self.per if n is None else n)


class Transfers:

    def __init__(self, handles, dmas, begun=1):
        self.handles, self.step, self.begun = handles, 16 * dmas, begun

    def __getitem__(self, u):
        return self.handles[u]

    def start(self, eng):
        for h in self.handles:
            for x in h if isinstance(h, list) else [h]:
                eng.sem_inc(x, self.step * self.begun)

    def of(self, k):
        return self.step * (k + 1 + self.begun)


class Chain:

    def __init__(self, eng, handle):
        self.eng, self.handle, self.base, self.n = eng, handle, 0, 0
        self.meanwhile = None

    def link(self, ins):
        self.mark(ins)
        self.settle()

    def mark(self, ins):
        ins.then_inc(self.handle, 1)
        self.n += 1

    def settle(self):
        if self.meanwhile:
            work, self.meanwhile = self.meanwhile, None
            work()
        self.eng.wait_ge(self.handle, self.base + self.n)

    def settle_apart(self):
        self.settle()
        self.apart()

    def apart(self):
        self.eng.sem_inc(self.handle, 1)
        self.n += 1

    def loop(self, i, per):
        self.base, self.n, self.entry, self.per = self.n_before + i * per, 0, self.n_before, per

    def before(self):
        self.n_before = self.base + self.n

    def done(self, times):
        assert self.n == self.per, (self.n, self.per)
        self.base, self.n = self.entry + times * self.per, 0


def build(nc, a, out):
    with ExitStack() as ctx:
        def sb(name, shape, dt=F32):
            return ctx.enter_context(nc.sbuf_tensor(name, shape, dt))

        def sem(name):
            return ctx.enter_context(nc.semaphore(name))

        def dram(name, shape, dt=F32):
            return nc.dram_tensor(name, shape, dt, kind="Internal").ap()

        mod_rows = [dram(f"mod_rows{l}", (B, 6 * D)) for l in range(2)]
        x_mid = [dram(f"x_mid{n}", (B * S, D)) for n in range(3)]
        gathered = [dram(f"gathered{l}", (E * REGION + TAIL * TOK, W)) for l in range(2)]
        expert_out = [dram(f"expert_out{l}", (CHOICES[l] * B * S + PADS * TOK, D)) for l in range(2)]

        ident = sb("ident", [P, P])
        ident_b = sb("ident_b", [P, P], BF16)
        slope_ident = sb("slope_ident", [P, HH, P], BF16)
        dist = sb("dist", [P, 2, P], BF16)
        before_tri = sb("before_tri", [P, P], BF16)
        ones_b = sb("ones_b", [P, P], BF16)
        ones_row = sb("ones_row", [1, P])
        ones_col = sb("ones_col", [P, 1, 1])
        rev_iota = sb("rev_iota", [P, 2, E])
        region_row = sb("region_row", [P, E])
        tile_iota = sb("tile_iota", [P, SLOTS[0], E + 1])
        token_ids = sb("token_ids", [P, B, NT])
        wq, wk, wv = (sb(n, [P, 2, P]) for n in ("wq", "wk", "wv"))
        wo = sb("wo", [P, P])
        qk_bias = sb("qk_bias", [P, 2])
        q_scale = sb("q_scale", [P, 2])
        qs_bias = sb("qs_bias", [P, 1])
        vo_bias = sb("vo_bias", [P, 2])
        out_bias = sb("out_bias", [P, 1])
        ln_cols = sb("ln_cols", [P, 3])
        gate_w = sb("gate_w", [P, 2, E])
        cT = sb("cT", [P, 2, B])
        silu = sb("silu", [P, 2, B])
        wmod = sb("wmod", [P, 2, 6 * D])
        modT = [sb(f"modT{l}", [P, 6, B]) for l in range(2)]
        gob = sb("gob", [P, B])
        mod_sb = sb("mod_sb", [B, 6 * D])
        w1 = sb("w1", [P, E, F])
        w2 = sb("w2", [P, E, FC, D])
        b1 = sb("b1", [P, E, FC])
        b2 = sb("b2", [1, E, D])

        X = [sb(f"X{u}", [P, NT, D]) for u in range(2)]
        XR = [sb(f"XR{u}", [P, NT, D]) for u in range(2)]
        X1 = [sb(f"X1{u}", [P, NT, D]) for u in range(2)]
        st = sb("st", [P, NT, 6])
        mv = [sb(f"mv{u}", [P, NT, 2]) for u in range(2)]
        rs = [sb(f"rs{u}", [P, NT]) for u in range(2)]
        xn = [sb(f"xn{u}", [P, NT, D]) for u in range(2)]
        hT = [sb(f"hT{u}", [P, S]) for u in range(2)]
        qk = sb("qk", [P, 2, S])
        rem = sb("rem", [P, 2, S])
        parts = [sb(f"parts{u}", [P, 2, 3, S], BF16) for u in range(2)]
        stack = [sb(f"stack{u}", [P, H, 2, S], BF16) for u in range(2)]
        vals = [sb(f"vals{u}", [P, NT, H, VW]) for u in range(2)]
        mx = [sb(f"mx{u}", [P, H, NT]) for u in range(2)]
        mneg = sb("mneg", [P, 2, NT, 2, HH], BF16)
        mrow = [sb(f"mrow{u}", [2 * HH, S], BF16) for u in range(2)]
        probs = [sb(f"probs{n}", [P, 2, NT, S]) for n in range(4)]
        heads = [sb(f"heads{n}", [P, S]) for n in range(2)]
        rsum = sb("rsum", [P, NT, 4])
        On = [sb(f"On{u}", [P, NT, H, HD]) for u in range(2)]
        OnT = sb("OnT", [P, S])
        yT = sb("yT", [P, S])
        st2 = sb("st2", [P, NT, 6])
        mv2 = sb("mv2", [P, NT, 2])
        rs2 = sb("rs2", [P, NT])
        xn2 = sb("xn2", [P, NT, D])
        front_rows = [sb(f"front_rows{u}", [P, 3, D]) for u in range(2)]
        back_rows = [sb(f"back_rows{u}", [P, 3, D]) for u in range(2)]
        xh = [sb(f"xh{u}", [P, NT, D]) for u in range(2)]
        gb_row = [sb(f"gb_row{u}", [P, 1, D]) for u in range(2)]
        lnrow = sb("lnrow", [P, 2, D])
        h2 = [sb(f"h2{u}", [P, NT, W]) for u in range(2)]
        h3 = [sb(f"h3{u}", [P, NT, W]) for u in range(2)]
        h2T = sb("h2T", [P, S])
        eps_col = sb("eps_col", [P, 2])
        lg = sb("lg", [P, NT, E])
        rt = sb("rt", [P, 8, NT, E])
        r1 = sb("r1", [P, 16, NT])
        sel = sb("sel", [P, NT, E], BF16)
        slot_in = [sb(f"slot_in{u}", [P, 2, NT], I32) for u in range(2)]
        run = sb("run", [P, E])
        run_i = sb("run_i", [P, E], I32)
        cnt_i = sb("cnt_i", [P, E], I32)
        n_tiles = sb("n_tiles", [P, E])
        tile_base = sb("tile_base", [P, E + 1])
        reached = sb("reached", [P, SLOTS[0], E + 1])
        tile_tab = sb("tile_tab", [P, 4, SLOTS[0]])
        tile_e = sb("tile_e", [P, SLOTS[0]], I32)
        tile_row = sb("tile_row", [P, SLOTS[0]], I32)
        tile_rev = sb("tile_rev", [P, SLOTS[0]])
        first_choice = [sb(f"first_choice{u}", [P, 2, NT]) for u in range(2)]
        row_weight = [sb(f"row_weight{u}", [P, 2, NT]) for u in range(2)]
        row_dest = [sb(f"row_dest{u}", [P, NT], I32) for u in range(2)]
        w1s = [sb(f"w1s{u}", [P, F]) for u in range(2)]
        w2s = [sb(f"w2s{u}", [P, FC, D]) for u in range(2)]
        b2s = [sb(f"b2s{u}", [1, D]) for u in range(2)]
        row_end = [sb(f"row_end{u}", [P, NT, W - D]) for u in range(2)]
        xt = [sb(f"xt{u}", [P, NT, W]) for u in range(2)]
        xtT = [sb(f"xtT{u}", [P, TOK]) for u in range(2)]
        hid = [sb(f"hid{u}", [P, FC, TOK]) for u in range(2)]
        yt = [sb(f"yt{u}", [P, NT, D]) for u in range(2)]
        Y = [sb(f"Y{u}", [P, 2, NT, D]) for u in range(2)]

        A = [ctx.enter_context(nc.psum_tensor(f"A{n}", [P, NT, S], F32)) for n in range(2)]
        Bp = [ctx.enter_context(nc.psum_tensor(f"B{n}", [P, 2, NT, S], F32)) for n in range(2)]
        M0 = ctx.enter_context(nc.psum_tensor("M0", [P, 512], F32))
        M1 = ctx.enter_context(nc.psum_tensor("M1", [P, 512], F32))
        M0b = M0[:, :].bitcast(BF16)

        x_view = [a["x"].rearrange("b (t p) d -> b p t d", p=P)] + [
            m.rearrange("(b t p) d -> b p t d", t=NT, p=P) for m in x_mid]

        loads = [
            (ident[:, :], a["ident"]), (ident_b[:, :], a["ident_b"].bitcast(BF16)), (slope_ident[:, :, :], a["slope_ident"].bitcast(BF16)),
            (dist[:, :, :], a["dist"].bitcast(BF16)), (before_tri[:, :], a["before_tri"].bitcast(BF16)), (ones_b[:, :], a["ones_b"].bitcast(BF16)),
            (rev_iota[:, :, :], a["rev_iota"]), (region_row[:, :], a["region_row"]),
            (tile_iota[:, :, :], a["tile_iota"]),
            (token_ids[:, :, :], a["token_ids"]),
            (wq[:, :, :], a["wq"]), (wk[:, :, :], a["wk"]), (wv[:, :, :], a["wv"]), (wo[:, :], a["wo"]),
            (qk_bias[:, :], a["qk_bias"]), (q_scale[:, :], a["q_scale"]), (vo_bias[:, :], a["vo_bias"]),
            (ln_cols[:, :], a["ln_cols"]), (lnrow[:, :, :], a["ln_rows"].broadcast_to([P, 2, D])), (gate_w[:, :, :], a["gate_w"]), (cT[:, :, :], a["cT"]),
            (wmod[:, 0, :], a["wmod0"]), (wmod[:, 1, :], a["wmod1"]),
        ]
        stack_rows = [(stack[u][first:first + 2, :, :, :], a["stack_rows0"][n:n + 2].bitcast(BF16))
                      for u in range(2) for n, first in ((0, LIN), (2, MROW))]
        loaded, ready, modp, moded, mod_out = (sem(n) for n in
            ("setup_loaded", "setup_ready", "setup_products", "setup_modulation", "mod_rows_written"))
        stack_zero, stack_loaded = sem("setup_stack_zeroed"), sem("setup_stack_loaded")
        set_act, set_dve = sem("setup_act_order"), sem("setup_dve_order")

        with nc.Block() as block:
            @block.sync
            def _(sp):
                for dst, src in loads:
                    sp.dma_start(dst, src).then_inc(loaded, 16)
                sp.wait_ge(stack_zero, 2)
                for dst, src in stack_rows:
                    sp.dma_start(dst, src).then_inc(stack_loaded, 16)
                for l in range(2):
                    sp.wait_ge(moded, 8 * (l + 1))
                    sp.dma_start(mod_rows[l], mod_sb[:, :]).then_inc(mod_out, 16)
                    sp.wait_ge(mod_out, 16 * (l + 1))
                sp.wait_ge(stack_loaded, 16 * len(stack_rows))

            @block.scalar
            def _(act):
                act.wait_ge(loaded, 16 * len(loads))
                act.activation(silu[:, :, :], cT[:, :, :], ACT.Exp, scale=-1.0).then_inc(set_act, 1)

            @block.tensor
            def _(pe):
                pe.wait_ge(ready, 1)
                for l in range(2):
                    if l:
                        pe.wait_ge(moded, 8)
                    for j in range(6):
                        pe.matmul(M0[:, j * B:(j + 1) * B], wmod[:, l, j * D:(j + 1) * D], silu[:, l, :],
                                  start=True, stop=True)
                    pe.matmul(A[0][0:B, :, :].rearrange("p t s -> p (t s)"), silu[:, l, :], wmod[:, l, 0:512],
                              start=True, stop=True)
                    pe.matmul(A[1][0:B, 0, :], silu[:, l, :], wmod[:, l, 512:768], start=True, stop=True)\
                        .then_inc(modp, 1)
                pe.matmul(M1[:, 0:1], wo[:, :], vo_bias[:, 0:1], start=True, stop=True).then_inc(modp, 1)

            @block.vector
            def _(dve):
                ch = Chain(dve, set_dve)
                for u in range(2):
                    dve.memset(stack[u][:, :, :, :], 0.0).then_inc(stack_zero, 1)
                for u in range(2):
                    dve.memset(vals[u][:, :, :, :], 0.0).then_inc(set_dve, 1)
                dve.wait_ge(set_dve, 2)
                ch.n = 2
                for u in range(2):
                    ch.mark(dve.memset(vals[u][:, :, :, HD:HD + 1], 1.0))
                ch.mark(dve.memset(ones_row[:, :], 1.0))
                ch.mark(dve.memset(eps_col[:, 0:1], EPS))
                ch.mark(dve.memset(eps_col[:, 1:2], EPS_IN))
                ch.mark(dve.memset(ones_col[:, :, :], 1.0))
                for u in range(2):
                    ch.mark(dve.memset(h3[u][:, :, :], 0.0))
                dve.wait_ge(loaded, 16 * len(loads))
                ch.mark(dve.tensor_copy(run[:, :], region_row[:, :]))
                ch.mark(dve.tensor_tensor(qs_bias[:, :], qk_bias[:, 0:1], q_scale[:, 0:1], ALU.mult))
                dve.wait_ge(set_act, 1)
                ch.link(dve.tensor_scalar(silu[:, :, :], silu[:, :, :], 1.0, None, ALU.add))
                ch.link(dve.reciprocal(silu[:, :, :], silu[:, :, :]))
                dve.tensor_tensor(silu[:, :, :], silu[:, :, :], cT[:, :, :], ALU.mult).then_inc(ready, 1)
                for l in range(2):
                    dve.wait_ge(modp, l + 1)
                    if l:
                        dve.wait_ge(mod_out, 16)
                    m = modT[l]
                    am = A[0][0:B, :, :].rearrange("p t s -> p (t s)")
                    ch.mark(dve.tensor_copy(m[:, :, :].rearrange("p j b -> p (j b)"), M0[:, 0:6 * B]))
                    ch.mark(dve.tensor_copy(mod_sb[:, 0:512], am))
                    ch.link(dve.tensor_copy(mod_sb[:, 512:768], A[1][0:B, 0, :]))
                    n = 0
                    for j in (CA, CB):
                        dve.tensor_scalar(m[:, j, :], m[:, j, :], 1.0, None, ALU.add).then_inc(moded, 1)
                        dve.tensor_scalar(mod_sb[:, j * D:(j + 1) * D], mod_sb[:, j * D:(j + 1) * D], 1.0, None,
                                          ALU.add).then_inc(moded, 1)
                    for j in (GA, GB):
                        for g, t in ((m[:, j, :], qk[:, 0, 0:B]), (mod_sb[:, j * D:(j + 1) * D], qk[0:B, 1, 0:D])):
                            ch.link(dve.tensor_scalar(t, g, 0.0, 2.0, ALU.is_ge, ALU.mult))
                            ch.link(dve.tensor_scalar(t, t, -1.0, None, ALU.add))
                            ch.link(dve.scalar_tensor_tensor(out=g, in0=g, scalar=-1.0, in1=g, op0=ALU.mult, op1=ALU.max))
                            dve.scalar_tensor_tensor(out=g, in0=g, scalar=0.25, in1=t, op0=ALU.max, op1=ALU.mult)\
                                .then_inc(moded, 1)
                dve.wait_ge(modp, 3)
                ch.link(dve.tensor_tensor(out_bias[:, :], M1[:, 0:1], vo_bias[:, 1:2], ALU.add))
                dve.wait_ge(moded, 16)
                ch.link(dve.tensor_scalar(gob[:, :], modT[0][:, GA, :], out_bias[:, 0:1], None, ALU.mult))

        for layer in range(2):
            with nc.cleanup_on_exit():
                attention(nc, layer, locals())
            with nc.cleanup_on_exit():
                experts(nc, layer, locals())
        with nc.cleanup_on_exit():
            combine(nc, locals())


DEPTH = 3


def run_ticks(eng, tick, ch=None, per=0):
    def peeled(i):
        return lambda off: (i + off, (i + off) // 2, (i + off) % 2) if 0 <= i + off < B else None

    for i in range(-DEPTH, DEPTH):
        tick(peeled(i))
    pairs = (B - 2 * DEPTH) // 2
    if ch:
        ch.before()
    with eng.Fori(0, pairs) as k:
        if ch:
            ch.loop(k, 2 * per)
        for i in (DEPTH, DEPTH + 1):
            tick(lambda off: (k * 2 + (i + off), k + (i + off) // 2, (i + off) % 2))
        if ch:
            assert ch.n == 2 * per, ch.n
    if ch:
        ch.done(pairs)
    for i in range(DEPTH + 2 * pairs, B + DEPTH):
        tick(peeled(i))


def attention(nc, l, g):
    (X, XR, X1, st, mv, rs, xn, hT, qk, rem, parts, stack, vals, mx, mneg, mrow, probs, heads, rsum, On, OnT, yT,
     st2, mv2, rs2, xn2, front_rows, back_rows, xh, qs_bias, h2, h3, h2T, eps_col, lg, rt, r1, sel, slot_in, token_ids, run) = (g[n] for n in (
        "X XR X1 st mv rs xn hT qk rem parts stack vals mx mneg mrow probs heads rsum On OnT yT "
        "st2 mv2 rs2 xn2 front_rows back_rows xh qs_bias h2 h3 h2T eps_col lg rt r1 sel slot_in token_ids run").split())
    A, Bp, M0, M1, M0b, ident, ident_b, slope_ident, dist = (g[n] for n in
        "A Bp M0 M1 M0b ident ident_b slope_ident dist".split())
    wq, wk, wv, wo, qk_bias, q_scale, modT, gob, gate_w, ln_cols = (g[n] for n in
        "wq wk wv wo qk_bias q_scale modT gob gate_w ln_cols".split())
    before_tri, ones_b, rev_iota, mod_rows, gathered, x_view, region_row = (g[n] for n in
        "before_tri ones_b rev_iota mod_rows gathered x_view region_row".split())
    gb_row, ones_col, lnrow, Y, expert_out, XR, a, w1, w2, b1, b2 = (g[n] for n in
        "gb_row ones_col lnrow Y expert_out XR a w1 w2 b1 b2".split())
    n_choice = CHOICES[l]
    mod = modT[l]

    def sem(name):
        return nc.alloc_semaphore(f"L{l}_{name}")

    def signal(name, per):
        return Signal(sem(name), per)

    def signals(*names, per=1):
        return [signal(n, per) for n in names]

    weights_in, lin_in = sem("weights_in"), sem("lin_in")

    def transfers(name, dmas, begun=1):
        return Transfers([sem(f"{name}{u}") for u in range(2)], dmas, begun)

    x_in = transfers("x_in", 1)
    front_in = transfers("front_in", 4)
    back_in = transfers("back_in", 2)
    base_out = transfers("base_out", 1)
    stack_in = Transfers([[sem(f"stack_in{u}{h}") for h in range(2)] for u in range(2)], len(PRODUCTS))
    m_in = Transfers([[sem(f"m_in{u}{h}") for h in range(2)] for u in range(2)], 1)
    x1_out = transfers("x1_out", 1)
    scat_out = transfers("rows_out", NT * n_choice, 0)
    y_view = expert_out[0][0:2 * B * S, :].rearrange("(c b t p) d -> c b p t d", c=2, b=B, p=P)

    stats, xn_ready, qk_f32, x1_ready, stats2, xn2_ready, logits_read, slots_ready, pos_read = signals(
        "stats", "xn_ready", "qk_f32", "x1_ready", "stats2", "xn2_ready", "logits_read", "slots_ready", "pos_read")
    sel_ready, w_den = signals("sel_ready", "w_den")
    a_max, o_norm, m_split = signal("a_max", H), signal("o_norm", 4), signal("m_split", 2)
    rsqrt, h_ready, v_ready, onT_read, y_read, rsqrt2, h2T_read, w_exp = signals(
        "rsqrt", "h_ready", "v_ready", "onT_read", "y_read", "rsqrt2", "h2T_read", "w_exp")
    mT_read, b_exp, o_read = signal("mT_read", 2), signal("b_exp", HH), signal("o_read", 4)
    xn_T, qk_proj, v_proj, on_T, y_proj, y_T, h2_T, logits, pos = signals(
        "xn_T", "qk_proj", "v_proj", "on_T", "y_proj", "y_T", "h2_T", "logits", "pos")
    a_scores, m_T, b_scores, pv, o_T = (signal("a_scores", H), signal("m_T", 2), signal("b_scores", HH),
                                        signal("pv", 4), signal("o_T", 4))
    split, h2_ready, scattered = signals("split", "h2_ready", "scattered")
    if l == 1:
        h3_ready = signal("h3_ready", 1)
        x2_ready, h_rows, base_ready, h_stats, h_rsqrt, rms_stats, rms_rsqrt = signals(
            "x2_ready", "h_rows", "base_ready", "h_stats", "h_rsqrt", "rms_stats", "rms_rsqrt")
    dve_order, act_order, pool_order = sem("dve_order"), sem("act_order"), sem("pool_order")

    def start(eng, *sigs):
        for s in sigs:
            eng.sem_inc(s.handle, 2 * s.per)

    with nc.Block() as block:

        @block.sync
        def _(sp):
            def rows_of(view, b):
                return view[bass.ds(b, 1)].rearrange("o p t d -> (o p) t d")

            def mod_of(layer, b, first, n):
                return mod_rows[layer][bass.ds(b, 1), first * D:(first + n) * D]\
                    .rearrange("o (j d) -> o j d", j=n).broadcast_to([P, n, D])

            def load_front(b, k, u):
                if l == 0:
                    sp.wait_ge(xn_ready.handle, xn_ready.after(b - 2))
                    sp.dma_start(X[u][:, :, :], rows_of(x_view[0], b)).then_inc(x_in[u], 16)
                else:
                    sp.wait_ge(base_ready.handle, base_ready.after(b - 2))
                    sp.dma_start(X[u][:, :, :], rows_of(x_view[1], b)).then_inc(x_in[u], 16)
                    for c in range(2):
                        sp.dma_start(Y[u][:, c, :, :], rows_of(y_view[c], b)).then_inc(front_in[u], 16)
                    sp.dma_start(front_rows[u][:, :, :], mod_of(1, b, SA, 3)).then_inc(front_in[u], 16)
                    sp.dma_start(gb_row[u][:, :, :], mod_of(0, b, GB, 1)).then_inc(front_in[u], 16)

            def load_back(b, k, u):
                sp.wait_ge(h2_ready.handle, h2_ready.after(b - 2))
                if l == 1:
                    sp.wait_ge(base_out[u], base_out.of(k))
                sp.dma_start(XR[u][:, :, :], rows_of(x_view[2 * l], b)).then_inc(back_in[u], 16)
                sp.dma_start(back_rows[u][:, :, :], mod_of(l, b, GA, 3)).then_inc(back_in[u], 16)

            def store_base(b, k, u):
                sp.wait_ge(base_ready.handle, base_ready.after(b))
                sp.dma_start(rows_of(x_view[2], b), xh[u][:, :, :]).then_inc(base_out[u], 16)

            def stack_up(b, k, u, half):
                if half == 0:
                    sp.wait_ge(split.handle, split.after(b))
                sp.wait_ge(b_scores.handle, b_scores.after(b - 2, 4 * half + 4))
                for r, (pq, pk) in enumerate(PRODUCTS):
                    src = parts[u][:, :, :, :].rearrange("p q r s -> p (q r) s")
                    sp.dma_start(stack[u][HD * r:HD * r + HD, HH * half:HH * half + HH, :, :],
                                 src[64 * half:64 * half + 64, pq:4 + pk:3 + pk - pq, :])\
                        .then_inc(stack_in[u][half], 16)

            def stack_max(b, k, u, half):
                sp.wait_ge(mT_read.handle, mT_read.after(b, half + 1))
                sp.dma_start(stack[u][MROW:MROW + 2, HH * half:HH * half + HH, 0, :], mrow[half][:, :])\
                    .then_inc(m_in[u][half], 16)

            def store_x1(b, k, u):
                sp.wait_ge(x1_ready.handle, x1_ready.after(b))
                sp.dma_start(rows_of(x_view[1 + 2 * l], b), X1[u][:, :, :]).then_inc(x1_out[u], 16)

            weights = [(w1[:, :, :], a[f"w1_{l}"]), (w2[:, :, :, :], a[f"w2_{l}"])]
            if l == 1:
                weights += [(b1[:, :, :], a["b1"]), (b2[:, :, :], a["b2"])]
                for u in range(2):
                    sp.dma_start(stack[u][LIN:LIN + 2, :, :, :], a["stack_rows1"][0:2].bitcast(BF16)).then_inc(lin_in, 16)
                sp.wait_ge(lin_in, 32)
            for t in (x_in, stack_in, m_in, x1_out, front_in, back_in, base_out):
                t.start(sp)

            def tick(at):
                if at(0):
                    stack_up(*at(0), 1)
                if at(-1):
                    stack_max(*at(-1), 1)
                if at(-1):
                    load_back(*at(-1))
                if at(3) and l == 0:
                    load_front(*at(3))
                if at(-2) and l:
                    store_x1(*at(-2))
                if at(1):
                    stack_up(*at(1), 0)
                if at(-2) and l == 0:
                    store_x1(*at(-2))
                if l and at(1):
                    store_base(*at(1))
                if l and at(3):
                    load_front(*at(3))
                if at(0):
                    stack_max(*at(0), 0)

            for dst, src in weights:
                sp.dma_start(dst, src).then_inc(weights_in, 16)
            run_ticks(sp, tick)
            sp.wait_ge(weights_in, 16 * len(weights))
            for u in range(2):
                sp.wait_ge(x1_out[u], x1_out.of(B // 2 - 1))
                if l == 1:
                    sp.wait_ge(base_out[u], base_out.of(B // 2 - 1))

        @block.gpsimd
        def _(pool):
            start(pool, split, h2_ready, scattered, *([base_ready, x2_ready] if l else []))
            ch = Chain(pool, pool_order)

            def split_qk(b, k, u):
                pool.wait_ge(qk_f32.handle, qk_f32.after(b))
                for half in range(2):
                    pool.wait_ge(stack_in[u][half], stack_in.of(k - 1))
                p = parts[u]
                one = ones_col[:, :, :].broadcast_to([P, 2, S])
                ch.link(pool.tensor_tensor(p[:, :, 0, :], qk[:, :, :], one, ALU.mult))
                ch.link(pool.tensor_tensor(rem[:, :, :], qk[:, :, :], p[:, :, 0, :], ALU.subtract))
                ch.link(pool.tensor_tensor(p[:, :, 1, :], rem[:, :, :], one, ALU.mult))
                pool.tensor_tensor(p[:, :, 2, :], rem[:, :, :], p[:, :, 1, :], ALU.subtract).then_inc(split.handle, 1)

            def add_experts(b, k, u):
                pool.wait_ge(x_in[u], x_in.of(k))
                pool.wait_ge(front_in[u], front_in.of(k))
                y = Y[u]
                ch.link(pool.tensor_tensor(y[:, 0, :, :], y[:, 0, :, :], y[:, 1, :, :], ALU.add))
                ch.link(pool.tensor_tensor(y[:, 0, :, :], y[:, 0, :, :], gb_row[u][:, :, :].broadcast_to([P, NT, D]), ALU.mult))
                pool.tensor_tensor(X[u][:, :, :], X[u][:, :, :], y[:, 0, :, :], ALU.add).then_inc(x2_ready.handle, 1)

            def residual_base(b, k, u):
                def row(n, x):
                    return x[:, n:n + 1, :].broadcast_to([P, NT, D])
                pool.wait_ge(xn_ready.handle, xn_ready.after(b))
                pool.wait_ge(base_out[u], base_out.of(k - 1))
                h = xh[u][:, :, :]
                ch.link(pool.tensor_tensor(h, xn[u][:, :, :], row(0, lnrow), ALU.mult))
                ch.link(pool.tensor_tensor(h, h, row(1, lnrow), ALU.add))
                ch.link(pool.tensor_tensor(h, h, row(GA, front_rows[u]), ALU.mult))
                pool.tensor_tensor(h, h, X[u][:, :, :], ALU.add).then_inc(base_ready.handle, 1)

            def modulate(b, k, u):
                pool.wait_ge(xn2_ready.handle, xn2_ready.after(b))
                pool.wait_ge(back_in[u], back_in.of(k))
                pool.wait_ge(scattered.handle, scattered.after(b - 2))
                ch.link(pool.tensor_tensor(h2[u][:, :, 0:D], xn2[:, :, :],
                                           back_rows[u][:, CB - GA:CB - GA + 1, :].broadcast_to([P, NT, D]), ALU.mult))
                pool.tensor_tensor(h2[u][:, :, 0:D], h2[u][:, :, 0:D],
                                   back_rows[u][:, SB - GA:SB - GA + 1, :].broadcast_to([P, NT, D]), ALU.add)\
                    .then_inc(h2_ready.handle, 1)

            def scatter(b, k, u):
                pool.wait_ge(slots_ready.handle, slots_ready.after(b))
                ch.apart()
                for c in range(n_choice):
                    for t in range(NT):
                        pool.indirect_dma_start(gathered[l], bass.IndirectOffsetOnAxis(ap=slot_in[u][:, c, t:t + 1], axis=0),
                                                (h3 if l else h2)[u][:, t, :], None).then_inc(scat_out[u], 16)

            def scatter_done(b, k, u):
                pool.wait_ge(scat_out[u], scat_out.of(k))
                pool.sem_inc(scattered.handle, 1)

            def tick(at):
                if at(1):
                    split_qk(*at(1))
                if l and at(1):
                    residual_base(*at(1))
                if l and at(-2):
                    modulate(*at(-2))
                if at(-2) and l == 0:
                    modulate(*at(-2))
                if at(-3):
                    scatter(*at(-3))
                if l and at(3):
                    add_experts(*at(3))
                if at(-3):
                    scatter_done(*at(-3))

            run_ticks(pool, tick, ch, 10 if l else 5)

        @block.scalar
        def _(act):
            start(act, rsqrt, h_ready, v_ready, onT_read, y_read, rsqrt2, h2T_read, w_exp, mT_read, b_exp, o_read, qk_f32)
            if l == 1:
                start(act, h_rsqrt, rms_rsqrt)
            ch = Chain(act, act_order)
            act.preload_act_table_set("natural_log_exp_and_others")

            def rsqrt_of(b, var, dst, ready, sig, eps=eps_col[:, 0:1]):
                act.wait_ge(ready.handle, ready.after(b))
                ch.link(act.activation(dst, var, ACT.Ln, bias=eps))
                act.activation(dst, dst, ACT.Exp, scale=-0.5).then_inc(sig.handle, 1)

            def first_rsqrt(b, k, u):
                rsqrt_of(b, mv[u][:, :, 1], rs[u][:, :], stats, rsqrt)

            def inner_rsqrt(b, k, u):
                rsqrt_of(b, mv[u][:, :, 1], rs[u][:, :], h_stats, h_rsqrt, eps_col[:, 1:2])

            def second_rsqrt(b, k, u):
                rsqrt_of(b, mv2[:, :, 1], rs2[:, :], stats2, rsqrt2)

            def rms_rsqrt_of(b, k, u):
                rsqrt_of(b, mv2[:, :, 1], rs2[:, :], rms_stats, rms_rsqrt, eps_col[:, 1:2])

            def first_h(b, k, u):
                act.wait_ge(xn_T.handle, xn_T.after(b))
                act.wait_ge(v_proj.handle, v_proj.after(b - 2))
                act.activation(hT[u][:, :], M0[:, 0:S], ACT.Identity,
                               bias=ln_cols[:, 1:2] if l else mod[:, SA, bass.ds(b, 1)],
                               scale=ln_cols[:, 0:1] if l else mod[:, CA, bass.ds(b, 1)]).then_inc(h_ready.handle, 1)

            def read_qk(b, k, u):
                act.wait_ge(qk_proj.handle, qk_proj.after(b))
                act.wait_ge(split.handle, split.after(b - 1))
                m = M0[:, :].rearrange("p (j s) -> p j s", j=2)
                if l:
                    ch.mark(act.activation(qk[:, 0, :], m[:, 0, :], ACT.Identity, scale=q_scale[:, 1:2]))
                    ins = act.activation(qk[:, 1, :], m[:, 1, :], ACT.Copy)
                else:
                    ch.mark(act.activation(qk[:, 0, :], m[:, 0, :], ACT.Identity, bias=qs_bias[:, 0:1],
                                           scale=q_scale[:, 0:1]))
                    ins = act.activation(qk[:, 1, :], m[:, 1, :], ACT.Identity, bias=qk_bias[:, 1:2])
                ins.then_inc(qk_f32.handle, 1)

            def values(b, k, u):
                act.wait_ge(v_proj.handle, v_proj.after(b))
                act.wait_ge(pv.handle, pv.after(b - 2))
                act.activation(vals[u][:, :, :, 0:HD],
                               M0[:, 0:NT * D].rearrange("p (t h d) -> p t h d", t=NT, h=H), ACT.Copy)\
                    .then_inc(v_ready.handle, 1)

            def max_rows(b, k, u, half):
                act.wait_ge(m_T.handle, m_T.after(b, half + 1))
                act.wait_ge(m_in[1 - u][half], m_in.of(k - 1 + u))
                act.activation(mrow[half][:, :], M0b[0:2 * HH, 2 * S:3 * S], ACT.Copy).then_inc(mT_read.handle, 1)

            def exps(b, k, u, c):
                act.wait_ge(b_scores.handle, b_scores.after(b, c + 1))
                g4 = c // 2
                act.wait_ge(pv.handle, pv.after(b, g4 - 1) if g4 >= 2 else pv.after(b - 1, g4 + 3))
                act.activation(probs[c % 4][:, :, :, :], Bp[c % 2][:, :, :, :], ACT.Exp,
                               scale=EXP_SCALE[l][c // 4]).then_inc(b_exp.handle, 1)

            def head_sums(b, k, u, g):
                act.wait_ge(pv.handle, pv.after(b, g + 1))
                act.wait_ge(o_T.handle, o_T.after(b, g - 1) if g >= 2 else o_T.after(b - 1, g + 3))
                act.activation(heads[g % 2][:, :], M1[:, 0:S], ACT.Copy).then_inc(o_read.handle, 1)

            def read_on(b, k, u):
                act.wait_ge(on_T.handle, on_T.after(b))
                act.activation(OnT[:, :], M0[:, 0:S], ACT.Copy).then_inc(onT_read.handle, 1)

            def read_y(b, k, u):
                act.wait_ge(y_proj.handle, y_proj.after(b))
                act.activation(yT[:, :], M0[:, S:2 * S], ACT.Identity, bias=gob[:, bass.ds(b, 1)],
                               scale=mod[:, GA, bass.ds(b, 1)]).then_inc(y_read.handle, 1)

            def second_h(b, k, u):
                act.wait_ge(h2_T.handle, h2_T.after(b))
                if l:
                    act.activation(h2T[:, :], M0[:, 0:S], ACT.Identity, scale=ln_cols[:, 2:3]).then_inc(h2T_read.handle, 1)
                else:
                    act.activation(h2T[:, :], M0[:, 0:S], ACT.Copy).then_inc(h2T_read.handle, 1)

            def weights(b, k, u):
                act.wait_ge(w_den.handle, w_den.after(b))
                if l:
                    act.activation(rt[:, 4, :, :], rt[:, 3, :, :], ACT.Exp).then_inc(w_exp.handle, 1)
                else:
                    act.activation(r1[:, 5, :], r1[:, 4, :], ACT.Exp).then_inc(w_exp.handle, 1)

            def tick(at):
                def chunk(c):
                    if at(-1):
                        exps(*at(-1), c)

                def layer(n, step, off):
                    if l == n and at(off):
                        step(*at(off))

                def step(f, off, *args):
                    if at(off):
                        f(*at(off), *args)

                chunk(0)
                step(head_sums, -2, 3)
                step(second_h, -3)
                layer(0, first_rsqrt, 2)
                chunk(1)
                step(read_qk, 1)
                chunk(2)
                layer(1, first_rsqrt, 2)
                step(max_rows, -1, 1)
                step(head_sums, -1, 0)
                chunk(3)
                step(values, 0)
                layer(1, second_rsqrt, -2)
                layer(0, read_on, -2)
                chunk(4)
                layer(0, read_y, -2)
                step(head_sums, -1, 1)
                chunk(5)
                step(weights, -3)
                layer(0, second_rsqrt, -2)
                chunk(6)
                layer(1, inner_rsqrt, 2)
                layer(1, rms_rsqrt_of, -2)
                step(head_sums, -1, 2)
                step(max_rows, 0, 0)
                chunk(7)
                step(first_h, 2)

            run_ticks(act, tick, ch, 5 if l else 3)

        @block.vector
        def _(dve):
            start(dve, stats, xn_ready, x1_ready, stats2, xn2_ready, logits_read, slots_ready, pos_read,
                  sel_ready, w_den, a_max, o_norm, m_split)
            if l == 1:
                start(dve, h_rows, h_stats, rms_stats, h3_ready)
            ch = Chain(dve, dve_order)
            if l == 1:
                ch.link(dve.tensor_copy(run[:, :], region_row[:, :]))

            def aggregate(st, mv, sig=None):
                ch.settle_apart()
                for t in range(NT):
                    ins = dve.bn_aggr(mv[:, t, :], st[:, t, :])
                    if t < NT - 1 or sig is None:
                        ch.mark(ins)
                ch.settle()
                if sig is not None:
                    ins.then_inc(sig.handle, 1)

            def moments(x, st, mv, sig):
                for t in range(NT):
                    ch.mark(dve.bn_stats(st[:, t, :], x[:, t, :]))
                aggregate(st, mv, sig)

            def normed(x, mv, rs, dst, sig):
                for t in range(NT):
                    ins = dve.tensor_scalar(dst[:, t, :], x[:, t, :], mv[:, t, 0:1], rs[:, t:t + 1],
                                            ALU.subtract, ALU.mult)
                    if t < NT - 1:
                        ch.mark(ins)
                ins.then_inc(sig.handle, 1)
                ch.settle()

            def first_stats(b, k, u):
                dve.wait_ge(x_in[u], x_in.of(k))
                moments(X[u], st, mv[u], stats)

            def first_norm(b, k, u):
                dve.wait_ge(rsqrt.handle, rsqrt.after(b))
                dve.wait_ge(xn_T.handle, xn_T.after(b - 2))
                normed(X[u], mv[u], rs[u], xn[u], xn_ready)

            def added_stats(b, k, u):
                dve.wait_ge(x2_ready.handle, x2_ready.after(b))
                moments(X[u], st, mv[u], stats)

            def outer_norm(b, k, u):
                dve.wait_ge(rsqrt.handle, rsqrt.after(b))
                dve.wait_ge(xn_T.handle, xn_T.after(b - 2))
                dve.wait_ge(base_ready.handle, base_ready.after(b - 2))
                normed(X[u], mv[u], rs[u], xn[u], h_rows)

            def modulate_rows(b, k, u):
                dve.wait_ge(h_rows.handle, h_rows.after(b))
                ch.link(dve.tensor_tensor(xn[u][:, :, :], xn[u][:, :, :],
                                          front_rows[u][:, CA:CA + 1, :].broadcast_to([P, NT, D]), ALU.mult))
                ch.link(dve.tensor_tensor(xn[u][:, :, :], xn[u][:, :, :],
                                          front_rows[u][:, SA:SA + 1, :].broadcast_to([P, NT, D]), ALU.add))

            def inner_stats(b, k, u):
                moments(xn[u], st, mv[u], h_stats)

            def inner_norm(b, k, u):
                dve.wait_ge(h_rsqrt.handle, h_rsqrt.after(b))
                normed(xn[u], mv[u], rs[u], xn[u], xn_ready)

            def row_max(b, k, u, h):
                dve.wait_ge(a_scores.handle, a_scores.after(b, h + 1))
                if h == 0:
                    dve.wait_ge(m_split.handle, m_split.after(b - 2))
                dve.tensor_reduce(mx[u][:, h, :], A[h % 2][:, :, :], AX.X, ALU.max).then_inc(a_max.handle, 1)

            def split_max(b, k, u, half):
                dve.wait_ge(a_max.handle, a_max.after(b, HH * (half + 1)))
                dve.wait_ge(m_T.handle, m_T.after(b - 1, half + 1))
                v = mx[u][:, HH * half:HH * half + HH, :].rearrange("p h t -> p t h")
                ch.link(dve.tensor_scalar(mneg[:, half, :, 0, :], v, -1.0, None, ALU.mult))
                dve.scalar_tensor_tensor(out=mneg[:, half, :, 1, :], in0=v, scalar=-1.0, in1=mneg[:, half, :, 0, :],
                                         op0=ALU.mult, op1=ALU.subtract).then_inc(m_split.handle, 1)

            def normalise(b, k, u, g):
                dve.wait_ge(o_T.handle, o_T.after(b, g + 1))
                if g == 0:
                    if l:
                        dve.wait_ge(x1_ready.handle, x1_ready.after(b - 2))
                    else:
                        dve.wait_ge(on_T.handle, on_T.after(b - 2))
                dve.wait_ge(o_norm.handle, o_norm.after(b, g) if g else o_norm.after(b - 1))
                o = M1[:, S:2 * S].rearrange("p (t j w) -> p t j w", t=NT, j=4)
                ch.link(dve.reciprocal(rsum[:, :, :], o[:, :, :, HD]))
                dst = On[u][:, :, 4 * g:4 * g + 4, :] if l == 0 else \
                    On[u][:, :, :, :].rearrange("p t (h f) d -> p t f h d", f=2)[:, :, g // 2, 4 * (g % 2):4 * (g % 2) + 4, :]
                dve.tensor_tensor(dst, o[:, :, :, 0:HD],
                                  rsum[:, :, :].unsqueeze(3).broadcast_to([P, NT, 4, HD]), ALU.mult)\
                    .then_inc(o_norm.handle, 1)

            def residual(b, k, u):
                dve.wait_ge(back_in[u], back_in.of(k))
                dve.wait_ge(x1_out[u], x1_out.of(k - 1))
                if l:
                    dve.wait_ge(o_norm.handle, o_norm.after(b))
                    ch.link(dve.tensor_tensor(X1[u][:, :, :], On[u][:, :, :, :].rearrange("p t h d -> p t (h d)"),
                                              back_rows[u][:, 0:1, :].broadcast_to([P, NT, D]), ALU.mult))
                    dve.tensor_tensor(X1[u][:, :, :], X1[u][:, :, :], XR[u][:, :, :], ALU.add).then_inc(x1_ready.handle, 1)
                else:
                    dve.wait_ge(y_T.handle, y_T.after(b))
                    dve.tensor_tensor(X1[u][:, :, :], XR[u][:, :, :], M0[:, 0:S].rearrange("p (t d) -> p t d", t=NT),
                                      ALU.add).then_inc(x1_ready.handle, 1)

            def second_stats(b, k, u):
                dve.wait_ge(x1_ready.handle, x1_ready.after(b))
                moments(X1[u], st2, mv2, stats2)

            def second_norm(b, k, u):
                dve.wait_ge(rsqrt2.handle, rsqrt2.after(b))
                dve.wait_ge(h2_ready.handle, h2_ready.after(b - 1))
                normed(X1[u], mv2, rs2, xn2, xn2_ready)

            def rms_moments(b, k, u):
                dve.wait_ge(h2_ready.handle, h2_ready.after(b))
                for t in range(NT):
                    ch.mark(dve.bn_stats(st2[:, t, :], h2[u][:, t, 0:D]))
                aggregate(st2, mv2)
                ch.link(dve.tensor_tensor(mv2[:, :, 0], mv2[:, :, 0], mv2[:, :, 0], ALU.mult))
                dve.tensor_tensor(mv2[:, :, 1], mv2[:, :, 1], mv2[:, :, 0], ALU.add).then_inc(rms_stats.handle, 1)

            def rms_norm(b, k, u):
                dve.wait_ge(rms_rsqrt.handle, rms_rsqrt.after(b))
                dve.wait_ge(scattered.handle, scattered.after(b - 2))
                ch.mark(dve.tensor_scalar(h3[u][:, 0, 0:D], h2[u][:, 0, 0:D], rs2[:, 0:1], None, ALU.mult))
                ch.settle()
                dve.tensor_scalar(h3[u][:, 1, 0:D], h2[u][:, 1, 0:D], rs2[:, 1:2], None, ALU.mult)\
                    .then_inc(h3_ready.handle, 1)

            def first_of(src, top, eq, cand, idx, dst):
                ch.link(dve.tensor_reduce(top, src, AX.X, ALU.max))
                ch.link(dve.tensor_tensor(eq, src, top.unsqueeze(2).broadcast_to([P, NT, E]), ALU.is_equal))
                ch.link(dve.tensor_tensor(cand, eq, rev_iota[:, :, :], ALU.mult))
                ch.link(dve.tensor_reduce(idx, cand, AX.X, ALU.max))
                ch.link(dve.tensor_tensor(dst, rev_iota[:, :, :], idx.unsqueeze(2).broadcast_to([P, NT, E]),
                                          ALU.is_equal))

            def read_logits(b, k, u):
                dve.wait_ge(logits.handle, logits.after(b))
                dve.tensor_copy(lg[:, :, :], M0[:, LG:LG + NT * E].rearrange("p (t e) -> p t e", t=NT))\
                    .then_inc(logits_read.handle, 1)

            def choose_first(b, k, u):
                row = (h3 if l else h2)[u]
                dve.wait_ge(scattered.handle, scattered.after(b - 2))
                ch.mark(dve.tensor_scalar(row[:, :, TOKEN], token_ids[:, bass.ds(b, 1), :].rearrange("p o t -> p (o t)"),
                                          1.0, None, ALU.mult))
                dve.wait_ge(logits_read.handle, logits_read.after(b))
                first_of(lg[:, :, :], r1[:, 0, :], rt[:, 0, :, :], rt[:, 1, :, :], row[:, :, REV], rt[:, 2, :, :])
                if l:
                    dve.wait_ge(pos.handle, pos.after(b - 1))
                    dve.tensor_copy(sel[:, :, :], rt[:, 2, :, :]).then_inc(sel_ready.handle, 1)
                    dve.tensor_tensor(rt[:, 3, :, :], lg[:, :, :], r1[:, 0, :].unsqueeze(2).broadcast_to([P, NT, E]),
                                      ALU.subtract).then_inc(w_den.handle, 1)

            def choose_second(b, k, u):
                ch.link(dve.scalar_tensor_tensor(out=rt[:, 3, :, :], in0=rt[:, 2, :, :], scalar=-BIG, in1=lg[:, :, :],
                                                 op0=ALU.mult, op1=ALU.add))
                first_of(rt[:, 3, :, :], r1[:, 2, :], rt[:, 0, :, :], rt[:, 1, :, :], r1[:, 3, :], rt[:, 4, :, :])
                dve.wait_ge(pos.handle, pos.after(b - 1))
                dve.tensor_tensor(sel[:, :, :], rt[:, 2, :, :], rt[:, 4, :, :], ALU.add).then_inc(sel_ready.handle, 1)
                dve.tensor_tensor(r1[:, 4, :], r1[:, 2, :], r1[:, 0, :], ALU.subtract).then_inc(w_den.handle, 1)

            def weigh_choices(b, k, u):
                row = (h3 if l else h2)[u]
                dve.wait_ge(w_exp.handle, w_exp.after(b))
                if l:
                    ch.link(dve.tensor_reduce(r1[:, 6, :], rt[:, 4, :, :], AX.X, ALU.add))
                    ch.mark(dve.reciprocal(row[:, :, W0], r1[:, 6, :]))
                else:
                    ch.link(dve.tensor_scalar(r1[:, 6, :], r1[:, 5, :], 1.0, None, ALU.add))
                    ch.link(dve.reciprocal(row[:, :, W0], r1[:, 6, :]))
                    ch.mark(dve.tensor_tensor(row[:, :, W1], r1[:, 5, :], row[:, :, W0], ALU.mult))

            def place(b, k, u):
                dve.wait_ge(pos.handle, pos.after(b))
                ch.settle()
                ch.link(dve.tensor_tensor(rt[:, 5, :, :], M0[:, PS:PS + NT * E].rearrange("p (t e) -> p t e", t=NT),
                                          run[:, :].unsqueeze(1).broadcast_to([P, NT, E]), ALU.add))
                dve.tensor_tensor(run[:, :], run[:, :], M0[:, PS + NT * E:PS + NT * E + E], ALU.add)\
                    .then_inc(pos_read.handle, 1)
                for c in range(n_choice):
                    ch.link(dve.tensor_tensor(rt[:, 6 + c, :, :], rt[:, 2 + 2 * c, :, :], rt[:, 5, :, :], ALU.mult))
                for c in range(n_choice):
                    ch.mark(dve.tensor_reduce(r1[:, 8 + c, :], rt[:, 6 + c, :, :], AX.X, ALU.add))
                ch.settle()
                dve.wait_ge(pos_read.handle, pos_read.after(b))
                dve.tensor_copy(slot_in[u][:, 0:n_choice, :], r1[:, 8:8 + n_choice, :]).then_inc(slots_ready.handle, 1)

            def tick(at):
                taken = []

                def maximum(h):
                    if at(0) and h not in taken:
                        taken.append(h)
                        row_max(*at(0), h)

                def maxima(first, n):
                    for h in range(first, first + n):
                        maximum(h)
                    ch.meanwhile = (lambda: maximum(first + n)) if l == 1 and first + n in MIDST else None

                def layer(n, step, off):
                    if l == n and at(off):
                        step(*at(off))

                def step(f, off, *args):
                    if at(off):
                        f(*at(off), *args)

                step(split_max, -1, 1)
                maxima(0, 1)
                step(normalise, -2, 2)
                maxima(1, 1)
                layer(0, first_stats, 2)
                maxima(2, 2)
                layer(0, first_norm, 2)
                layer(1, added_stats, 2)
                maxima(4, 1)
                step(normalise, -2, 3)
                maxima(5, 1)
                step(read_logits, -3)
                layer(1, residual, -2)
                maxima(6, 1)
                layer(0, choose_first, -3)
                layer(1, second_stats, -2)
                layer(1, outer_norm, 2)
                maxima(7, 1)
                step(split_max, 0, 0)
                maxima(8, 1)
                step(normalise, -1, 0)
                layer(1, modulate_rows, 2)
                maxima(9, 1)
                layer(0, choose_second, -3)
                layer(1, choose_first, -3)
                maxima(10, 1)
                layer(0, residual, -2)
                layer(1, inner_stats, 2)
                maxima(11, 1)
                layer(0, second_stats, -2)
                layer(1, second_norm, -2)
                maxima(12, 1)
                step(normalise, -1, 1)
                step(weigh_choices, -3)
                maxima(13, 1)
                layer(1, rms_moments, -2)
                step(place, -3)
                maxima(14, 1)
                layer(0, second_norm, -2)
                layer(1, inner_norm, 2)
                maxima(15, 1)
                layer(1, rms_norm, -2)

            run_ticks(dve, tick, ch, DVE_MARKS[l])

        @block.tensor
        def _(pe):
            start(pe, xn_T, qk_proj, v_proj, on_T, y_proj, y_T, h2_T, logits, pos, a_scores, m_T, b_scores, pv, o_T)

            def turn(tiles, ready, b, sig):
                pe.wait_ge(ready.handle, ready.after(b))
                for t in range(NT):
                    ins = pe.transpose(M0[:, t * P:(t + 1) * P], tiles[t], ident[:, :])
                ins.then_inc(sig.handle, 1)

            def by_tile(x):
                return [x[:, t, 0:D] for t in range(NT)]

            def turn_h2(b, k, u):
                turn(by_tile((h3 if l else h2)[u]), h3_ready if l else h2_ready, b, h2_T)

            def project_qk(b, k, u):
                pe.wait_ge(h_ready.handle, h_ready.after(b))
                pe.matmul(M0[:, 0:S], wq[:, l, :], hT[u][:, :], start=True, stop=True)
                pe.matmul(M0[:, S:2 * S], wk[:, l, :], hT[u][:, :], start=True, stop=True).then_inc(qk_proj.handle, 1)

            def project_v(b, k, u):
                for t in range(NT):
                    ins = pe.matmul(M0[:, t * P:(t + 1) * P], hT[u][:, t * P:(t + 1) * P], wv[:, l, :],
                                    start=True, stop=True)
                ins.then_inc(v_proj.handle, 1)

            def scores_a(b, k, u, h):
                if h % HH == 0:
                    pe.wait_ge(stack_in[u][h // HH], stack_in.of(k))
                pe.wait_ge(a_max.handle, a_max.after(b, h - 1) if h >= 2 else a_max.after(b - 1, H + h - 1))
                n = MROW
                for t in range(NT):
                    ins = pe.matmul(A[h % 2][:, t, :], stack[u][0:n, h, 0, t * P:(t + 1) * P],
                                    stack[u][0:n, h, 1, :], start=True, stop=(l == 1))
                    if l == 0:
                        ins = pe.matmul(A[h % 2][:, t, t * P:(t + 1) * P], slope_ident[:, h % HH, :],
                                        dist[:, t, :], start=False, stop=True)
                ins.then_inc(a_scores.handle, 1)

            def turn_max(b, k, u, half):
                pe.wait_ge(m_split.handle, m_split.after(b, half + 1))
                for t in range(NT):
                    ins = pe.transpose(M0b[0:2 * HH, 2 * S + t * P:2 * S + (t + 1) * P],
                                       mneg[:, half, t, :, :].rearrange("p c h -> p (c h)"), ident_b[:, :])
                ins.then_inc(m_T.handle, 1)

            def scores_b(b, k, u, c):
                if c % 4 == 0:
                    pe.wait_ge(m_in[u][c // 4], m_in.of(k))
                pe.wait_ge(b_exp.handle, b_exp.after(b, c - 1) if c >= 2 else b_exp.after(b - 1, HH + c - 1))
                for j in range(2):
                    h = 2 * c + j
                    for t in range(NT):
                        ins = pe.matmul(Bp[c % 2][:, j, t, :], stack[u][:, h, 1, t * P:(t + 1) * P],
                                        stack[u][:, h, 0, :], start=True, stop=(l == 1))
                        if l == 0:
                            ins = pe.matmul(Bp[c % 2][:, j, t, t * P:(t + 1) * P], slope_ident[:, h % HH, :],
                                            dist[:, 1 - t, :], start=False, stop=True)
                ins.then_inc(b_scores.handle, 1)

            def weigh(b, k, u, g):
                if g == 0:
                    pe.wait_ge(v_ready.handle, v_ready.after(b))
                pe.wait_ge(b_exp.handle, b_exp.after(b, 2 * g + 2))
                pe.wait_ge(o_norm.handle, o_norm.after(b, g) if g else o_norm.after(b - 1))
                for t in range(NT):
                    for j in range(4):
                        ins = pe.matmul(M1[VW * j:VW * j + VW, 0:S], vals[u][:, t, 4 * g + j, :],
                                        probs[(2 * g + j // 2) % 4][:, j % 2, t, :],
                                        start=(t == 0), stop=(t == NT - 1), tile_position=(0, VW * j))
                ins.then_inc(pv.handle, 1)

            def turn_heads(b, k, u, g):
                pe.wait_ge(o_read.handle, o_read.after(b, g + 1))
                for t in range(NT):
                    ins = pe.transpose(M1[:, S + t * P:S + (t + 1) * P], heads[g % 2][:, t * P:(t + 1) * P], ident[:, :])
                ins.then_inc(o_T.handle, 1)

            def project_out(b, k, u):
                pe.wait_ge(onT_read.handle, onT_read.after(b))
                pe.matmul(M0[:, S:2 * S], wo[:, :], OnT[:, :], start=True, stop=True).then_inc(y_proj.handle, 1)

            def gate(b, k, u):
                pe.wait_ge(h2T_read.handle, h2T_read.after(b))
                for t in range(NT):
                    ins = pe.matmul(M0[:, LG + t * E:LG + (t + 1) * E], h2T[:, t * P:(t + 1) * P], gate_w[:, l, :],
                                    start=True, stop=True)
                ins.then_inc(logits.handle, 1)

            def count(b, k, u):
                pe.wait_ge(sel_ready.handle, sel_ready.after(b))
                pe.matmul(M0[:, PS:PS + E], before_tri[:, :], sel[:, 0, :], start=True, stop=True)
                pe.matmul(M0[:, PS + E:PS + 2 * E], before_tri[:, :], sel[:, 1, :], start=True, stop=False)
                pe.matmul(M0[:, PS + E:PS + 2 * E], ones_b[:, :], sel[:, 0, :], start=False, stop=True)
                pe.matmul(M0[:, PS + 2 * E:PS + 3 * E], ones_b[:, :], sel[:, 0, :], start=True, stop=False)
                pe.matmul(M0[:, PS + 2 * E:PS + 3 * E], ones_b[:, :], sel[:, 1, :], start=False, stop=True)\
                    .then_inc(pos.handle, 1)

            def tick(at):
                def a_pass(*hs):
                    if at(0):
                        for h in hs:
                            scores_a(*at(0), h)

                def m0_read(*uses):
                    for sig, off, *n in uses:
                        if at(off):
                            pe.wait_ge(sig.handle, sig.after(at(off)[0], *n))
                            return

                def chunk(c):
                    if at(-1):
                        scores_b(*at(-1), c)

                def heads_step(step, off, g):
                    if at(off):
                        step(*at(off), g)

                a_pass(0, 1)
                chunk(0)
                a_pass(2)
                heads_step(weigh, -2, 3)
                if at(-3):
                    m0_read((h_ready, 1), (mT_read, -1, 1), (mT_read, -2, 2))
                    turn_h2(*at(-3))
                a_pass(3)
                chunk(1)
                if at(1):
                    m0_read((h2T_read, -3))
                    project_qk(*at(1))
                a_pass(4)
                heads_step(turn_heads, -2, 3)
                a_pass(5)
                if at(-3):
                    m0_read((qk_f32, 1))
                    gate(*at(-3))
                chunk(2)
                a_pass(6)
                if at(-1):
                    m0_read((logits_read, -3), (qk_f32, 1))
                    turn_max(*at(-1), 1)
                heads_step(weigh, -1, 0)
                a_pass(7)
                chunk(3)
                if at(0):
                    m0_read((mT_read, -1, 2), (qk_f32, 1))
                    project_v(*at(0))
                a_pass(8)
                heads_step(turn_heads, -1, 0)
                if at(-2) and l == 0:
                    m0_read((v_ready, 0), (mT_read, -1, 2), (logits_read, -3))
                    turn([On[at(-2)[2]][:, t, :, :].rearrange("p h d -> p (h d)") for t in range(NT)], o_norm, at(-2)[0], on_T)
                a_pass(9)
                chunk(4)
                if at(-2) and l == 0:
                    project_out(*at(-2))
                a_pass(10)
                heads_step(weigh, -1, 1)
                if at(-2) and l == 0:
                    turn([yT[:, t * P:(t + 1) * P] for t in range(NT)], y_read, at(-2)[0], y_T)
                a_pass(11)
                chunk(5)
                a_pass(12)
                heads_step(turn_heads, -1, 1)
                if at(-3):
                    m0_read(*[(x1_ready, -2)] * (l == 0), (v_ready, 0), (mT_read, -1, 2))
                    count(*at(-3))
                a_pass(13)
                chunk(6)
                a_pass(14)
                heads_step(weigh, -1, 2)
                a_pass(15)
                if at(0):
                    m0_read((pos_read, -3), *[(x1_ready, -2)] * (l == 0), (v_ready, 0))
                    turn_max(*at(0), 0)
                chunk(7)
                if at(2):
                    m0_read((mT_read, 0, 1), (qk_f32, 1))
                    turn(by_tile(xn[at(2)[2]]), xn_ready, at(2)[0], xn_T)
                heads_step(turn_heads, -1, 2)

            run_ticks(pe, tick)


def experts(nc, l, g):
    (ident, ones_row, a, region_row, tile_iota, run, run_i, cnt_i, n_tiles, tile_base, reached, tile_tab,
     tile_e, tile_row, tile_rev, first_choice, row_weight, row_dest, w1, w2, b1, b2, w1s, w2s, b2s, row_end, xt, xtT, hid, yt, A, Bp,
     M0, M1, ln_cols, gathered, expert_out) = (g[n] for n in (
        "ident ones_row a region_row tile_iota run run_i cnt_i n_tiles tile_base reached tile_tab "
        "tile_e tile_row tile_rev first_choice row_weight row_dest w1 w2 b1 b2 w1s w2s b2s row_end xt xtT hid yt A Bp "
        "M0 M1 ln_cols gathered expert_out").split())
    slots = SLOTS[l]
    pairs = slots // 2

    def sem(name):
        return nc.alloc_semaphore(f"L{l}_{name}")

    def signals(*names):
        return [Signal(sem(n), 1) for n in names]

    run_ready, table_ready = sem("run_ready"), sem("table_ready")
    zeroed = sem("slack_zeroed")
    xt_in = Transfers([sem(f"xt_in{u}") for u in range(2)], 1)
    yt_out = Transfers([sem(f"yt_out{u}") for u in range(2)], NT, 0)
    xt_T, xtT_ready, w1_staged, w2_staged, end_read, routed, first, hidden, second, y_done, scattered = signals(
        "xt_T", "xtT_ready", "w1_staged", "w2_staged", "end_read", "routed", "first_products", "hidden", "second_products", "y_done", "y_scattered")
    dve_order, pool_order = sem("tiles_dve_order"), sem("tiles_pool_order")

    def tile(k, n):
        return k * 2 + n, k + n // 2, n % 2

    with nc.Block() as block:

        @block.sync
        def _(sp):
            xt_in.start(sp)
            pads = a["pads"].rearrange("(j r) w -> j r w", r=TOK)
            sp.dma_start(gathered[l][E * REGION:E * REGION + TAIL * TOK, :], a["pads"][E * TOK:PADS * TOK, :]).then_inc(zeroed, 16)
            sp.wait_ge(run_ready, 1)
            for e in range(E):
                r = sp.value_load(run_i[0:1, e:e + 1], min_val=e * REGION, max_val=(e + 1) * REGION - TOK)
                sp.dma_start(gathered[l][bass.ds(r, TOK), :], pads[e])\
                    .then_inc(zeroed, 16)
            sp.wait_ge(table_ready, 1)
            sp.wait_ge(zeroed, 16 * (E + 1))

            def load_tile(s, k, u):
                row = sp.value_load(tile_row[0:1, bass.ds(s, 1)], min_val=0, max_val=E * REGION + (TAIL - 1) * TOK)
                sp.wait_ge(xt_T.handle, xt_T.after(s - 2))
                sp.wait_ge(end_read.handle, end_read.after(s - 2))
                sp.dma_start(xt[u][:, :, :], gathered[l][bass.ds(row, TOK), :].rearrange("(t p) d -> p t d", p=P))\
                    .then_inc(xt_in[u], 16)

            with sp.Fori(0, pairs) as k:
                for n in range(2):
                    load_tile(*tile(k, n))

        @block.gpsimd
        def _(pool):
            pool.sem_inc(scattered.handle, 2)
            ch = Chain(pool, pool_order)

            def scatter(s, k, u):
                pool.wait_ge(y_done.handle, y_done.after(s))
                ch.apart()
                for t in range(NT):
                    pool.indirect_dma_start(expert_out[l], bass.IndirectOffsetOnAxis(ap=row_dest[u][:, t:t + 1], axis=0),
                                            yt[u][:, t, :], None).then_inc(yt_out[u], 16)

            def scatter_done(s, k, u):
                pool.wait_ge(yt_out[u], yt_out.of(k))
                pool.sem_inc(scattered.handle, 1)

            with pool.Fori(0, pairs) as k:
                for n in range(2):
                    scatter(*tile(k, n))
                for n in range(2):
                    scatter_done(*tile(k, n))

        @block.vector
        def _(dve):
            ch = Chain(dve, dve_order)
            for s in (xtT_ready, w1_staged, w2_staged, end_read, routed, y_done):
                dve.sem_inc(s.handle, 2)
            dve.tensor_copy(run_i[:, :], run[:, :]).then_inc(run_ready, 1)
            ch.link(dve.tensor_tensor(n_tiles[:, :], run[:, :], region_row[:, :], ALU.subtract))
            ch.link(dve.tensor_scalar(n_tiles[:, :], n_tiles[:, :], float(TOK - 1), None, ALU.add))
            ch.link(dve.tensor_copy(cnt_i[:, :], n_tiles[:, :]))
            ch.link(dve.tensor_scalar(cnt_i[:, :], cnt_i[:, :], TOK.bit_length() - 1, None, ALU.logical_shift_right))
            ch.mark(dve.tensor_copy(n_tiles[:, :], cnt_i[:, :]))
            ch.link(dve.memset(tile_base[:, 0:1], 0.0))
            for e in range(E):
                ch.link(dve.tensor_tensor(tile_base[:, e + 1:e + 2], tile_base[:, e:e + 1], n_tiles[:, e:e + 1], ALU.add))
            base = tile_base[:, :].unsqueeze(1).broadcast_to([P, slots, E + 1])
            r = reached[:, 0:slots, :]
            tab = tile_tab[:, :, 0:slots]
            ch.link(dve.tensor_tensor(r, tile_iota[:, 0:slots, :], base, ALU.is_ge))
            ch.link(dve.tensor_reduce(tab[:, 0, :], r, AX.X, ALU.add))
            ch.link(dve.tensor_tensor(r, r, base, ALU.mult))
            ch.link(dve.tensor_reduce(tab[:, 1, :], r, AX.X, ALU.max))
            ch.link(dve.tensor_tensor(tab[:, 1, :], tile_iota[:, 0:slots, 0], tab[:, 1, :], ALU.subtract))
            ch.link(dve.tensor_scalar(tab[:, 0, :], tab[:, 0, :], -1.0, None, ALU.add))
            ch.link(dve.tensor_scalar(tab[:, 1, :], tab[:, 1, :], float(TOK), None, ALU.mult))
            ch.mark(dve.scalar_tensor_tensor(out=tile_row[:, 0:slots], in0=tab[:, 0, :], scalar=float(REGION),
                                             in1=tab[:, 1, :], op0=ALU.mult, op1=ALU.add))
            ch.mark(dve.tensor_scalar(tile_rev[:, 0:slots], tab[:, 0, :], -1.0, float(E), ALU.mult, ALU.add))
            ch.link(dve.tensor_scalar(tile_e[:, 0:slots], tab[:, 0, :], float(E - 1), None, ALU.min))
            dve.sem_inc(table_ready, 1)

            def stage_w1(s, k, u):
                e = dve.value_load(tile_e[0:1, bass.ds(s, 1)], min_val=0, max_val=E - 1)
                dve.wait_ge(first.handle, first.after(s - 2))
                dve.tensor_scalar(w1s[u][:, :], w1[:, bass.ds(e, 1), :].rearrange("p o f -> p (o f)"), 1.0, None, ALU.mult)\
                    .then_inc(w1_staged.handle, 1)
                return e

            def stage_w2(s, k, u, e):
                dve.wait_ge(second.handle, second.after(s - 2))
                if l:
                    ch.link(dve.tensor_scalar(b2s[u][:, :], b2[:, bass.ds(e, 1), :].rearrange("p o d -> p (o d)"),
                                              1.0, None, ALU.mult))
                dve.tensor_scalar(w2s[u][:, :, :], w2[:, bass.ds(e, 1), :, :].rearrange("p o f d -> p (o f) d"),
                                  1.0, None, ALU.mult).then_inc(w2_staged.handle, 1)

            def read_end(s, k, u):
                dve.wait_ge(xt_in[u], xt_in.of(k))
                dve.tensor_copy(row_end[u][:, :, :], xt[u][:, :, D:W]).then_inc(end_read.handle, 1)

            def read_xT(s, k, u):
                dve.wait_ge(xt_T.handle, xt_T.after(s))
                m = (M0, M1)[u]
                if l:
                    dve.tensor_scalar(xtT[u][:, :], m[:, 0:TOK], ln_cols[:, 2:3], None, ALU.mult).then_inc(xtT_ready.handle, 1)
                else:
                    dve.tensor_copy(xtT[u][:, :], m[:, 0:TOK]).then_inc(xtT_ready.handle, 1)

            def route(s, k, u):
                dve.wait_ge(end_read.handle, end_read.after(s))
                dve.wait_ge(y_done.handle, y_done.after(s - 2))
                x, w = row_end[u], row_weight[u]
                if l == 0:
                    is_first = first_choice[u]
                    ch.link(dve.tensor_scalar(is_first[:, 0, :], x[:, :, REV - D], tile_rev[:, bass.ds(s, 1)], None, ALU.is_equal))
                    ch.mark(dve.tensor_tensor(w[:, 0, :], is_first[:, 0, :], x[:, :, W0 - D], ALU.mult))
                    ch.link(dve.tensor_scalar(is_first[:, 1, :], is_first[:, 0, :], -1.0, 1.0, ALU.mult, ALU.add))
                    ch.link(dve.tensor_tensor(w[:, 1, :], is_first[:, 1, :], x[:, :, W1 - D], ALU.mult))
                    ch.mark(dve.tensor_tensor(w[:, 0, :], w[:, 0, :], w[:, 1, :], ALU.add))
                    dve.wait_ge(scattered.handle, scattered.after(s - 2))
                    dve.scalar_tensor_tensor(out=row_dest[u][:, :], in0=is_first[:, 1, :], scalar=float(B * S),
                                             in1=x[:, :, TOKEN - D], op0=ALU.mult, op1=ALU.add).then_inc(routed.handle, 1)
                else:
                    ch.mark(dve.tensor_scalar(w[:, 0, :], x[:, :, W0 - D], 1.0, None, ALU.mult))
                    dve.wait_ge(scattered.handle, scattered.after(s - 2))
                    dve.tensor_scalar(row_dest[u][:, :], x[:, :, TOKEN - D], 1.0, None, ALU.mult).then_inc(routed.handle, 1)

            def read_y(s, k, u):
                dve.wait_ge(second.handle, second.after(s))
                dve.wait_ge(scattered.handle, scattered.after(s - 2))
                dve.wait_ge(routed.handle, routed.after(s))
                ch.settle()
                for t in range(NT):
                    ins = dve.tensor_scalar(yt[u][:, t, :], A[u][:, t, 0:D], row_weight[u][:, 0, t:t + 1], None, ALU.mult)
                    if t < NT - 1:
                        ch.link(ins)
                ins.then_inc(y_done.handle, 1)

            def ahead(k, n, e):
                read_end(*tile(k, n))
                read_xT(*tile(k, n))
                stage_w2(*tile(k, n), e)

            def pair(k, more):
                if more:
                    e = [stage_w1(*tile(k, 2))]
                route(*tile(k, 0))
                if more:
                    e.append(stage_w1(*tile(k, 3)))
                route(*tile(k, 1))
                read_y(*tile(k, 0))
                if more:
                    ahead(k, 2, e[0])
                read_y(*tile(k, 1))
                if more:
                    ahead(k, 3, e[1])

            for n in range(2):
                ahead(0, n, stage_w1(*tile(0, n)))
            ch.before()
            with dve.Fori(0, pairs - 1) as k:
                ch.loop(k, 2 * (3 if l else 6))
                pair(k, True)
                assert ch.n == ch.per, ch.n
            ch.done(pairs - 1)
            pair(pairs - 1, False)

        @block.scalar
        def _(act):
            act.sem_inc(hidden.handle, 2)
            act.preload_act_table(ACT.Silu if l else ACT.Relu)
            act.wait_ge(table_ready, 1)

            def activate(s, k, u):
                act.wait_ge(first.handle, first.after(s))
                act.wait_ge(second.handle, second.after(s - 2))
                src = Bp[u][:, :, :, :].rearrange("p j t s -> p (j t) s")
                if l == 0:
                    act.activation(hid[u][:, :, :], src, ACT.Relu).then_inc(hidden.handle, 1)
                else:
                    e = act.value_load(tile_e[0:1, bass.ds(s, 1)], min_val=0, max_val=E - 1)
                    for f in range(FC):
                        ins = act.activation(hid[u][:, f, :], src[:, f, :], ACT.Silu,
                                             bias=b1[:, bass.ds(e, 1), f:f + 1].rearrange("p o f -> p (o f)"))
                    ins.then_inc(hidden.handle, 1)

            with act.Fori(0, pairs) as k:
                for n in range(2):
                    activate(*tile(k, n))

        @block.tensor
        def _(pe):
            for s in (xt_T, first, second):
                pe.sem_inc(s.handle, 2)
            pe.wait_ge(table_ready, 1)

            def turn_x(s, k, u):
                pe.wait_ge(xt_in[u], xt_in.of(k))
                pe.wait_ge(xtT_ready.handle, xtT_ready.after(s - 2))
                for t in range(NT):
                    ins = pe.transpose((M0, M1)[u][:, t * P:(t + 1) * P], xt[u][:, t, 0:D], ident[:, :])
                ins.then_inc(xt_T.handle, 1)

            def to_hidden(s, k, u):
                pe.wait_ge(w1_staged.handle, w1_staged.after(s))
                pe.wait_ge(xtT_ready.handle, xtT_ready.after(s))
                pe.wait_ge(hidden.handle, hidden.after(s - 2))
                dst = Bp[u][:, :, :, :].rearrange("p j t s -> p (j t) s")
                for f in range(FC):
                    ins = pe.matmul(dst[:, f, :], w1s[u][:, f * P:(f + 1) * P], xtT[u][:, :], start=True, stop=True)
                ins.then_inc(first.handle, 1)

            def from_hidden(s, k, u):
                pe.wait_ge(w2_staged.handle, w2_staged.after(s))
                pe.wait_ge(hidden.handle, hidden.after(s))
                pe.wait_ge(y_done.handle, y_done.after(s - 2))
                for t in range(NT):
                    for f in range(FC):
                        ins = pe.matmul(A[u][:, t, 0:D], hid[u][:, f, t * P:(t + 1) * P],
                                        w2s[u][:, f, :],
                                        start=(f == 0), stop=(l == 0 and f == FC - 1))
                    if l:
                        ins = pe.matmul(A[u][:, t, 0:D], ones_row[:, :], b2s[u][:, :],
                                        start=False, stop=True)
                ins.then_inc(second.handle, 1)

            def pair(k, more):
                to_hidden(*tile(k, 0))
                to_hidden(*tile(k, 1))
                if more:
                    turn_x(*tile(k, 2))
                from_hidden(*tile(k, 0))
                if more:
                    turn_x(*tile(k, 3))
                from_hidden(*tile(k, 1))

            for n in range(2):
                turn_x(*tile(0, n))
            with pe.Fori(0, pairs - 1) as k:
                pair(k, True)
            pair(pairs - 1, False)


def combine(nc, g):
    hid, w1, w2, x_mid, expert_out, mod_rows, out = (g[n] for n in
        "hid w1 w2 x_mid expert_out mod_rows out".split())
    G = FC * TOK // S
    groups = B // G
    rows = "(g q p) d -> g p q d"
    x_view = x_mid[2].rearrange(rows, p=P, q=G * NT)
    y_view = expert_out[1][0:B * S, :].rearrange(rows, p=P, q=G * NT)
    out_view = out.rearrange("b s d -> (b s) d").rearrange(rows, p=P, q=G * NT)
    x_tile = [hid[u][:, :, :].rearrange("p f s -> p (f s)") for u in range(2)]
    y_tile = [w1[:, 4 * u:4 * u + 2, :].rearrange("p e f -> p (e f)") for u in range(2)]
    out_tile = [w1[:, 4 * u + 2:4 * u + 4, :].rearrange("p e f -> p (e f)") for u in range(2)]
    gb_tile = [w2[:, u, 0:G, :] for u in range(2)]

    def by_row(x):
        return x.rearrange("p (q d) -> p q d", d=D)

    def by_batch(x):
        return x.rearrange("p (b t d) -> p b t d", b=G, t=NT)

    def sem(name):
        return nc.alloc_semaphore(f"out_{name}")

    x_in = Transfers([sem(f"x_in{u}") for u in range(2)], 3)
    stored = Transfers([sem(f"stored{u}") for u in range(2)], 1)
    summed = Signal(sem("summed"), 1)
    dve_order = sem("dve_order")

    with nc.Block() as block:

        @block.sync
        def _(sp):
            x_in.start(sp)
            with sp.Fori(0, groups // 2) as k:
                for u in range(2):
                    n = k * 2 + u
                    sp.wait_ge(summed.handle, summed.after(n - 2))
                    sp.dma_start(by_row(x_tile[u]), x_view[bass.ds(n, 1)].rearrange("o p q d -> (o p) q d"))\
                        .then_inc(x_in[u], 16)
                    sp.dma_start(by_row(y_tile[u]), y_view[bass.ds(n, 1)].rearrange("o p q d -> (o p) q d"))\
                        .then_inc(x_in[u], 16)
                    sp.dma_start(gb_tile[u], mod_rows[1].rearrange("(g b) c -> g b c", b=G)[bass.ds(n, 1), :, GB * D:(GB + 1) * D]
                                 .broadcast_to([P, G, D])).then_inc(x_in[u], 16)

        @block.scalar
        def _(act):
            stored.start(act)
            with act.Fori(0, groups // 2) as k:
                for u in range(2):
                    n = k * 2 + u
                    act.wait_ge(summed.handle, summed.after(n))
                    act.dma_start(out_view[bass.ds(n, 1)].rearrange("o p q d -> (o p) q d"), by_row(out_tile[u]))\
                        .then_inc(stored[u], 16)
            for u in range(2):
                act.wait_ge(stored[u], stored.of(groups // 2 - 1))

        @block.vector
        def _(dve):
            ch = Chain(dve, dve_order)
            dve.sem_inc(summed.handle, 2)
            ch.before()
            with dve.Fori(0, groups // 2) as k:
                ch.loop(k, 2)
                for u in range(2):
                    dve.wait_ge(x_in[u], x_in.of(k))
                    dve.wait_ge(stored[u], stored.of(k - 1))
                    ch.link(dve.tensor_tensor(by_batch(y_tile[u]), by_batch(y_tile[u]),
                                              gb_tile[u].unsqueeze(2).broadcast_to([P, G, NT, D]), ALU.mult))
                    dve.tensor_tensor(out_tile[u], x_tile[u], y_tile[u], ALU.add).then_inc(summed.handle, 1)
                assert ch.n == ch.per


def inputs_of(x):
    import numpy as np

    def bits(x):
        return (np.ascontiguousarray(x, np.float32).view(np.uint32) >> 16).astype(np.uint16)

    n = {k: np.asarray(v) for k, v in x.items()}
    r, c = np.arange(P)[:, None], np.arange(P)[None, :]
    half, d, h8 = np.meshgrid(np.arange(2), np.arange(HD), np.arange(HH), indexing="ij")
    stacked = (16 * h8 + 8 * half + d).reshape(-1)
    half, h8, d = np.meshgrid(np.arange(2), np.arange(HH), np.arange(HD), indexing="ij")
    by_head = (16 * h8 + 8 * half + d).reshape(-1)
    wqkv, bqkv = n["L0_attn_W_qkv"], n["L0_attn_b_qkv"]
    slope = 2.0 ** -np.arange(HH)
    pos = np.arange(S)
    rows = np.zeros((4, H, 2, S))
    sign = np.where(pos < P, 1.0, -1.0)
    rows[0, :, 0] = np.tile(slope, 2)[:, None] * (sign * pos)[None]
    rows[1, :, 0] = -np.tile(slope, 2)[:, None] * sign[None]
    rows[0, :, 1] = 1.0
    rows[1, :, 1] = pos
    rows[2:, :, 1] = 1.0
    rows1 = rows.copy()
    rows1[:2, :, 0] = 0.0
    f = np.float32
    slots = SLOTS[0]
    pads = np.zeros((PADS * TOK, W), f)
    pads[:, TOKEN] = B * S + np.arange(PADS * TOK)
    pads[:, REV] = -1.0
    return {
        "x": n["L0_attn_x"],
        "ident": np.eye(P, dtype=f), "ident_b": bits(np.eye(P)),
        "slope_ident": bits(np.eye(P)[:, None, :] * slope[None, :, None]),
        "dist": bits(np.stack([-2.0 * np.maximum(r - c, 0), -2.0 * np.maximum(c - r, 0)], 1)),
        "before_tri": bits(r < c), "ones_b": bits(np.ones((P, P))),
        "rev_iota": np.broadcast_to(E - np.arange(E, dtype=f), (P, 2, E)).copy(),
        "region_row": np.broadcast_to(np.arange(E, dtype=f) * REGION, (P, E)).copy(),
        "tile_iota": np.broadcast_to(np.arange(slots, dtype=f)[None, :, None], (P, slots, E + 1)).copy(),
        "token_ids": (np.arange(P)[:, None, None] + S * np.arange(B)[None, :, None]
                      + P * np.arange(NT)[None, None, :]).astype(f),
        "pads": pads, "stack_rows0": bits(rows), "stack_rows1": bits(rows1),
        "wq": np.stack([wqkv[0:D].T[:, stacked], n["L1_attn_wq"][:, stacked]], 1),
        "wk": np.stack([wqkv[D:2 * D].T[:, stacked], n["L1_attn_wk"][:, stacked]], 1),
        "wv": np.stack([wqkv[2 * D:].T[:, by_head], n["L1_attn_wv"][:, by_head]], 1),
        "wo": n["L0_attn_W_out"].T[by_head],
        "qk_bias": np.stack([bqkv[0:D][stacked], bqkv[D:2 * D][stacked]], 1),
        "q_scale": np.stack([np.where(np.arange(D) < 64, HD ** -0.5, (2.0 / HD) ** 0.5), np.full(D, D ** -0.5)], 1).astype(f),
        "vo_bias": np.stack([bqkv[2 * D:][by_head], n["L0_attn_b_out"]], 1),
        "ln_cols": np.stack([n["L1_attn_ln_scale"], n["L1_attn_ln_bias"], n["L1_ffn_rms_w"]], 1),
        "ln_rows": np.stack([n["L1_attn_ln_scale"], n["L1_attn_ln_bias"]])[None],
        "gate_w": np.stack([n["L0_ffn_Wr"], n["L1_ffn_gate_w"].T], 1),
        "cT": np.stack([n["L0_c"].T, n["L1_c"].T], 1),
        "wmod0": n["L0_wmod"], "wmod1": n["L1_wmod"],
        "w1_0": n["L0_ffn_W1"].transpose(1, 0, 2), "w1_1": n["L1_ffn_W1"].transpose(1, 0, 2),
        "w2_0": n["L0_ffn_W2"].reshape(E, FC, P, D).transpose(2, 0, 1, 3),
        "w2_1": n["L1_ffn_W2"].reshape(E, FC, P, D).transpose(2, 0, 1, 3),
        "b1": n["L1_ffn_b1"].reshape(E, FC, P).transpose(2, 0, 1),
        "b2": n["L1_ffn_b2"][None],
    }


def kernel(**inputs):
    import numpy as np
    import concourse.bacc as bacc
    from concourse.bass_utils import run_bass_kernel_spmd as launch

    nc = bacc.Bacc("TRN2", target_bir_lowering=False, num_devices=1)
    arrays = {f"in_{k}": np.ascontiguousarray(v) for k, v in inputs_of(inputs).items()}
    aps = {k[3:]: nc.dram_tensor(k, v.shape, mybir.dt.from_np(v.dtype), kind="ExternalInput").ap()
           for k, v in arrays.items()}
    out = nc.dram_tensor("out_0", (B, S, D), F32, kind="ExternalOutput").ap()
    build(nc, aps, out)
    return launch(nc, [arrays], core_ids=[0]).results[0]["out_0"]
```
